# Optimizing a Trainium2 kernel written in Bass

```python
import numpy as np
import jax
import jax.numpy as jnp

def _softmax(x, axis=-1):
    return jax.nn.softmax(x, axis=axis)

def _gelu(x):
    return jax.nn.gelu(x, approximate=True)

def _silu(x):
    return jax.nn.silu(x)

def _sigmoid(x):
    return jax.nn.sigmoid(x)

def _layernorm(x, axis=-1, eps=1e-05):
    m = jnp.mean(x, axis=axis, keepdims=True)
    v = jnp.var(x, axis=axis, keepdims=True)
    return (x - m) / jnp.sqrt(v + eps)

def _scatter_add(tgt, idx, src, axis=0):
    return tgt.at[idx].add(src)

def _segment_sum(src, seg, n):
    return jax.ops.segment_sum(src, seg, n)
kernel_name = 'mk_adaln_d1_jaxref_r4_15fa87'

def setup_inputs(seed: int=0):
    np.random.seed(seed)
    _w = jnp.asarray

    def _L0_attn_setup():
        import jax, jax.numpy as jnp
        import numpy as np
        import math
        B, L, D, H = (32, 128, 1024, 32)
        HD = D // H
        key = jax.random.key(seed)
        ks = jax.random.split(key, 9)
        s = 1.0 / math.sqrt(D)
        return {'x': jax.random.normal(ks[0], (B, L, D), jnp.float32), 'Wq': jax.random.normal(ks[1], (D, D), jnp.float32) * s, 'bq': jax.random.normal(ks[2], (D,), jnp.float32) * s, 'Wk': jax.random.normal(ks[3], (D, D), jnp.float32) * s, 'bk': jax.random.normal(ks[4], (D,), jnp.float32) * s, 'Wv': jax.random.normal(ks[5], (D, D), jnp.float32) * s, 'bv': jax.random.normal(ks[6], (D,), jnp.float32) * s, 'Wo': jax.random.normal(ks[7], (D, D), jnp.float32) * s, 'bo': jax.random.normal(ks[8], (D,), jnp.float32) * s}
    _L0_attn_in = _L0_attn_setup()

    def _L0_ffn_setup():
        import jax, jax.numpy as jnp
        import numpy as np
        LORA_SCALE = 16.0 / jnp.sqrt(16.0)
        TOP_K = 2
        key = jax.random.key(seed)
        k1, k2, k3, k4 = jax.random.split(key, 4)
        B_, S, D, O, E, R = (4, 512, 1024, 1024, 4, 16)
        x = jax.random.normal(k1, (B_, S, D), dtype=jnp.float32)
        router_w = jax.random.normal(k2, (E, D), dtype=jnp.float32) * 0.02
        A = jax.random.normal(k3, (E, R, D), dtype=jnp.float32) * 0.02
        B = jax.random.normal(k4, (O,), dtype=jnp.float32)
        B = jax.random.normal(k4, (E, O, R), dtype=jnp.float32) * 0.02
        return {'x': x, 'router_w': router_w, 'A': A, 'B': B}
    _L0_ffn_in = _L0_ffn_setup()
    _L0_c = _w((lambda *s: np.random.randn(*s).astype(np.float32) * 0.05)(4, 1024))
    _L0_wmod = _w((lambda *s: np.random.randn(*s).astype(np.float32) * 0.05)(1024, 6 * 1024) * 1024 ** (-0.5))
    _d = {'L0_attn_x': _L0_attn_in['x'], 'L0_attn_Wq': _L0_attn_in['Wq'], 'L0_attn_bq': _L0_attn_in['bq'], 'L0_attn_Wk': _L0_attn_in['Wk'], 'L0_attn_bk': _L0_attn_in['bk'], 'L0_attn_Wv': _L0_attn_in['Wv'], 'L0_attn_bv': _L0_attn_in['bv'], 'L0_attn_Wo': _L0_attn_in['Wo'], 'L0_attn_bo': _L0_attn_in['bo'], 'L0_ffn_router_w': _L0_ffn_in['router_w'], 'L0_ffn_A': _L0_ffn_in['A'], 'L0_ffn_B': _L0_ffn_in['B'], 'L0_c': _L0_c, 'L0_wmod': _L0_wmod}
    _x0 = _d['L0_attn_x']
    _d['L0_attn_x'] = jax.random.normal(jax.random.fold_in(jax.random.key(seed), 1), (4, 1024, 1024), dtype=_x0.dtype)
    del _x0
    return _d

def reference(L0_attn_x, L0_attn_Wq, L0_attn_bq, L0_attn_Wk, L0_attn_bk, L0_attn_Wv, L0_attn_bv, L0_attn_Wo, L0_attn_bo, L0_ffn_router_w, L0_ffn_A, L0_ffn_B, L0_c, L0_wmod):

    def _L0_attn_ref(x, Wq, bq, Wk, bk, Wv, bv, Wo, bo):
        import jax, jax.numpy as jnp
        import numpy as np
        import math
        B, L, D, H = (32, 128, 1024, 32)
        HD = D // H
        b, l, d = x.shape
        h, hd = (H, HD)
        q = (x @ Wq.T + bq).reshape(b, l, h, hd).transpose(0, 2, 1, 3)
        k = (x @ Wk.T + bk).reshape(b, l, h, hd).transpose(0, 2, 1, 3)
        v = (x @ Wv.T + bv).reshape(b, l, h, hd).transpose(0, 2, 1, 3)
        scores = jnp.einsum('bhqd,bhkd->bhqk', q, k) / math.sqrt(hd)
        causal = jnp.tril(jnp.ones((l, l), bool))
        scores = jnp.where(causal, scores, -jnp.inf)
        att = jax.nn.softmax(scores, axis=-1)
        out = jnp.einsum('bhqk,bhkd->bhqd', att, v)
        out = out.transpose(0, 2, 1, 3).reshape(b, l, d)
        return out @ Wo.T + bo

    def _L0_ffn_ref(x, router_w, A, B):
        import jax, jax.numpy as jnp
        import numpy as np
        LORA_SCALE = 16.0 / jnp.sqrt(16.0)
        TOP_K = 2
        D = x.shape[-1]
        flat = x.reshape(-1, D)
        logits = flat @ router_w.T
        topk_vals, topk_idx = jax.lax.top_k(logits, TOP_K)
        sparse = jnp.full_like(logits, -jnp.inf)
        rows = jnp.arange(logits.shape[0])[:, None]
        sparse = sparse.at[rows, topk_idx].set(topk_vals)
        gates = jax.nn.softmax(sparse, axis=-1)
        mid = jnp.einsum('tf,erf->ter', flat, A)
        all_deltas = jnp.einsum('ter,eor->teo', mid, B) * LORA_SCALE
        delta = jnp.einsum('te,teo->to', gates, all_deltas)
        return delta.reshape(*x.shape[:-1], -1)
    x = L0_attn_x
    mod = (_silu(L0_c) @ L0_wmod).reshape(L0_c.shape[0], 6, 1, -1)
    sa, ca, ga, sb, cb, gb = (mod[:, 0], mod[:, 1], mod[:, 2], mod[:, 3], mod[:, 4], mod[:, 5])
    ga = (2 * (ga >= 0) - 1) * jnp.maximum(jnp.abs(ga), 0.25)
    gb = (2 * (gb >= 0) - 1) * jnp.maximum(jnp.abs(gb), 0.25)
    h = _layernorm(x, axis=-1) * (1 + ca) + sa
    x = x + ga * _L0_attn_ref(h, L0_attn_Wq, L0_attn_bq, L0_attn_Wk, L0_attn_bk, L0_attn_Wv, L0_attn_bv, L0_attn_Wo, L0_attn_bo)
    h = _layernorm(x, axis=-1) * (1 + cb) + sb
    x = x + gb * _L0_ffn_ref(h, L0_ffn_router_w, L0_ffn_A, L0_ffn_B)
    return x

_drawn_inputs = setup_inputs


def setup_inputs(seed=0):
    import zlib

    import numpy as np

    out = dict(_drawn_inputs(seed))
    spreads = {}
    factors = {'L0_attn_bq': 61.738, 'L0_attn_bk': 64.0, 'L0_attn_bv': 6.779, 'L0_attn_bo': 7.477}
    for name, (base, spread) in spreads.items():
        noise = np.random.default_rng([zlib.crc32(name.encode()), seed]).standard_normal(out[name].shape)
        drawn = base * np.exp(spread * noise) if base else spread * noise
        out[name] = jnp.asarray(drawn.astype(out[name].dtype))
    for name, factor in factors.items():
        out[name] = (out[name] * factor).astype(out[name].dtype)
    return out
```

```python
from contextlib import ExitStack

import numpy as np

import concourse.bass as bass
from concourse import mybir

F32 = mybir.dt.float32
F32R = mybir.dt.float32r
BF16 = mybir.dt.bfloat16
ALU = mybir.AluOpType
ACT = mybir.ActivationFunctionType
AX = mybir.AxisListType

P = 128
BANK = 512
HEADS = 32
EPS = 1e-5
LORA_SCALE = 4.0
MASKED = -3.0e38


def wait_apart(eng, sem, value, tally):
    eng.wait_ge(sem, value)
    eng.sem_inc(tally, 1)


class Chain:

    def __init__(self, eng, sem, tally, base=0):
        self.eng, self.sem, self.tally, self.value = eng, sem, tally, base

    def link(self, ins):
        ins.then_inc(self.sem, 1)
        self.value = self.value + 1
        wait_apart(self.eng, self.sem, self.value, self.tally)


def adaln_block(nc, x, Wq, bq, Wk, bk, Wv, bv, Wo, bo, router_w, lora_a, lora_b, c, wmod, out):
    NB, L, D = x.shape
    KT = D // P
    TT = L // P
    HD = D // HEADS
    HG = P // HD
    E, R, _ = lora_a.shape
    ER = E * R
    NR = ER + E
    QC = L // BANK
    NG = NB * KT
    SCALE = float(HD) ** -0.5
    QK_ROWS = 3 * HD
    SHIFT_ROW = QK_ROWS
    assert HD == 32 and L == 1024 and D == 1024

    mod_rows = nc.dram_tensor("mod_rows", [NB, 6 * D], F32).ap()
    w_split = nc.dram_tensor("w_split", [4, KT, 2, P, D], F32).ap()
    qk_split = nc.dram_tensor("qk_split", [NG, 4, P, L], F32).ap()
    v_tok = nc.dram_tensor("v_tok", [NG, P, TT, P], F32).ap()
    att_split = nc.dram_tensor("att_split", [NB, 2, KT, P, L], F32).ap()

    with ExitStack() as top:
        def keep(name, shape, dt=F32):
            return top.enter_context(nc.sbuf_tensor(name, shape, dt))

        ident = keep("ident", [P, P])
        bias_col = keep("bias_col", [P, 3 * KT])
        mod1_col = keep("mod1_col", [P, NB * 2 * KT])
        mod2_col = keep("mod2_col", [P, NB * 2 * KT])
        down_t = keep("down_t", [P, KT, NR])
        up_t = keep("up_t", [ER, D])

        tally = top.enter_context(nc.semaphore("tally"))

        prepare(nc, locals())
        project(nc, locals())
        attend(nc, locals())
        finish(nc, locals())


def prepare(nc, s):
    tally = s["tally"]
    (NB, D, KT, NR, ER, E, R, ident, bias_col, mod1_col, mod2_col, down_t, up_t, mod_rows, w_split) = (
        s[n] for n in "NB D KT NR ER E R ident bias_col mod1_col mod2_col down_t up_t mod_rows w_split".split())
    ROUNDS = 6 * D // (4 * BANK)
    RC = 4 * BANK
    CB = NB * KT
    MR = 2 * KT * NB
    weights = (s["Wq"], s["Wk"], s["Wv"], s["Wo"])
    with ExitStack() as ctx:
        def sb(name, shape, dt=F32):
            return ctx.enter_context(nc.sbuf_tensor(name, shape, dt))

        def sem(name):
            return ctx.enter_context(nc.semaphore(name))

        c_in = sb("c_in", [CB, P])
        bias_in = sb("bias_in", [3 * KT, P])
        down_in = sb("down_in", [NR, D])
        up_in = sb("up_in", [P, KT, ER])
        mod1_in = sb("mod1_in", [MR, P])
        mod2_in = sb("mod2_in", [MR, P])
        silu_e = sb("silu_e", [P, CB])
        silu_r = sb("silu_r", [P, CB])
        silu_c = sb("silu_c", [P, KT, NB])
        wm = sb("wm", [P, 2, KT, RC])
        rows = sb("rows", [P, ROUNDS, BANK])
        sign = sb("sign", [P, BANK])
        mag = sb("mag", [P, BANK])
        w_in = sb("w_in", [P, 2, D])
        w_hi = sb("w_hi", [P, 2, D], F32R)
        w_lo = sb("w_lo", [P, 2, D], F32R)
        ps_small = ctx.enter_context(nc.psum_tensor("ps_small", [P, BANK], F32))
        ps_mod = ctx.enter_context(nc.psum_tensor("ps_mod", [P, ROUNDS, BANK], F32))
        ps_w = ctx.enter_context(nc.psum_tensor("ps_w", [P, 2, D], F32))

        ident_ready = sem("ident_ready")
        small_loaded, mod_loaded = sem("small_loaded"), sem("mod_loaded")
        small_done, small_copied = sem("small_done"), sem("small_copied")
        silu_exp, silu_ready, dve_chain = sem("silu_exp"), sem("silu_ready"), sem("dve_chain")
        wm_loaded = [sem(f"wm_loaded{i}") for i in range(2)]
        mod_done, rows_ready, rows_stored = sem("mod_done"), sem("rows_ready"), sem("rows_stored")
        w_loaded = [sem(f"w_loaded{i}") for i in range(2)]
        w_turned, w_hi_done, w_lo_done = sem("w_turned"), sem("w_hi_done"), sem("w_lo_done")
        w_stored = [sem(f"w_stored{i}") for i in range(2)]
        block = ctx.enter_context(nc.Block())

        wm_view = s["wmod"].rearrange("(k p) n -> p k n", p=P)

        @block.sync
        def _(sp):
            sp.dma_start(c_in[:], s["c"].rearrange("b (k p) -> (b k) p", p=P)).then_inc(small_loaded, 16)
            for i, b in enumerate((s["bq"], s["bk"], s["bv"])):
                sp.dma_start(bias_in[i * KT:(i + 1) * KT, :], b.rearrange("(g p) -> g p", p=P)).then_inc(small_loaded, 16)
            sp.dma_start(down_in[0:ER, :], s["lora_a"].rearrange("e r d -> (e r) d")).then_inc(small_loaded, 16)
            sp.dma_start(down_in[ER:NR, :], s["router_w"]).then_inc(small_loaded, 16)
            lb = s["lora_b"].rearrange("e (t p) r -> e p t r", p=P)
            for e in range(E):
                sp.dma_start(up_in[:, :, e * R:(e + 1) * R], lb[e]).then_inc(small_loaded, 16)
            for r in range(ROUNDS):
                if r >= 2:
                    sp.wait_ge(mod_done, r - 1)
                sp.dma_start(wm[:, r % 2], wm_view[:, :, r * RC:(r + 1) * RC]).then_inc(wm_loaded[r % 2], 16)
            for m in range(4):
                with sp.Fori(0, KT // 2) as tt:
                    for i in range(2):
                        n = m * KT + tt * 2 + i
                        sp.wait_ge(w_turned, n + 1)
                        sp.dma_start(w_in[:, i], weights[m].rearrange("(t p) n -> t p n", p=P)[tt * 2 + i]).then_inc(w_loaded[i], 16)

        @block.gpsimd
        def _(pool):
            nc.gpsimd.memset(ident[:], 0.0).then_inc(ident_ready, 1)
            pool.wait_ge(ident_ready, 1)
            nc.gpsimd.affine_select(out=ident[:], in_=ident[:], compare_op=ALU.not_equal, fill=1.0, base=0,
                                    pattern=[[-1, P]], channel_multiplier=1).then_inc(ident_ready, 1)
            for r in range(ROUNDS):
                pool.wait_ge(rows_ready, r + 1)
                for j in range(4):
                    col = r * RC + j * BANK
                    pool.dma_start(mod_rows[:, col:col + BANK], rows[32 * j:32 * j + NB, r]).then_inc(rows_stored, 16)
            pool.wait_ge(rows_stored, 16 * 4 * ROUNDS)
            for b in range(NB):
                for v, dst in ((0, mod1_in), (3, mod2_in)):
                    src = mod_rows[b, v * D:(v + 2) * D].rearrange("(r p) -> r p", p=P)
                    pool.dma_start(dst[b * 2 * KT:(b + 1) * 2 * KT, :], src).then_inc(mod_loaded, 16)

        @block.tensor
        def _(pe):
            pe.sem_inc(w_turned, 2)
            pe.wait_ge(ident_ready, 2)
            pe.wait_ge(small_loaded, 16 * (6 + E))
            nc.tensor.transpose(ps_small[:, 0:CB], c_in[:], ident[0:CB, 0:CB])
            nc.tensor.transpose(ps_small[:, P:P + 3 * KT], bias_in[:], ident[0:3 * KT, 0:3 * KT]).then_inc(small_done, 1)
            pe.wait_ge(silu_ready, 1)
            for r in range(ROUNDS):
                pe.wait_ge(wm_loaded[r % 2], 16 * (r // 2 + 1))
                for k in range(KT):
                    for j in range(4):
                        last = nc.tensor.matmul(ps_mod[32 * j:32 * j + NB, r], silu_c[:, k], wm[:, r % 2, k, j * BANK:(j + 1) * BANK],
                                                start=k == 0, stop=k == KT - 1)
                last.then_inc(mod_done, 1)
            for k in range(KT):
                pe.wait_ge(small_copied, k + 1)
                nc.tensor.transpose(ps_small[:, 0:NR], down_in[:, k * P:(k + 1) * P], ident[0:NR, 0:NR])
                nc.tensor.transpose(ps_small[0:ER, P:2 * P], up_in[:, k], ident[:]).then_inc(small_done, 1)
            for m in range(4):
                with pe.Fori(0, KT // 2) as tt:
                    for i in range(2):
                        n = m * KT + tt * 2 + i
                        pe.wait_ge(w_loaded[i], 16 * (m * (KT // 2) + tt + 1))
                        pe.wait_ge(w_lo_done, n + 1)
                        for k in range(KT):
                            last = nc.tensor.transpose(ps_w[:, i, k * P:(k + 1) * P], w_in[:, i, k * P:(k + 1) * P], ident[:])
                        last.then_inc(w_turned, 1)
            pe.wait_ge(mod_loaded, 16 * 2 * NB)
            pe.wait_ge(small_copied, KT + 1)
            nc.tensor.transpose(ps_small[:, 0:MR], mod1_in[:], ident[0:MR, 0:MR])
            nc.tensor.transpose(ps_small[:, P:P + MR], mod2_in[:], ident[0:MR, 0:MR]).then_inc(small_done, 1)

        @block.scalar
        def _(act):
            act.wait_ge(small_done, 1)
            nc.scalar.activation(silu_e[:], ps_small[:, 0:CB], ACT.Exp, scale=-1.0).then_inc(silu_exp, 1)
            for m in range(4):
                with act.Fori(0, KT // 2) as tt:
                    for i in range(2):
                        n = m * KT + tt * 2 + i
                        act.wait_ge(w_turned, n + 3)
                        act.wait_ge(w_stored[i], 32 * (m * (KT // 2) + tt + 1))
                        nc.scalar.activation(w_hi[:, i], ps_w[:, i], ACT.Copy).then_inc(w_hi_done, 1)
                        act.wait_ge(w_hi_done, n + 1)
                        act.dma_start(w_split[m, tt * 2 + i, 0], w_hi[:, i].bitcast(F32)).then_inc(w_stored[i], 16)
                        act.wait_ge(w_lo_done, n + 3)
                        act.dma_start(w_split[m, tt * 2 + i, 1], w_lo[:, i].bitcast(F32)).then_inc(w_stored[i], 16)
            for i in range(2):
                act.wait_ge(w_stored[i], 32 + 32 * 2 * KT)

        @block.vector
        def _(dve):
            dve.sem_inc(w_lo_done, 2)
            for i in range(2):
                dve.sem_inc(w_stored[i], 32)
            chain = Chain(dve, dve_chain, tally)
            dve.wait_ge(silu_exp, 1)
            chain.link(nc.vector.tensor_scalar_add(silu_e[:], silu_e[:], 1.0))
            chain.link(nc.vector.reciprocal(silu_r[:], silu_e[:]))
            nc.vector.tensor_tensor(silu_c[:].rearrange("p k b -> p b k"), ps_small[:, 0:CB].rearrange("p (b k) -> p b k", b=NB),
                                    silu_r[:].rearrange("p (b k) -> p b k", b=NB), ALU.mult).then_inc(silu_ready, 1)
            chain.link(nc.vector.tensor_copy(bias_col[:], ps_small[:, P:P + 3 * KT]))
            dve.sem_inc(small_copied, 1)
            for r in range(ROUNDS):
                dve.wait_ge(mod_done, r + 1)
                for j in range(4):
                    part = slice(32 * j, 32 * j + NB)
                    if (r * 4 + j) * BANK // D in (2, 5):
                        chain.link(nc.vector.tensor_scalar(sign[part], ps_mod[part, r], 0.0, 2.0, ALU.is_ge, ALU.mult))
                        chain.link(nc.vector.tensor_scalar(mag[part], ps_mod[part, r], -1.0, None, ALU.mult))
                        chain.link(nc.vector.tensor_tensor(mag[part], ps_mod[part, r], mag[part], ALU.max))
                        chain.link(nc.vector.tensor_scalar(mag[part], mag[part], 0.25, None, ALU.max))
                        chain.link(nc.vector.scalar_tensor_tensor(rows[part, r], sign[part], -1.0, mag[part], ALU.add, ALU.mult))
                    else:
                        chain.link(nc.vector.tensor_copy(rows[part, r], ps_mod[part, r]))
                dve.sem_inc(rows_ready, 1)
            for k in range(KT):
                dve.wait_ge(small_done, k + 2)
                chain.link(nc.vector.tensor_copy(down_t[:, k], ps_small[:, 0:NR]))
                nc.vector.tensor_copy(up_t[:, k * P:(k + 1) * P], ps_small[0:ER, P:2 * P]).then_inc(small_copied, 1)
            for m in range(4):
                with dve.Fori(0, KT // 2) as tt:
                    for i in range(2):
                        n = m * KT + tt * 2 + i
                        dve.wait_ge(w_hi_done, n + 1)
                        nc.vector.tensor_tensor(w_lo[:, i], ps_w[:, i], w_hi[:, i].bitcast(F32), ALU.subtract).then_inc(w_lo_done, 1)
            dve.wait_ge(small_done, KT + 2)
            for base, dst in ((0, mod1_col), (P, mod2_col)):
                src = ps_small[:, base:base + MR].rearrange("p (b v k) -> p b v k", b=NB, v=2)
                col = dst[:].rearrange("p (b v k) -> p b v k", b=NB, v=2)
                chain.link(nc.vector.tensor_copy(col[:, :, 0], src[:, :, 0]))
                chain.link(nc.vector.tensor_scalar_add(col[:, :, 1], src[:, :, 1], 1.0))


def project(nc, s):
    tally = s["tally"]
    (x, NB, L, D, KT, TT, QC, NG, ident, bias_col, mod1_col, w_split, qk_split, v_tok) = (
        s[n] for n in "x NB L D KT TT QC NG ident bias_col mod1_col w_split qk_split v_tok".split())
    NH = KT * QC
    UNITS = 3 * QC
    ORDER = (2, 0, 1)
    with ExitStack() as ctx:
        def sb(name, shape, dt=F32):
            return ctx.enter_context(nc.sbuf_tensor(name, shape, dt))

        def sem(name):
            return ctx.enter_context(nc.semaphore(name))

        xn = sb("xn", [P, TT, D])
        stats = sb("stats", [P, 2, 6])
        mean_var = sb("mean_var", [P, 2])
        rstd = sb("rstd", [P, 1])
        minus_half = sb("minus_half", [P, 1])
        h_full = sb("h_full", [P, 3, BANK])
        h_hi = sb("h_hi", [P, KT, L], F32R)
        h_lo = sb("h_lo", [P, KT, L], F32R)
        w_hi = sb("w_hi2", [P, 3, KT, P], F32R)
        w_lo = sb("w_lo2", [P, 3, KT, P], F32R)
        qk_hi = sb("qk_hi", [P, 2, L], F32R)
        qk_lo = sb("qk_lo", [P, 2, L], F32R)
        v_feat = sb("v_feat", [P, QC, BANK])
        v_out = sb("v_out", [P, TT, P])
        ps_h = [ctx.enter_context(nc.psum_tensor(f"ps_h{i}", [P, BANK], F32)) for i in range(2)]
        ps_u = [ctx.enter_context(nc.psum_tensor(f"ps_u{i}", [P, BANK], F32)) for i in range(2)]
        ps_v = [ctx.enter_context(nc.psum_tensor(f"ps_v{i}", [P, BANK], F32)) for i in range(QC)]

        x_loaded = [sem(f"x_loaded{i}") for i in range(QC)]
        var_ready, rstd_ready, dve_chain = sem("var_ready"), sem("rstd_ready"), sem("dve_chain2")
        xn_ready = sem("xn_ready")
        h_turned, h_full_done, h_hi_done, h_lo_done = sem("h_turned"), sem("h_full_done"), sem("h_hi_done"), sem("h_lo_done")
        w_loaded = [sem(f"w_loaded_{n}") for n in "vqk"]
        unit_done, unit_free, hi_done = sem("unit_done"), sem("unit_free"), sem("hi_done")
        v_turned, v_copied = sem("v_turned"), sem("v_copied")
        v_stored, q_stored, k_stored = sem("v_stored"), sem("q_stored"), sem("k_stored")
        half_set = sem("half_set")
        block = ctx.enter_context(nc.Block())

        def load_weights(sp, m, g):
            w = ORDER[m]
            sp.dma_start(w_hi[:, m].bitcast(F32), w_split[w, g, 0].rearrange("p (k n) -> p k n", k=KT)).then_inc(w_loaded[m], 16)
            sp.dma_start(w_lo[:, m].bitcast(F32), w_split[w, g, 1].rearrange("p (k n) -> p k n", k=KT)).then_inc(w_loaded[m], 16)

        def load_x(sp, b):
            for i in range(QC):
                half = TT // QC
                sp.dma_start(xn[:, i * half:(i + 1) * half], x[b, i * BANK:(i + 1) * BANK, :].rearrange("(t p) d -> p t d", p=P)).then_inc(x_loaded[i], 16)

        @block.sync
        def _(sp):
            load_x(sp, 0)
            for m in range(3):
                load_weights(sp, m, 0)

            def batch(b, more):
                if more:
                    wait_apart(sp, h_turned, NH * (b + 1), tally)
                    load_x(sp, b + 1)
                with sp.Fori(0, KT) as g:
                    n = b * KT + g
                    after = (g + 1) % KT
                    wait_apart(sp, unit_done, UNITS * n + 2, tally)
                    load_weights(sp, 0, after)
                    wait_apart(sp, unit_done, UNITS * n + 4, tally)
                    load_weights(sp, 1, after)
                    wait_apart(sp, v_copied, QC * (n + 2), tally)
                    sp.dma_start(v_tok[n], v_out[:]).then_inc(v_stored, 16)
                    sp.wait_ge(unit_free, UNITS * n + 4 + 2)
                    sp.dma_start(qk_split[n, 0], qk_hi[:, 0].bitcast(F32)).then_inc(q_stored, 16)
                    sp.dma_start(qk_split[n, 1], qk_lo[:, 0].bitcast(F32)).then_inc(q_stored, 16)
                    wait_apart(sp, unit_done, UNITS * n + 6, tally)
                    load_weights(sp, 2, after)
                    sp.wait_ge(unit_free, UNITS * n + 6 + 2)
                    sp.dma_start(qk_split[n, 2], qk_hi[:, 1].bitcast(F32)).then_inc(k_stored, 16)
                    sp.dma_start(qk_split[n, 3], qk_lo[:, 1].bitcast(F32)).then_inc(k_stored, 16)

            with sp.Fori(0, NB - 1) as b:
                batch(b, True)
            batch(NB - 1, False)
            sp.wait_ge(v_stored, 16 * (NG + 1))
            sp.wait_ge(q_stored, 32 * (NG + 1))
            sp.wait_ge(k_stored, 32 * (NG + 1))
            for m in range(3):
                sp.wait_ge(w_loaded[m], 32 * (NG + 1))

        @block.gpsimd
        def _(pool):
            nc.gpsimd.memset(minus_half[:], -0.5).then_inc(half_set, 1)
            pool.wait_ge(half_set, 1)

            def rsqrt(tile):
                pool.wait_ge(var_ready, tile + 1)
                nc.gpsimd.tensor_tensor(rstd[:], mean_var[:, 1:2], minus_half[:], ALU.pow).then_inc(rstd_ready, 1)

            def batch(b, more):
                for i in range(NH):
                    half, k = divmod(i, KT)
                    pool.wait_ge(h_hi_done, NH * b + i + 1)
                    cols = slice(half * BANK, (half + 1) * BANK)
                    nc.gpsimd.tensor_tensor(h_lo[:, k, cols], h_full[:, i % 3], h_hi[:, k, cols].bitcast(F32), ALU.subtract).then_inc(h_lo_done, 1)
                if more:
                    with pool.Fori(0, TT) as t:
                        rsqrt((b + 1) * TT + t)

            with pool.Fori(0, TT) as t:
                rsqrt(t)
            with pool.Fori(0, NB - 1) as b:
                batch(b, True)
            batch(NB - 1, False)

        @block.scalar
        def _(act):
            for st, n in ((v_stored, 16), (q_stored, 32), (k_stored, 32)):
                act.sem_inc(st, n)
            act.sem_inc(v_copied, QC)

            def split_hi(n, g, u):
                m, ch = divmod(u, QC)
                if ch == 0:
                    act.wait_ge((q_stored, k_stored)[m - 1], 32 * (n + 1))
                wait_apart(act, unit_done, UNITS * n + u + 1, tally)
                bias = bias_col[:, bass.ds(ORDER[m] * KT + g, 1)]
                nc.scalar.activation(qk_hi[:, m - 1, ch * BANK:(ch + 1) * BANK], ps_u[u % 2][:], ACT.Identity, bias=bias, scale=1.0).then_inc(hi_done, 1)

            def copy_v(n, ch):
                act.wait_ge(v_turned, QC * n + ch + 1)
                if ch == 0:
                    act.wait_ge(v_stored, 16 * (n + 1))
                half = TT // QC
                nc.scalar.activation(v_out[:, ch * half:(ch + 1) * half], ps_v[ch][:].rearrange("p (t n) -> p t n", n=P), ACT.Copy).then_inc(v_copied, 1)

            with act.Fori(0, NB) as b:
                for i in range(NH):
                    half, k = divmod(i, KT)
                    act.wait_ge(h_full_done, NH * b + i + 1 + 2)
                    nc.scalar.activation(h_hi[:, k, half * BANK:(half + 1) * BANK], h_full[:, i % 3], ACT.Copy).then_inc(h_hi_done, 1)
                with act.Fori(0, KT) as g:
                    n = b * KT + g
                    split_hi(n, g, 2)
                    copy_v(n, 0)
                    copy_v(n, 1)
                    split_hi(n, g, 3)
                    split_hi(n, g, 4)
                    split_hi(n, g, 5)

        @block.vector
        def _(dve):
            dve.sem_inc(unit_free, 2)
            dve.sem_inc(h_full_done, 2)
            dve.sem_inc(h_lo_done, 3)

            def layernorm(tile, t):
                chain = Chain(dve, dve_chain, tally, tile * 3)
                src = xn[:, t]
                for i in range(2):
                    last = nc.vector.bn_stats(stats[:, i], src[:, i * (D // 2):(i + 1) * (D // 2)])
                    chain.link(last)
                chain.link(nc.vector.bn_aggr(mean_var[:], stats[:].rearrange("p a b -> p (a b)")))
                nc.vector.tensor_scalar_add(mean_var[:, 1:2], mean_var[:, 1:2], EPS).then_inc(var_ready, 1)
                dve.wait_ge(rstd_ready, tile + 1)
                nc.vector.tensor_scalar(src, src, mean_var[:, 0:1], rstd[:], ALU.subtract, ALU.mult).then_inc(xn_ready, 1)

            def batch(b, more):
                cols = mod1_col[:].rearrange("p (b v k) -> p b v k", b=NB, v=2)
                for i in range(NH):
                    half, k = divmod(i, KT)
                    dve.wait_ge(h_turned, NH * b + i + 1)
                    dve.wait_ge(h_lo_done, NH * b + i + 1)
                    nc.vector.tensor_scalar(h_full[:, i % 3], ps_h[i % 2][:], cols[:, b, 1, k:k + 1], cols[:, b, 0, k:k + 1],
                                            ALU.mult, ALU.add).then_inc(h_full_done, 1)
                with dve.Fori(0, KT) as g:
                    n = b * KT + g
                    for u in range(UNITS):
                        m, ch = divmod(u, QC)
                        bias = bias_col[:, bass.ds(ORDER[m] * KT + g, 1)]
                        if m == 0:
                            dve.wait_ge(unit_done, UNITS * n + u + 1)
                            dve.wait_ge(v_copied, QC * n + ch + 1)
                            nc.vector.tensor_scalar(v_feat[:, ch], ps_u[u % 2][:], bias, None, ALU.add).then_inc(unit_free, 1)
                        else:
                            dve.wait_ge(hi_done, (UNITS - QC) * n + u - QC + 1)
                            part = slice(ch * BANK, (ch + 1) * BANK)
                            nc.vector.scalar_tensor_tensor(qk_lo[:, m - 1, part], ps_u[u % 2][:], bias, qk_hi[:, m - 1, part].bitcast(F32),
                                                           ALU.add, ALU.subtract).then_inc(unit_free, 1)
                    if more:
                        for i in range(QC):
                            dve.wait_ge(x_loaded[i], 16 * (b + 2))
                        layernorm((b + 1) * TT + g, g)

            for i in range(QC):
                dve.wait_ge(x_loaded[i], 16)
                half = TT // QC
                with dve.Fori(i * half, (i + 1) * half) as t:
                    layernorm(t, t)
            with dve.Fori(0, NB - 1) as b:
                batch(b, True)
            batch(NB - 1, False)

        @block.tensor
        def _(pe):
            with pe.Fori(0, NB) as b:
                for i in range(NH):
                    half, k = divmod(i, KT)
                    if k == 0:
                        pe.wait_ge(xn_ready, TT * b + (half + 1) * (TT // QC))
                    pe.wait_ge(h_full_done, NH * b + i + 1)
                    for t in range(BANK // P):
                        last = nc.tensor.transpose(ps_h[i % 2][:, t * P:(t + 1) * P], xn[:, half * (BANK // P) + t, k * P:(k + 1) * P], ident[:])
                    last.then_inc(h_turned, 1)
                pe.wait_ge(h_hi_done, NH * (b + 1))
                wait_apart(pe, h_lo_done, NH * (b + 1) + 3, tally)
                with pe.Fori(0, KT) as g:
                    n = b * KT + g

                    def unit(u):
                        m, ch = divmod(u, QC)
                        if ch == 0:
                            pe.wait_ge(w_loaded[m], 32 * (n + 1))
                        pe.wait_ge(unit_free, UNITS * n + u + 1)
                        tok = slice(ch * BANK, (ch + 1) * BANK)
                        for k in range(KT):
                            for j, (w, h) in enumerate(((w_hi, h_hi), (w_lo, h_hi), (w_hi, h_lo))):
                                last = nc.tensor.matmul(ps_u[u % 2][:], w[:, m, k], h[:, k, tok], start=k == 0 and j == 0, stop=k == KT - 1 and j == 2)
                        last.then_inc(unit_done, 1)

                    def turn_v(ch):
                        pe.wait_ge(unit_free, UNITS * n + ch + 1 + 2)
                        pe.wait_ge(v_copied, QC * n + ch + 1)
                        for t in range(BANK // P):
                            last = nc.tensor.transpose(ps_v[ch][:, t * P:(t + 1) * P], v_feat[:, ch, t * P:(t + 1) * P], ident[:])
                        last.then_inc(v_turned, 1)

                    unit(0)
                    unit(1)
                    unit(2)
                    turn_v(0)
                    turn_v(1)
                    for u in range(3, UNITS):
                        unit(u)


def attend(nc, s):
    tally = s["tally"]
    (L, KT, TT, HD, HG, QC, NG, SCALE, QK_ROWS, SHIFT_ROW, ident, qk_split, v_tok, att_split) = (
        s[n] for n in "L KT TT HD HG QC NG SCALE QK_ROWS SHIFT_ROW ident qk_split v_tok att_split".split())
    SLOTS = 4
    CT = BANK // P
    steps = [(ch, j) for ch in range(QC) for j in range((ch + 1) * CT)]
    NSTEP = len(steps)
    diagonal = [k for k, (ch, j) in enumerate(steps) if j >= ch * CT]
    PBUF = 3
    rows = [(i, ch, h) for i in range(TT) for ch in range(i // CT + 1) for h in range(HG)]
    NROW = len(rows)
    ROW_USES = NROW + 1
    PER_STEP = [5] * 8 + [4] * 2
    assert sum(PER_STEP) == NROW and NG % SLOTS == 0 and NSTEP % PBUF == 0
    with ExitStack() as ctx:
        def sb(name, shape, dt=F32):
            return ctx.enter_context(nc.sbuf_tensor(name, shape, dt))

        def sem(name):
            return ctx.enter_context(nc.semaphore(name))

        q_st = [sb(f"q_st{i}", [SHIFT_ROW + 1, HG, L], F32R) for i in range(SLOTS)]
        k_st = [sb(f"k_st{i}", [SHIFT_ROW + 1, HG, L], F32R) for i in range(SLOTS)]
        v_sb = [sb(f"v_sb{i}", [P, TT, P]) for i in range(SLOTS)]
        prob = sb("prob", [P, PBUF, HG, BANK])
        ones = sb("ones", [P, HD])
        ident_b = sb("ident_b", [P, P], BF16)
        mask_b = sb("mask_b", [P, P], BF16)
        part_max = sb("part_max", [P, HG * TT, QC])
        row_max = sb("row_max", [P, HG * TT])
        shift = sb("shift", [HG * TT, P], F32R)
        inv_sum = sb("inv_sum", [P, BANK])
        att_full = sb("att_full", [P, QC, BANK])
        att_hi = sb("att_hi", [P, L], F32R)
        att_lo = sb("att_lo", [P, L], F32R)
        ps_s = [ctx.enter_context(nc.psum_tensor(f"ps_s{i}", [P, 2, BANK], F32)) for i in range(2)]
        ps_r = [ctx.enter_context(nc.psum_tensor(f"ps_r{i}", [P, BANK], F32)) for i in range(2)]
        ps_o = ctx.enter_context(nc.psum_tensor("ps_o", [P, BANK], F32))
        ps_sum = ctx.enter_context(nc.psum_tensor("ps_sum", [P, BANK], F32))

        const_ready, pool_const = sem("const_ready"), sem("pool_const")
        qkv_loaded = [sem(f"qkv_loaded{i}") for i in range(SLOTS)]
        slot_free = sem("slot_free")
        row_done, row_free, max_ready, dve_chain = sem("row_done"), sem("row_free"), sem("max_ready"), sem("dve_chain3")
        shift_loaded = [sem(f"shift_loaded{i}") for i in range(SLOTS)]
        score_done, score_free, masked = sem("score_done"), sem("score_free"), sem("masked")
        prob_free, out_free = sem("prob_free"), sem("out_free")
        att_done, att_hi_done, att_lo_done, att_stored = sem("att_done"), sem("att_hi_done"), sem("att_lo_done"), sem("att_stored")
        block = ctx.enter_context(nc.Block())

        def groups(eng, body):
            with eng.Fori(0, NG // SLOTS - 1) as tb:
                for i in range(SLOTS):
                    body(tb, i, False)
            for i in range(SLOTS):
                body(NG // SLOTS - 1, i, True)

        @block.sync
        def _(sp):
            def load(t, slot):
                for place, part in ((0, 0), (1, 1), (2, 0)):
                    sp.dma_start(q_st[slot][place * HD:(place + 1) * HD].bitcast(F32), qk_split[t, part].rearrange("(h d) n -> d h n", d=HD)).then_inc(qkv_loaded[slot], 16)
                for place, part in ((0, 2), (1, 2), (2, 3)):
                    sp.dma_start(k_st[slot][place * HD:(place + 1) * HD].bitcast(F32), qk_split[t, part].rearrange("(h d) n -> d h n", d=HD)).then_inc(qkv_loaded[slot], 16)
                sp.dma_start(v_sb[slot][:], v_tok[t]).then_inc(qkv_loaded[slot], 16)

            def load_shift(t, slot):
                sp.wait_ge(row_free, ROW_USES * (t + 1) + 2)
                sp.dma_start(q_st[slot][SHIFT_ROW:SHIFT_ROW + 1].bitcast(F32).rearrange("o h n -> o (h n)"),
                             shift[:].bitcast(F32)).then_inc(shift_loaded[slot], 16)

            for t in range(SLOTS - 1):
                load(t, t)
            load_shift(0, 0)

            def group(tb, i, last):
                t = tb * SLOTS + i
                if not (last and i > 0):
                    sp.wait_ge(slot_free, t + 1)
                    load(t + SLOTS - 1, (i + SLOTS - 1) % SLOTS)
                if not (last and i == SLOTS - 1):
                    load_shift(t + 1, (i + 1) % SLOTS)
                sp.wait_ge(att_lo_done, QC * (t + 1) + QC)
                b, g = (tb * SLOTS + i) // KT, (tb * SLOTS + i) % KT
                sp.dma_start(att_split[b, 0, g], att_hi[:].bitcast(F32)).then_inc(att_stored, 16)
                sp.dma_start(att_split[b, 1, g], att_lo[:].bitcast(F32)).then_inc(att_stored, 16)

            groups(sp, group)
            sp.wait_ge(att_stored, 32 * (NG + 1))

        @block.gpsimd
        def _(pool):
            for i in range(SLOTS):
                nc.gpsimd.memset(k_st[i][SHIFT_ROW:SHIFT_ROW + 1].bitcast(F32), 1.0).then_inc(const_ready, 1)
            pool.wait_ge(const_ready, SLOTS)
            nc.gpsimd.memset(ones[:], 1.0).then_inc(const_ready, 1)
            nc.gpsimd.memset(mask_b[:], 0.0).then_inc(pool_const, 1)
            nc.gpsimd.tensor_copy(ident_b[:], ident[:]).then_inc(const_ready, 1)
            pool.wait_ge(pool_const, 1)
            nc.gpsimd.affine_select(out=mask_b[:], in_=mask_b[:], compare_op=ALU.is_ge, fill=MASKED, base=0,
                                    pattern=[[-1, P]], channel_multiplier=1).then_inc(const_ready, 1)
            pool.sem_inc(att_lo_done, QC)

            def split(t, ch):
                cols = slice(ch * BANK, (ch + 1) * BANK)
                if ch == 0:
                    pool.wait_ge(att_stored, 32 * (t + 1))
                wait_apart(pool, att_done, QC * t + ch + 1, tally)
                nc.gpsimd.tensor_copy(att_hi[:, cols], att_full[:, ch]).then_inc(att_hi_done, 1)
                pool.wait_ge(att_hi_done, QC * t + ch + 1)
                nc.gpsimd.tensor_tensor(att_lo[:, cols], att_full[:, ch], att_hi[:, cols].bitcast(F32), ALU.subtract).then_inc(att_lo_done, 1)

            def group(tb, i, last):
                t = tb * SLOTS + i
                for k, (ch, j) in enumerate(steps):
                    if k in diagonal:
                        wait_apart(pool, score_free, 2 * NSTEP * t + 2 * (k + 1) + 2, tally)
                        off = j * P - ch * BANK
                        block_p = prob[:, k % PBUF, :, off:off + P]
                        nc.gpsimd.affine_select(out=block_p, in_=block_p, compare_op=ALU.is_ge, fill=0.0, base=0,
                                                pattern=[[0, HG], [1, P]], channel_multiplier=-1).then_inc(masked, 1)
                    if k == CT + 4:
                        split(t, 0)
                split(t, 1)

            groups(pool, group)

        @block.scalar
        def _(act):
            act.sem_inc(score_free, 2)
            act.sem_inc(att_stored, 32)

            def group(tb, i, last):
                t = tb * SLOTS + i
                for k, (ch, j) in enumerate(steps):
                    off = max(j * P - ch * BANK, 0)
                    act.wait_ge(prob_free, NSTEP * t + k + 1)
                    for pair in range(2):
                        act.wait_ge(score_done, 2 * NSTEP * t + 2 * k + pair + 1)
                        nc.scalar.activation(prob[:, k % PBUF, 2 * pair:2 * pair + 2, off:], ps_s[pair][:, :, off:], ACT.Exp, scale=SCALE).then_inc(score_free, 1)

            groups(act, group)

        @block.vector
        def _(dve):
            dve.sem_inc(row_free, 2)
            dve.sem_inc(out_free, 1)
            nc.vector.memset(part_max[:], MASKED).then_inc(dve_chain, 1)
            dve.wait_ge(dve_chain, 1)

            def max_row(t, parity, u):
                i, ch, h = rows[u]
                width = min(BANK, (i + 1) * P - ch * BANK)
                dve.wait_ge(row_done, ROW_USES * t + u + 1)
                nc.vector.reduce_max(part_max[:, h * TT + i, ch:ch + 1], ps_r[(parity + u) % 2][:, 0:width], AX.X).then_inc(row_free, 1)

            def max_all(t, parity, before):
                dve.wait_ge(row_free, ROW_USES * t + NROW + 2)
                nc.vector.reduce_max(row_max[:], part_max[:], AX.X).then_inc(max_ready, 1)
                if before is not None:
                    dve.wait_ge(*before)
                dve.wait_ge(row_done, ROW_USES * t + NROW + 1)
                nc.vector.tensor_scalar(shift[:], ps_r[(parity + NROW) % 2][0:HG * TT, 0:P], -1.0, None, ALU.mult).then_inc(row_free, 1)

            def normalize(t, ch):
                dve.wait_ge(prob_free, NSTEP * t + (CT if ch == 0 else NSTEP) + PBUF)
                nc.vector.reciprocal(inv_sum[:], ps_sum[:]).then_inc(dve_chain, 1)
                dve.wait_ge(dve_chain, QC * t + ch + 2)
                dve.wait_ge(att_lo_done, QC * t + ch + 1)
                nc.vector.tensor_tensor(att_full[:, ch], ps_o[:], inv_sum[:], ALU.mult).then_inc(out_free, 1)
                dve.wait_ge(out_free, QC * t + ch + 2)
                dve.sem_inc(att_done, 1)

            for u in range(NROW):
                max_row(0, 0, u)
            max_all(0, 0, None)

            def group(tb, i, last):
                t = tb * SLOTS + i
                ahead = not (last and i == SLOTS - 1)
                u = 0
                for k in range(NSTEP):
                    if ahead and k < len(PER_STEP):
                        for _ in range(PER_STEP[k]):
                            max_row(t + 1, i + 1, u)
                            u += 1
                    if k == CT:
                        normalize(t, 0)
                if ahead:
                    max_all(t + 1, i + 1, (shift_loaded[i], 16 * (tb + 1)))
                normalize(t, 1)

            groups(dve, group)

        @block.tensor
        def _(pe):
            pe.sem_inc(prob_free, PBUF)
            pe.sem_inc(slot_free, 1)
            pe.wait_ge(const_ready, SLOTS + 3)

            def row(t, parity, slot, u):
                i, ch, h = rows[u]
                width = min(BANK, (i + 1) * P - ch * BANK)
                cols = max(width, 2 * P)
                on_diagonal = ch == i // CT
                bank = ps_r[(parity + u) % 2]
                pe.wait_ge(row_free, ROW_USES * t + u + 1)
                last = nc.tensor.matmul(bank[:, 0:cols], q_st[slot][0:QK_ROWS, h, i * P:(i + 1) * P],
                                        k_st[slot][0:QK_ROWS, h, ch * BANK:ch * BANK + cols], start=True, stop=not on_diagonal)
                if on_diagonal:
                    last = nc.tensor.matmul(bank[:, width - P:width], ident_b[:], mask_b[:], start=False, stop=True)
                last.then_inc(row_done, 1)

            def turn_max(t, parity):
                pe.wait_ge(max_ready, t + 1)
                pe.wait_ge(row_free, ROW_USES * t + NROW + 1)
                nc.tensor.transpose(ps_r[(parity + NROW) % 2][0:HG * TT, 0:P], row_max[:], ident[:]).then_inc(row_done, 1)

            def scores(t, slot, k):
                ch, j = steps[k]
                off = max(j * P - ch * BANK, 0)
                off = min(off, BANK - 2 * P)
                for pair in range(2):
                    pe.wait_ge(score_free, 2 * NSTEP * t + 2 * k + pair + 1)
                    for h in range(2):
                        last = nc.tensor.matmul(ps_s[pair][:, h, off:], k_st[slot][:, 2 * pair + h, j * P:(j + 1) * P],
                                                q_st[slot][:, 2 * pair + h, ch * BANK + off:(ch + 1) * BANK], start=True, stop=True)
                    last.then_inc(score_done, 1)

            def weigh(t, slot, k):
                ch, j = steps[k]
                off = max(j * P - ch * BANK, 0)
                if j == 0:
                    pe.wait_ge(out_free, QC * t + ch + 1)
                if k in diagonal:
                    pe.wait_ge(masked, len(diagonal) * t + diagonal.index(k) + 1)
                else:
                    pe.wait_ge(score_free, 2 * NSTEP * t + 2 * (k + 1) + 2)
                final = j == (ch + 1) * CT - 1
                for dst, src in ((ps_o, v_sb[slot]), (ps_sum, None)):
                    for h in range(HG):
                        part = slice(h * HD, (h + 1) * HD)
                        lhs = ones[:] if src is None else src[:, j, part]
                        last = nc.tensor.matmul(dst[part, off:], lhs, prob[:, k % PBUF, h, off:], start=j == 0, stop=final)
                last.then_inc(prob_free, 1)

            pe.wait_ge(qkv_loaded[0], 16 * 7)
            for u in range(NROW):
                row(0, 0, 0, u)
            turn_max(0, 0)

            def group(tb, i, last):
                t = tb * SLOTS + i
                ahead = not (last and i == SLOTS - 1)
                after = (i + 1) % SLOTS
                pe.wait_ge(shift_loaded[i], 16 * (tb + 1))
                if ahead:
                    pe.wait_ge(qkv_loaded[after], 16 * 7 * (tb + 1 + (i + 1) // SLOTS))
                u = 0
                for k in range(NSTEP):
                    scores(t, i, k)
                    if ahead and k < len(PER_STEP):
                        for _ in range(PER_STEP[k]):
                            row(t + 1, i + 1, after, u)
                            u += 1
                    if k > 0:
                        weigh(t, i, k - 1)
                if ahead:
                    turn_max(t + 1, i + 1)
                weigh(t, i, NSTEP - 1)
                pe.wait_ge(prob_free, NSTEP * (t + 1) + PBUF)
                pe.sem_inc(slot_free, 1)

            groups(pe, group)


def finish(nc, s):
    tally = s["tally"]
    (x, out, bo, NB, L, D, KT, E, R, ER, NR, ident, mod2_col, down_t, up_t, mod_rows, w_split, att_split) = (
        s[n] for n in "x out bo NB L D KT E R ER NR ident mod2_col down_t up_t mod_rows w_split att_split".split())
    T = 2
    CW = T * P
    CPB = L // CW
    NC = NB * CPB
    HV = D // BANK
    UN = T * HV
    KP = BANK // CW
    TG = KT // KP
    with ExitStack() as ctx:
        def sb(name, shape, dt=F32):
            return ctx.enter_context(nc.sbuf_tensor(name, shape, dt))

        def sem(name):
            return ctx.enter_context(nc.semaphore(name))

        wo_hi = sb("wo_hi", [P, KT, D], F32R)
        wo_lo = sb("wo_lo", [P, KT, D], F32R)
        at_hi = [sb(f"at_hi{i}", [P, KT, CW], F32R) for i in range(2)]
        at_lo = [sb(f"at_lo{i}", [P, KT, CW], F32R) for i in range(2)]
        res = [sb(f"res{i}", [P, T, D]) for i in range(2)]
        gates_bc = sb("gates_bc", [P, 2, NB, D])
        bo_bc = sb("bo_bc", [P, D])
        att_y = sb("att_y", [P, T, D])
        xn = sb("xn4", [P, T, D])
        h2t = sb("h2t", [P, KT, CW])
        delta = sb("delta", [P, T, D])
        stats = sb("stats4", [P, 2, 6])
        mean_var = sb("mean_var4", [P, T, 2])
        rstd = sb("rstd4", [P, T])
        minus_half = sb("minus_half4", [P, 1])
        lower = sb("lower", [P, E, E])
        down = sb("down", [P, T, NR])
        top1 = sb("top1", [P, T])
        above = sb("above", [P, T, E, E])
        equal = sb("equal", [P, T, E, E])
        rank = sb("rank", [P, T, E])
        logit = sb("logit", [P, T, E])
        expo = sb("expo", [P, T, E])
        kept = sb("kept", [P, T, E])
        denom = sb("denom", [P, T])
        gate = sb("gate", [P, T, E])
        mid = sb("mid", [P, T, ER])
        mid_t = sb("mid_t", [ER, CW])
        ps_y = [ctx.enter_context(nc.psum_tensor(f"ps_y{i}", [P, BANK], F32)) for i in range(UN)]
        ps_t = [ctx.enter_context(nc.psum_tensor(f"ps_t{i}", [P, BANK], F32)) for i in range(2)]
        ps_l = ctx.enter_context(nc.psum_tensor("ps_l", [P, BANK], F32))
        ps_d = ctx.enter_context(nc.psum_tensor("ps_d", [P, BANK], F32))

        wo_loaded, bc_loaded, const_ready = sem("wo_loaded"), sem("bc_loaded"), sem("const_ready4")
        at_loaded = [sem(f"at_loaded{i}") for i in range(2)]
        res_loaded = [sem(f"res_loaded{i}") for i in range(2)]
        y_done, y_free, gated, x1_ready = sem("y_done"), sem("y_free"), sem("gated"), sem("x1_ready")
        dve_chain, var_ready, rstd_ready, xn_ready = sem("dve_chain4"), sem("var_ready4"), sem("rstd_ready4"), sem("xn_ready4")
        turned, h2_ready, down_done = sem("turned"), sem("h2_ready"), sem("down_done")
        logit_ready, exp_ready, mid_ready = sem("logit_ready"), sem("exp_ready"), sem("mid_ready")
        mid_turned, mid_t_ready = sem("mid_turned"), sem("mid_t_ready")
        d_done, d_free, out_ready, out_stored = sem("d_done"), sem("d_free"), sem("out_ready"), sem("out_stored")
        block = ctx.enter_context(nc.Block())

        def chunks(eng, body):
            with eng.Fori(0, NB - 1) as b:
                for i in range(CPB):
                    body(b, i, False)
            for i in range(CPB):
                body(NB - 1, i, True)

        def tokens(a, b, i):
            return a[b + i // CPB, (i % CPB) * CW:(i % CPB + 1) * CW, :].rearrange("(t p) d -> p t d", p=P)

        @block.sync
        def _(sp):
            def load_at(b, i):
                for w, dst in ((0, at_hi), (1, at_lo)):
                    src = att_split[b + i // CPB, w].rearrange("g p n -> p g n")[:, :, (i % CPB) * CW:(i % CPB + 1) * CW]
                    sp.dma_start(dst[i % 2][:].bitcast(F32), src).then_inc(at_loaded[i % 2], 16)

            def load_res(b, i):
                sp.dma_start(res[i % 2][:], tokens(x, b, i)).then_inc(res_loaded[i % 2], 16)

            load_at(0, 0)
            for w, dst in ((0, wo_hi), (1, wo_lo)):
                for t in range(KT):
                    sp.dma_start(dst[:, :, t * P:(t + 1) * P].bitcast(F32), w_split[3, t, w].rearrange("p (g n) -> p g n", g=KT)).then_inc(wo_loaded, 16)
            sp.dma_start(bo_bc[:], bo.rearrange("(o d) -> o d", o=1).to_broadcast([P, D])).then_inc(bc_loaded, 16)
            for b in range(NB):
                for n, v in enumerate((2, 5)):
                    sp.dma_start(gates_bc[:, n, b], mod_rows[b:b + 1, v * D:(v + 1) * D].to_broadcast([P, D])).then_inc(bc_loaded, 16)
            load_res(0, 0)
            load_at(0, 1)
            load_res(0, 1)
            sp.wait_ge(y_done, UN)
            load_at(0, 2)

            def chunk(b, i, last):
                n = b * CPB + i
                if not (last and i + 3 >= CPB):
                    sp.wait_ge(y_done, UN * (n + 2))
                    load_at(b, i + 3)
                sp.wait_ge(out_ready, T * (n + 1))
                sp.dma_start(tokens(out, b, i), delta[:]).then_inc(out_stored, 16)
                if not (last and i + 2 >= CPB):
                    load_res(b, i + 2)

            chunks(sp, chunk)
            sp.wait_ge(out_stored, 16 * (NC + 1))

        @block.gpsimd
        def _(pool):
            nc.gpsimd.memset(minus_half[:], -0.5).then_inc(const_ready, 1)
            nc.gpsimd.memset(lower[:], 1.0).then_inc(const_ready, 1)
            pool.wait_ge(const_ready, 2)
            nc.gpsimd.affine_select(out=lower[:], in_=lower[:], compare_op=ALU.is_gt, fill=0.0, base=0,
                                    pattern=[[1, E], [-1, E]], channel_multiplier=0).then_inc(const_ready, 1)
            pool.wait_ge(bc_loaded, 16 * (1 + 2 * NB))

            def residual(b, i, a):
                n = b * CPB + i
                bb = b + i // CPB
                wait_apart(pool, y_free, UN * n + HV * (a + 1) + UN, tally)
                nc.gpsimd.tensor_tensor(att_y[:, a], att_y[:, a], gates_bc[:, 0, bb], ALU.mult).then_inc(gated, 1)
                pool.wait_ge(gated, T * n + a + 1)
                pool.wait_ge(res_loaded[i % 2], 16 * (b * (CPB // 2) + i // 2 + 1))
                nc.gpsimd.tensor_tensor(res[i % 2][:, a], res[i % 2][:, a], att_y[:, a], ALU.add).then_inc(x1_ready, 1)

            def rsqrt(b, i, a):
                pool.wait_ge(var_ready, T * (b * CPB + i) + a + 1)
                nc.gpsimd.tensor_tensor(rstd[:, a:a + 1], mean_var[:, a, 1:2], minus_half[:], ALU.pow).then_inc(rstd_ready, 1)

            for a in range(T):
                residual(0, 0, a)
                rsqrt(0, 0, a)

            def chunk(b, i, last):
                n = b * CPB + i
                ahead = not (last and i == CPB - 1)
                if ahead:
                    residual(b, i + 1, 0)
                    rsqrt(b, i + 1, 0)
                    residual(b, i + 1, 1)
                for a in range(T):
                    pool.wait_ge(d_free, UN * n + HV * (a + 1) + 1)
                    nc.gpsimd.tensor_tensor(delta[:, a], delta[:, a], res[i % 2][:, a], ALU.add).then_inc(out_ready, 1)
                if ahead:
                    rsqrt(b, i + 1, 1)

            chunks(pool, chunk)

        @block.scalar
        def _(act):
            act.sem_inc(h2_ready, 2 * KP)
            cols = mod2_col[:].rearrange("p (b v k) -> p b v k", b=NB, v=2)

            def chunk(b, i, last):
                n = b * CPB + i
                for q in range(TG):
                    if q == 0:
                        act.wait_ge(down_done, n + 1)
                    wait_apart(act, turned, TG * n + q + 1, tally)
                    for j in range(KP):
                        k = q * KP + j
                        nc.scalar.activation(h2t[:, k], ps_t[q % 2][:, j * CW:(j + 1) * CW], ACT.Identity,
                                             bias=cols[:, b, 0, k:k + 1], scale=cols[:, b, 1, k:k + 1]).then_inc(h2_ready, 1)
                act.wait_ge(logit_ready, n + 1)
                nc.scalar.activation(expo[:], logit[:], ACT.Exp).then_inc(exp_ready, 1)

            chunks(act, chunk)

        @block.vector
        def _(dve):
            dve.sem_inc(y_free, UN)
            dve.sem_inc(d_free, 1)
            dve.sem_inc(mid_t_ready, 1)
            dve.sem_inc(out_stored, 16)

            def add_bo(b, i, u, first=False):
                n = b * CPB + i
                a, hv = divmod(u, HV)
                cols = slice(hv * BANK, (hv + 1) * BANK)
                dve.wait_ge(y_done, UN * n + u + 1)
                if hv == 0 and not first:
                    dve.wait_ge(x1_ready, T * (n - 1) + a + 1)
                nc.vector.tensor_tensor(att_y[:, a, cols], ps_y[u][:], bo_bc[:, cols], ALU.add).then_inc(y_free, 1)

            def layernorm(b, i, a, chain):
                n = b * CPB + i
                r = res[i % 2]
                dve.wait_ge(x1_ready, T * n + a + 1)
                for hv in range(2):
                    chain.link(nc.vector.bn_stats(stats[:, hv], r[:, a, hv * (D // 2):(hv + 1) * (D // 2)]))
                chain.link(nc.vector.bn_aggr(mean_var[:, a], stats[:].rearrange("p a b -> p (a b)")))
                nc.vector.tensor_scalar_add(mean_var[:, a, 1:2], mean_var[:, a, 1:2], EPS).then_inc(var_ready, 1)
                dve.wait_ge(rstd_ready, T * n + a + 1)
                nc.vector.tensor_scalar(xn[:, a], r[:, a], mean_var[:, a, 0:1], rstd[:, a:a + 1], ALU.subtract, ALU.mult).then_inc(xn_ready, 1)

            def gates(n, chain):
                dve.wait_ge(down_done, n + 2)
                chain.link(nc.vector.tensor_copy(down[:], ps_l[:, 0:T * NR].rearrange("p (t r) -> p t r", t=T)))
                lg = down[:, :, ER:NR]
                own = lg.unsqueeze(3).to_broadcast([P, T, E, E])
                other = lg.unsqueeze(2).to_broadcast([P, T, E, E])
                chain.link(nc.vector.reduce_max(top1[:], lg, AX.X))
                nc.vector.tensor_tensor(logit[:], lg, top1[:].unsqueeze(2).to_broadcast([P, T, E]), ALU.subtract).then_inc(logit_ready, 1)
                chain.link(nc.vector.tensor_tensor(above[:], other, own, ALU.is_gt))
                chain.link(nc.vector.tensor_tensor(equal[:], other, own, ALU.is_equal))
                chain.link(nc.vector.tensor_tensor(equal[:], equal[:], lower[:].unsqueeze(1).to_broadcast([P, T, E, E]), ALU.mult))
                chain.link(nc.vector.tensor_tensor(above[:], above[:], equal[:], ALU.add))
                chain.link(nc.vector.reduce_sum(rank[:], above[:], AX.X))
                dve.wait_ge(exp_ready, n + 1)
                chain.link(nc.vector.scalar_tensor_tensor(kept[:], rank[:], 2.0, expo[:], ALU.is_lt, ALU.mult))
                chain.link(nc.vector.reduce_sum(denom[:], kept[:], AX.X))
                chain.link(nc.vector.reciprocal(denom[:], denom[:]))
                chain.link(nc.vector.scalar_tensor_tensor(gate[:], kept[:], LORA_SCALE, denom[:].unsqueeze(2).to_broadcast([P, T, E]), ALU.mult, ALU.mult))
                nc.vector.tensor_tensor(mid[:].rearrange("p t (e r) -> p t e r", e=E), down[:, :, 0:ER].rearrange("p t (e r) -> p t e r", e=E),
                                        gate[:].unsqueeze(3).to_broadcast([P, T, E, R]), ALU.mult).then_inc(mid_ready, 1)

            def experts(b, i):
                n = b * CPB + i
                for u in range(UN):
                    a, hv = divmod(u, HV)
                    cols = slice(hv * BANK, (hv + 1) * BANK)
                    dve.wait_ge(d_done, UN * n + u + 1)
                    if u == 0:
                        dve.wait_ge(out_stored, 16 * (n + 1))
                    nc.vector.tensor_tensor(delta[:, a, cols], ps_d[:], gates_bc[:, 1, b, cols], ALU.mult).then_inc(d_free, 1)

            dve.wait_ge(bc_loaded, 16 * (1 + 2 * NB))
            dve.wait_ge(const_ready, 3)
            chain = Chain(dve, dve_chain, tally)
            for u in range(UN):
                add_bo(0, 0, u, first=True)
            for a in range(T):
                layernorm(0, 0, a, chain)
            PRO = 3 * T

            def chunk(b, i, last):
                n = b * CPB + i
                ahead = not (last and i == CPB - 1)
                chain = Chain(dve, dve_chain, tally, n * (PRO + 11) + PRO)
                if ahead:
                    add_bo(b, i + 1, 0)
                    add_bo(b, i + 1, 1)
                gates(n, chain)
                dve.wait_ge(mid_turned, n + 1)
                nc.vector.tensor_copy(mid_t[:], ps_l[0:ER, CW:CW + CW]).then_inc(mid_t_ready, 1)
                if ahead:
                    add_bo(b, i + 1, 2)
                    layernorm(b, i + 1, 0, chain)
                    add_bo(b, i + 1, 3)
                experts(b, i)
                if ahead:
                    layernorm(b, i + 1, 1, chain)

            chunks(dve, chunk)

        @block.tensor
        def _(pe):
            pe.sem_inc(down_done, 1)
            pe.wait_ge(wo_loaded, 16 * 2 * KT)

            def project(b, i, u):
                n = b * CPB + i
                a, hv = divmod(u, HV)
                if u == 0:
                    pe.wait_ge(at_loaded[i % 2], 32 * (b * (CPB // 2) + i // 2 + 1))
                pe.wait_ge(y_free, UN * n + u + 1)
                tok, cols = slice(a * P, (a + 1) * P), slice(hv * BANK, (hv + 1) * BANK)
                for g in range(KT):
                    for j, (h, w) in enumerate(((at_hi, wo_hi), (at_lo, wo_hi), (at_hi, wo_lo))):
                        last = nc.tensor.matmul(ps_y[u][:], h[i % 2][:, g, tok], w[:, g, cols], start=g == 0 and j == 0, stop=g == KT - 1 and j == 2)
                last.then_inc(y_done, 1)

            def turn(n):
                pe.wait_ge(xn_ready, T * (n + 1))
                for q in range(TG):
                    pe.wait_ge(h2_ready, KT * n + (q + 1) * KP)
                    for j in range(KP):
                        for a in range(T):
                            k = q * KP + j
                            last = nc.tensor.transpose(ps_t[q % 2][:, j * CW + a * P:j * CW + (a + 1) * P], xn[:, a, k * P:(k + 1) * P], ident[:])
                    last.then_inc(turned, 1)

            def go_down(n):
                pe.wait_ge(h2_ready, KT * (n + 1) + 2 * KP)
                pe.wait_ge(mid_t_ready, n + 1)
                for a in range(T):
                    for k in range(KT):
                        last = nc.tensor.matmul(ps_l[:, a * NR:(a + 1) * NR], h2t[:, k, a * P:(a + 1) * P], down_t[:, k], start=k == 0, stop=k == KT - 1)
                last.then_inc(down_done, 1)

            def turn_mid(n):
                wait_apart(pe, mid_ready, n + 1, tally)
                for a in range(T):
                    last = nc.tensor.transpose(ps_l[0:ER, CW + a * P:CW + (a + 1) * P], mid[:, a], ident[:])
                last.then_inc(mid_turned, 1)

            def go_up(n):
                pe.wait_ge(mid_t_ready, n + 2)
                for u in range(UN):
                    a, hv = divmod(u, HV)
                    pe.wait_ge(d_free, UN * n + u + 1)
                    nc.tensor.matmul(ps_d[:], mid_t[:, a * P:(a + 1) * P], up_t[:, hv * BANK:(hv + 1) * BANK], start=True, stop=True).then_inc(d_done, 1)

            for u in range(UN):
                project(0, 0, u)

            def chunk(b, i, last):
                n = b * CPB + i
                ahead = not (last and i == CPB - 1)
                for u, other in enumerate((turn, go_down, turn_mid, go_up)):
                    if ahead:
                        project(b, i + 1, u)
                    other(n)

            chunks(pe, chunk)


_INS = ["L0_attn_x", "L0_attn_Wq", "L0_attn_bq", "L0_attn_Wk", "L0_attn_bk", "L0_attn_Wv", "L0_attn_bv", "L0_attn_Wo",
        "L0_attn_bo", "L0_ffn_router_w", "L0_ffn_A", "L0_ffn_B", "L0_c", "L0_wmod"]


def kernel(**inputs):
    import concourse.bacc as _bacc
    from concourse.bass_utils import run_bass_kernel_spmd as _run

    nc = _bacc.Bacc("TRN2", target_bir_lowering=False, num_devices=1)
    arrays, args = {}, []
    for name in _INS:
        a = np.ascontiguousarray(inputs[name])
        arrays[f"in_{name}"] = a
        args.append(nc.dram_tensor(f"in_{name}", a.shape, mybir.dt.from_np(a.dtype), kind="ExternalInput").ap())
    out = nc.dram_tensor("out_x", arrays["in_L0_attn_x"].shape, F32, kind="ExternalOutput").ap()
    adaln_block(nc, *args, out)
    r = _run(nc, [arrays], core_ids=[0])
    return r.results[0]["out_x"]
```

```python
from contextlib import ExitStack

import numpy as np

import concourse.bass as bass
from concourse import mybir

F32 = mybir.dt.float32
F32R = mybir.dt.float32r
BF16 = mybir.dt.bfloat16
ALU = mybir.AluOpType
ACT = mybir.ActivationFunctionType
AX = mybir.AxisListType

P = 128
BANK = 512
HEADS = 32
EPS = 1e-5
LORA_SCALE = 4.0
MASKED = -3.0e38


def wait_apart(eng, sem, value, tally):
    eng.wait_ge(sem, value)
    eng.sem_inc(tally, 1)


class Chain:

    def __init__(self, eng, sem, tally, base=0):
        self.eng, self.sem, self.tally, self.value = eng, sem, tally, base

    def link(self, ins):
        ins.then_inc(self.sem, 1)
        self.value = self.value + 1
        wait_apart(self.eng, self.sem, self.value, self.tally)


def adaln_block(nc, x, Wq, bq, Wk, bk, Wv, bv, Wo, bo, router_w, lora_a, lora_b, c, wmod, out):
    NB, L, D = x.shape
    KT = D // P
    TT = L // P
    HD = D // HEADS
    HG = P // HD
    E, R, _ = lora_a.shape
    ER = E * R
    NR = ER + E
    QC = L // BANK
    NG = NB * KT
    SCALE = float(HD) ** -0.5
    QK_ROWS = 3 * HD
    SHIFT_ROW = QK_ROWS
    assert HD == 32 and L == 1024 and D == 1024

    mod_rows = nc.dram_tensor("mod_rows", [NB, 6 * D], F32).ap()
    w_split = nc.dram_tensor("w_split", [4, KT, 2, P, D], F32).ap()
    qk_split = nc.dram_tensor("qk_split", [NG, 4, P, L], F32).ap()
    v_tok = nc.dram_tensor("v_tok", [NG, P, TT, P], F32).ap()
    att_raw = nc.dram_tensor("att_raw", [NB, KT, P, L], F32).ap()
    att_sum = nc.dram_tensor("att_sum", [NB, KT, HG, L], F32).ap()
    att_inv = nc.dram_tensor("att_inv", [NB, KT, HG, L], F32).ap()

    with ExitStack() as top:
        def keep(name, shape, dt=F32):
            return top.enter_context(nc.sbuf_tensor(name, shape, dt))

        ident = keep("ident", [P, P])
        bias_col = keep("bias_col", [P, 3 * KT])
        mod1_col = keep("mod1_col", [P, NB * 2 * KT])
        mod2_col = keep("mod2_col", [P, NB * 2 * KT])
        down_t = keep("down_t", [P, KT, NR])
        up_t = keep("up_t", [ER, D])

        tally = top.enter_context(nc.semaphore("tally"))

        prepare(nc, locals())
        project(nc, locals())
        attend(nc, locals())
        finish(nc, locals())


def prepare(nc, s):
    tally = s["tally"]
    (NB, D, KT, NR, ER, E, R, ident, bias_col, mod1_col, mod2_col, down_t, up_t, mod_rows, w_split) = (
        s[n] for n in "NB D KT NR ER E R ident bias_col mod1_col mod2_col down_t up_t mod_rows w_split".split())
    ROUNDS = 6 * D // (4 * BANK)
    RC = 4 * BANK
    CB = NB * KT
    MR = 2 * KT * NB
    weights = (s["Wq"], s["Wk"], s["Wv"], s["Wo"])
    with ExitStack() as ctx:
        def sb(name, shape, dt=F32):
            return ctx.enter_context(nc.sbuf_tensor(name, shape, dt))

        def sem(name):
            return ctx.enter_context(nc.semaphore(name))

        c_in = sb("c_in", [CB, P])
        bias_in = sb("bias_in", [3 * KT, P])
        down_in = sb("down_in", [NR, D])
        up_in = sb("up_in", [P, KT, ER])
        mod1_in = sb("mod1_in", [MR, P])
        mod2_in = sb("mod2_in", [MR, P])
        silu_e = sb("silu_e", [P, CB])
        silu_r = sb("silu_r", [P, CB])
        silu_c = sb("silu_c", [P, KT, NB])
        wm = sb("wm", [P, 2, KT, RC])
        rows = sb("rows", [P, ROUNDS, BANK])
        sign = sb("sign", [P, BANK])
        mag = sb("mag", [P, BANK])
        w_in = sb("w_in", [P, 2, D])
        w_hi = sb("w_hi", [P, 2, D], F32R)
        w_lo = sb("w_lo", [P, 2, D], F32R)
        ps_small = ctx.enter_context(nc.psum_tensor("ps_small", [P, BANK], F32))
        ps_mod = ctx.enter_context(nc.psum_tensor("ps_mod", [P, ROUNDS, BANK], F32))
        ps_w = ctx.enter_context(nc.psum_tensor("ps_w", [P, 2, D], F32))

        ident_ready = sem("ident_ready")
        small_loaded, mod_loaded = sem("small_loaded"), sem("mod_loaded")
        small_done, small_copied = sem("small_done"), sem("small_copied")
        silu_exp, silu_ready, dve_chain = sem("silu_exp"), sem("silu_ready"), sem("dve_chain")
        wm_loaded = [sem(f"wm_loaded{i}") for i in range(2)]
        mod_done, rows_ready, rows_stored = sem("mod_done"), sem("rows_ready"), sem("rows_stored")
        w_loaded = [sem(f"w_loaded{i}") for i in range(2)]
        w_turned, w_hi_done, w_lo_done = sem("w_turned"), sem("w_hi_done"), sem("w_lo_done")
        w_stored = [sem(f"w_stored{i}") for i in range(2)]
        block = ctx.enter_context(nc.Block())

        wm_view = s["wmod"].rearrange("(k p) n -> p k n", p=P)

        @block.sync
        def _(sp):
            sp.dma_start(c_in[:], s["c"].rearrange("b (k p) -> (b k) p", p=P)).then_inc(small_loaded, 16)
            for i, b in enumerate((s["bq"], s["bk"], s["bv"])):
                sp.dma_start(bias_in[i * KT:(i + 1) * KT, :], b.rearrange("(g p) -> g p", p=P)).then_inc(small_loaded, 16)
            sp.dma_start(down_in[0:ER, :], s["lora_a"].rearrange("e r d -> (e r) d")).then_inc(small_loaded, 16)
            sp.dma_start(down_in[ER:NR, :], s["router_w"]).then_inc(small_loaded, 16)
            lb = s["lora_b"].rearrange("e (t p) r -> e p t r", p=P)
            for e in range(E):
                sp.dma_start(up_in[:, :, e * R:(e + 1) * R], lb[e]).then_inc(small_loaded, 16)
            for r in range(ROUNDS):
                if r >= 2:
                    sp.wait_ge(mod_done, r - 1)
                sp.dma_start(wm[:, r % 2], wm_view[:, :, r * RC:(r + 1) * RC]).then_inc(wm_loaded[r % 2], 16)
            for m in range(4):
                with sp.Fori(0, KT // 2) as tt:
                    for i in range(2):
                        n = m * KT + tt * 2 + i
                        sp.wait_ge(w_turned, n + 1)
                        sp.dma_start(w_in[:, i], weights[m].rearrange("(t p) n -> t p n", p=P)[tt * 2 + i]).then_inc(w_loaded[i], 16)

        @block.gpsimd
        def _(pool):
            nc.gpsimd.memset(ident[:], 0.0).then_inc(ident_ready, 1)
            pool.wait_ge(ident_ready, 1)
            nc.gpsimd.affine_select(out=ident[:], in_=ident[:], compare_op=ALU.not_equal, fill=1.0, base=0,
                                    pattern=[[-1, P]], channel_multiplier=1).then_inc(ident_ready, 1)
            for r in range(ROUNDS):
                pool.wait_ge(rows_ready, r + 1)
                for j in range(4):
                    col = r * RC + j * BANK
                    pool.dma_start(mod_rows[:, col:col + BANK], rows[32 * j:32 * j + NB, r]).then_inc(rows_stored, 16)
            pool.wait_ge(rows_stored, 16 * 4 * ROUNDS)
            for b in range(NB):
                for v, dst in ((0, mod1_in), (3, mod2_in)):
                    src = mod_rows[b, v * D:(v + 2) * D].rearrange("(r p) -> r p", p=P)
                    pool.dma_start(dst[b * 2 * KT:(b + 1) * 2 * KT, :], src).then_inc(mod_loaded, 16)

        @block.tensor
        def _(pe):
            pe.sem_inc(w_turned, 2)
            pe.wait_ge(ident_ready, 2)
            pe.wait_ge(small_loaded, 16 * (6 + E))
            nc.tensor.transpose(ps_small[:, 0:CB], c_in[:], ident[0:CB, 0:CB])
            nc.tensor.transpose(ps_small[:, P:P + 3 * KT], bias_in[:], ident[0:3 * KT, 0:3 * KT]).then_inc(small_done, 1)
            pe.wait_ge(silu_ready, 1)
            for r in range(ROUNDS):
                pe.wait_ge(wm_loaded[r % 2], 16 * (r // 2 + 1))
                for k in range(KT):
                    for j in range(4):
                        last = nc.tensor.matmul(ps_mod[32 * j:32 * j + NB, r], silu_c[:, k], wm[:, r % 2, k, j * BANK:(j + 1) * BANK],
                                                start=k == 0, stop=k == KT - 1)
                last.then_inc(mod_done, 1)
            for k in range(KT):
                pe.wait_ge(small_copied, k + 1)
                nc.tensor.transpose(ps_small[:, 0:NR], down_in[:, k * P:(k + 1) * P], ident[0:NR, 0:NR])
                nc.tensor.transpose(ps_small[0:ER, P:2 * P], up_in[:, k], ident[:]).then_inc(small_done, 1)
            for m in range(4):
                with pe.Fori(0, KT // 2) as tt:
                    for i in range(2):
                        n = m * KT + tt * 2 + i
                        pe.wait_ge(w_loaded[i], 16 * (m * (KT // 2) + tt + 1))
                        pe.wait_ge(w_lo_done, n + 1)
                        for k in range(KT):
                            last = nc.tensor.transpose(ps_w[:, i, k * P:(k + 1) * P], w_in[:, i, k * P:(k + 1) * P], ident[:])
                        last.then_inc(w_turned, 1)
            pe.wait_ge(mod_loaded, 16 * 2 * NB)
            pe.wait_ge(small_copied, KT + 1)
            nc.tensor.transpose(ps_small[:, 0:MR], mod1_in[:], ident[0:MR, 0:MR])
            nc.tensor.transpose(ps_small[:, P:P + MR], mod2_in[:], ident[0:MR, 0:MR]).then_inc(small_done, 1)

        @block.scalar
        def _(act):
            act.wait_ge(small_done, 1)
            nc.scalar.activation(silu_e[:], ps_small[:, 0:CB], ACT.Exp, scale=-1.0).then_inc(silu_exp, 1)
            for m in range(4):
                with act.Fori(0, KT // 2) as tt:
                    for i in range(2):
                        n = m * KT + tt * 2 + i
                        act.wait_ge(w_turned, n + 3)
                        act.wait_ge(w_stored[i], 32 * (m * (KT // 2) + tt + 1))
                        nc.scalar.activation(w_hi[:, i], ps_w[:, i], ACT.Copy).then_inc(w_hi_done, 1)
                        act.wait_ge(w_hi_done, n + 1)
                        act.dma_start(w_split[m, tt * 2 + i, 0], w_hi[:, i].bitcast(F32)).then_inc(w_stored[i], 16)
                        act.wait_ge(w_lo_done, n + 3)
                        act.dma_start(w_split[m, tt * 2 + i, 1], w_lo[:, i].bitcast(F32)).then_inc(w_stored[i], 16)
            for i in range(2):
                act.wait_ge(w_stored[i], 32 + 32 * 2 * KT)

        @block.vector
        def _(dve):
            dve.sem_inc(w_lo_done, 2)
            for i in range(2):
                dve.sem_inc(w_stored[i], 32)
            chain = Chain(dve, dve_chain, tally)
            dve.wait_ge(silu_exp, 1)
            chain.link(nc.vector.tensor_scalar_add(silu_e[:], silu_e[:], 1.0))
            chain.link(nc.vector.reciprocal(silu_r[:], silu_e[:]))
            nc.vector.tensor_tensor(silu_c[:].rearrange("p k b -> p b k"), ps_small[:, 0:CB].rearrange("p (b k) -> p b k", b=NB),
                                    silu_r[:].rearrange("p (b k) -> p b k", b=NB), ALU.mult).then_inc(silu_ready, 1)
            chain.link(nc.vector.tensor_copy(bias_col[:], ps_small[:, P:P + 3 * KT]))
            dve.sem_inc(small_copied, 1)
            for r in range(ROUNDS):
                dve.wait_ge(mod_done, r + 1)
                for j in range(4):
                    part = slice(32 * j, 32 * j + NB)
                    if (r * 4 + j) * BANK // D in (2, 5):
                        chain.link(nc.vector.tensor_scalar(sign[part], ps_mod[part, r], 0.0, 2.0, ALU.is_ge, ALU.mult))
                        chain.link(nc.vector.tensor_scalar(mag[part], ps_mod[part, r], -1.0, None, ALU.mult))
                        chain.link(nc.vector.tensor_tensor(mag[part], ps_mod[part, r], mag[part], ALU.max))
                        chain.link(nc.vector.tensor_scalar(mag[part], mag[part], 0.25, None, ALU.max))
                        chain.link(nc.vector.scalar_tensor_tensor(rows[part, r], sign[part], -1.0, mag[part], ALU.add, ALU.mult))
                    else:
                        chain.link(nc.vector.tensor_copy(rows[part, r], ps_mod[part, r]))
                dve.sem_inc(rows_ready, 1)
            for k in range(KT):
                dve.wait_ge(small_done, k + 2)
                chain.link(nc.vector.tensor_copy(down_t[:, k], ps_small[:, 0:NR]))
                nc.vector.tensor_copy(up_t[:, k * P:(k + 1) * P], ps_small[0:ER, P:2 * P]).then_inc(small_copied, 1)
            for m in range(4):
                with dve.Fori(0, KT // 2) as tt:
                    for i in range(2):
                        n = m * KT + tt * 2 + i
                        dve.wait_ge(w_hi_done, n + 1)
                        nc.vector.tensor_tensor(w_lo[:, i], ps_w[:, i], w_hi[:, i].bitcast(F32), ALU.subtract).then_inc(w_lo_done, 1)
            dve.wait_ge(small_done, KT + 2)
            for base, dst in ((0, mod1_col), (P, mod2_col)):
                src = ps_small[:, base:base + MR].rearrange("p (b v k) -> p b v k", b=NB, v=2)
                col = dst[:].rearrange("p (b v k) -> p b v k", b=NB, v=2)
                chain.link(nc.vector.tensor_copy(col[:, :, 0], src[:, :, 0]))
                chain.link(nc.vector.tensor_scalar_add(col[:, :, 1], src[:, :, 1], 1.0))


def project(nc, s):
    tally = s["tally"]
    (x, NB, L, D, KT, TT, QC, NG, ident, bias_col, mod1_col, w_split, qk_split, v_tok) = (
        s[n] for n in "x NB L D KT TT QC NG ident bias_col mod1_col w_split qk_split v_tok".split())
    NH = KT * QC
    UNITS = 3 * QC
    ORDER = (2, 0, 1)
    with ExitStack() as ctx:
        def sb(name, shape, dt=F32):
            return ctx.enter_context(nc.sbuf_tensor(name, shape, dt))

        def sem(name):
            return ctx.enter_context(nc.semaphore(name))

        xn = sb("xn", [P, TT, D])
        stats = sb("stats", [P, 2, 6])
        mean_var = sb("mean_var", [P, 2])
        rstd = sb("rstd", [P, 1])
        minus_half = sb("minus_half", [P, 1])
        h_full = sb("h_full", [P, 3, BANK])
        h_hi = sb("h_hi", [P, KT, L], F32R)
        h_lo = sb("h_lo", [P, KT, L], F32R)
        w_hi = sb("w_hi2", [P, 3, KT, P], F32R)
        w_lo = sb("w_lo2", [P, 3, KT, P], F32R)
        qk_hi = sb("qk_hi", [P, 2, L], F32R)
        qk_lo = sb("qk_lo", [P, 2, L], F32R)
        v_feat = sb("v_feat", [P, QC, BANK])
        v_out = sb("v_out", [P, TT, P])
        ps_h = [ctx.enter_context(nc.psum_tensor(f"ps_h{i}", [P, BANK], F32)) for i in range(2)]
        ps_u = [ctx.enter_context(nc.psum_tensor(f"ps_u{i}", [P, BANK], F32)) for i in range(2)]
        ps_v = [ctx.enter_context(nc.psum_tensor(f"ps_v{i}", [P, BANK], F32)) for i in range(QC)]

        x_loaded = [sem(f"x_loaded{i}") for i in range(QC)]
        var_ready, rstd_ready, dve_chain = sem("var_ready"), sem("rstd_ready"), sem("dve_chain2")
        xn_ready = sem("xn_ready")
        h_turned, h_full_done, h_hi_done, h_lo_done = sem("h_turned"), sem("h_full_done"), sem("h_hi_done"), sem("h_lo_done")
        w_loaded = [sem(f"w_loaded_{n}") for n in "vqk"]
        unit_done, unit_free, hi_done = sem("unit_done"), sem("unit_free"), sem("hi_done")
        v_turned, v_copied = sem("v_turned"), sem("v_copied")
        v_stored, q_stored, k_stored = sem("v_stored"), sem("q_stored"), sem("k_stored")
        half_set = sem("half_set")
        block = ctx.enter_context(nc.Block())

        def load_weights(sp, m, g):
            w = ORDER[m]
            sp.dma_start(w_hi[:, m].bitcast(F32), w_split[w, g, 0].rearrange("p (k n) -> p k n", k=KT)).then_inc(w_loaded[m], 16)
            sp.dma_start(w_lo[:, m].bitcast(F32), w_split[w, g, 1].rearrange("p (k n) -> p k n", k=KT)).then_inc(w_loaded[m], 16)

        def load_x(sp, b):
            for i in range(QC):
                half = TT // QC
                sp.dma_start(xn[:, i * half:(i + 1) * half], x[b, i * BANK:(i + 1) * BANK, :].rearrange("(t p) d -> p t d", p=P)).then_inc(x_loaded[i], 16)

        @block.sync
        def _(sp):
            load_x(sp, 0)
            for m in range(3):
                load_weights(sp, m, 0)

            def batch(b, more):
                if more:
                    wait_apart(sp, h_turned, NH * (b + 1), tally)
                    load_x(sp, b + 1)
                with sp.Fori(0, KT) as g:
                    n = b * KT + g
                    after = (g + 1) % KT
                    wait_apart(sp, unit_done, UNITS * n + 2, tally)
                    load_weights(sp, 0, after)
                    wait_apart(sp, unit_done, UNITS * n + 4, tally)
                    load_weights(sp, 1, after)
                    wait_apart(sp, v_copied, QC * (n + 2), tally)
                    sp.dma_start(v_tok[n], v_out[:]).then_inc(v_stored, 16)
                    sp.wait_ge(unit_free, UNITS * n + 4 + 2)
                    sp.dma_start(qk_split[n, 0], qk_hi[:, 0].bitcast(F32)).then_inc(q_stored, 16)
                    sp.dma_start(qk_split[n, 1], qk_lo[:, 0].bitcast(F32)).then_inc(q_stored, 16)
                    wait_apart(sp, unit_done, UNITS * n + 6, tally)
                    load_weights(sp, 2, after)
                    sp.wait_ge(unit_free, UNITS * n + 6 + 2)
                    sp.dma_start(qk_split[n, 2], qk_hi[:, 1].bitcast(F32)).then_inc(k_stored, 16)
                    sp.dma_start(qk_split[n, 3], qk_lo[:, 1].bitcast(F32)).then_inc(k_stored, 16)

            with sp.Fori(0, NB - 1) as b:
                batch(b, True)
            batch(NB - 1, False)
            sp.wait_ge(v_stored, 16 * (NG + 1))
            sp.wait_ge(q_stored, 32 * (NG + 1))
            sp.wait_ge(k_stored, 32 * (NG + 1))
            for m in range(3):
                sp.wait_ge(w_loaded[m], 32 * (NG + 1))

        @block.gpsimd
        def _(pool):
            nc.gpsimd.memset(minus_half[:], -0.5).then_inc(half_set, 1)
            pool.wait_ge(half_set, 1)

            def rsqrt(tile):
                pool.wait_ge(var_ready, tile + 1)
                nc.gpsimd.tensor_tensor(rstd[:], mean_var[:, 1:2], minus_half[:], ALU.pow).then_inc(rstd_ready, 1)

            def batch(b, more):
                for i in range(NH):
                    half, k = divmod(i, KT)
                    pool.wait_ge(h_hi_done, NH * b + i + 1)
                    cols = slice(half * BANK, (half + 1) * BANK)
                    nc.gpsimd.tensor_tensor(h_lo[:, k, cols], h_full[:, i % 3], h_hi[:, k, cols].bitcast(F32), ALU.subtract).then_inc(h_lo_done, 1)
                if more:
                    with pool.Fori(0, TT) as t:
                        rsqrt((b + 1) * TT + t)

            with pool.Fori(0, TT) as t:
                rsqrt(t)
            with pool.Fori(0, NB - 1) as b:
                batch(b, True)
            batch(NB - 1, False)

        @block.scalar
        def _(act):
            for st, n in ((v_stored, 16), (q_stored, 32), (k_stored, 32)):
                act.sem_inc(st, n)
            act.sem_inc(v_copied, QC)

            def split_hi(n, g, u):
                m, ch = divmod(u, QC)
                if ch == 0:
                    act.wait_ge((q_stored, k_stored)[m - 1], 32 * (n + 1))
                wait_apart(act, unit_done, UNITS * n + u + 1, tally)
                bias = bias_col[:, bass.ds(ORDER[m] * KT + g, 1)]
                nc.scalar.activation(qk_hi[:, m - 1, ch * BANK:(ch + 1) * BANK], ps_u[u % 2][:], ACT.Identity, bias=bias, scale=1.0).then_inc(hi_done, 1)

            def copy_v(n, ch):
                act.wait_ge(v_turned, QC * n + ch + 1)
                if ch == 0:
                    act.wait_ge(v_stored, 16 * (n + 1))
                half = TT // QC
                nc.scalar.activation(v_out[:, ch * half:(ch + 1) * half], ps_v[ch][:].rearrange("p (t n) -> p t n", n=P), ACT.Copy).then_inc(v_copied, 1)

            with act.Fori(0, NB) as b:
                for i in range(NH):
                    half, k = divmod(i, KT)
                    act.wait_ge(h_full_done, NH * b + i + 1 + 2)
                    nc.scalar.activation(h_hi[:, k, half * BANK:(half + 1) * BANK], h_full[:, i % 3], ACT.Copy).then_inc(h_hi_done, 1)
                with act.Fori(0, KT) as g:
                    n = b * KT + g
                    split_hi(n, g, 2)
                    copy_v(n, 0)
                    copy_v(n, 1)
                    split_hi(n, g, 3)
                    split_hi(n, g, 4)
                    split_hi(n, g, 5)

        @block.vector
        def _(dve):
            dve.sem_inc(unit_free, 2)
            dve.sem_inc(h_full_done, 2)
            dve.sem_inc(h_lo_done, 3)

            def layernorm(tile, t):
                chain = Chain(dve, dve_chain, tally, tile * 3)
                src = xn[:, t]
                for i in range(2):
                    last = nc.vector.bn_stats(stats[:, i], src[:, i * (D // 2):(i + 1) * (D // 2)])
                    chain.link(last)
                chain.link(nc.vector.bn_aggr(mean_var[:], stats[:].rearrange("p a b -> p (a b)")))
                nc.vector.tensor_scalar_add(mean_var[:, 1:2], mean_var[:, 1:2], EPS).then_inc(var_ready, 1)
                dve.wait_ge(rstd_ready, tile + 1)
                nc.vector.tensor_scalar(src, src, mean_var[:, 0:1], rstd[:], ALU.subtract, ALU.mult).then_inc(xn_ready, 1)

            def batch(b, more):
                cols = mod1_col[:].rearrange("p (b v k) -> p b v k", b=NB, v=2)
                for i in range(NH):
                    half, k = divmod(i, KT)
                    dve.wait_ge(h_turned, NH * b + i + 1)
                    dve.wait_ge(h_lo_done, NH * b + i + 1)
                    nc.vector.tensor_scalar(h_full[:, i % 3], ps_h[i % 2][:], cols[:, b, 1, k:k + 1], cols[:, b, 0, k:k + 1],
                                            ALU.mult, ALU.add).then_inc(h_full_done, 1)
                with dve.Fori(0, KT) as g:
                    n = b * KT + g
                    for u in range(UNITS):
                        m, ch = divmod(u, QC)
                        bias = bias_col[:, bass.ds(ORDER[m] * KT + g, 1)]
                        if m == 0:
                            dve.wait_ge(unit_done, UNITS * n + u + 1)
                            dve.wait_ge(v_copied, QC * n + ch + 1)
                            nc.vector.tensor_scalar(v_feat[:, ch], ps_u[u % 2][:], bias, None, ALU.add).then_inc(unit_free, 1)
                        else:
                            dve.wait_ge(hi_done, (UNITS - QC) * n + u - QC + 1)
                            part = slice(ch * BANK, (ch + 1) * BANK)
                            nc.vector.scalar_tensor_tensor(qk_lo[:, m - 1, part], ps_u[u % 2][:], bias, qk_hi[:, m - 1, part].bitcast(F32),
                                                           ALU.add, ALU.subtract).then_inc(unit_free, 1)
                    if more:
                        for i in range(QC):
                            dve.wait_ge(x_loaded[i], 16 * (b + 2))
                        layernorm((b + 1) * TT + g, g)

            for i in range(QC):
                dve.wait_ge(x_loaded[i], 16)
                half = TT // QC
                with dve.Fori(i * half, (i + 1) * half) as t:
                    layernorm(t, t)
            with dve.Fori(0, NB - 1) as b:
                batch(b, True)
            batch(NB - 1, False)

        @block.tensor
        def _(pe):
            with pe.Fori(0, NB) as b:
                for i in range(NH):
                    half, k = divmod(i, KT)
                    if k == 0:
                        pe.wait_ge(xn_ready, TT * b + (half + 1) * (TT // QC))
                    pe.wait_ge(h_full_done, NH * b + i + 1)
                    for t in range(BANK // P):
                        last = nc.tensor.transpose(ps_h[i % 2][:, t * P:(t + 1) * P], xn[:, half * (BANK // P) + t, k * P:(k + 1) * P], ident[:])
                    last.then_inc(h_turned, 1)
                pe.wait_ge(h_hi_done, NH * (b + 1))
                wait_apart(pe, h_lo_done, NH * (b + 1) + 3, tally)
                with pe.Fori(0, KT) as g:
                    n = b * KT + g

                    def unit(u):
                        m, ch = divmod(u, QC)
                        if ch == 0:
                            pe.wait_ge(w_loaded[m], 32 * (n + 1))
                        pe.wait_ge(unit_free, UNITS * n + u + 1)
                        tok = slice(ch * BANK, (ch + 1) * BANK)
                        for k in range(KT):
                            for j, (w, h) in enumerate(((w_hi, h_hi), (w_lo, h_hi), (w_hi, h_lo))):
                                last = nc.tensor.matmul(ps_u[u % 2][:], w[:, m, k], h[:, k, tok], start=k == 0 and j == 0, stop=k == KT - 1 and j == 2)
                        last.then_inc(unit_done, 1)

                    def turn_v(ch):
                        pe.wait_ge(unit_free, UNITS * n + ch + 1 + 2)
                        pe.wait_ge(v_copied, QC * n + ch + 1)
                        for t in range(BANK // P):
                            last = nc.tensor.transpose(ps_v[ch][:, t * P:(t + 1) * P], v_feat[:, ch, t * P:(t + 1) * P], ident[:])
                        last.then_inc(v_turned, 1)

                    unit(0)
                    unit(1)
                    unit(2)
                    turn_v(0)
                    turn_v(1)
                    for u in range(3, UNITS):
                        unit(u)


def attend(nc, s):
    tally = s["tally"]
    (L, KT, TT, HD, HG, QC, NG, SCALE, QK_ROWS, SHIFT_ROW, ident, qk_split, v_tok, att_raw, att_sum) = (
        s[n] for n in "L KT TT HD HG QC NG SCALE QK_ROWS SHIFT_ROW ident qk_split v_tok att_raw att_sum".split())
    SLOTS = 4
    CT = BANK // P
    steps = [(ch, j) for ch in reversed(range(QC)) for j in range((ch + 1) * CT)]
    NSTEP = len(steps)
    diagonal = [k for k, (ch, j) in enumerate(steps) if j >= ch * CT]
    PBUF = 3
    rows = [(i, ch, h) for i in range(TT) for ch in range(i // CT + 1) for h in range(HG)]
    NROW = len(rows)
    ROW_USES = NROW + 1
    HALF = NROW // 2
    ends = [k for k, (ch, j) in enumerate(steps) if j == (ch + 1) * CT - 1]
    assert NROW == 4 * NSTEP and NG % SLOTS == 0 and NSTEP % PBUF == 0

    def strewn(i, last):
        one = [(1, u) for u in range(HALF, NROW + 1)] if not (last and i + 1 >= SLOTS) else []
        two = [(2, u) for u in range(HALF)] if not (last and i + 2 >= SLOTS) else []
        return one + two
    with ExitStack() as ctx:
        def sb(name, shape, dt=F32):
            return ctx.enter_context(nc.sbuf_tensor(name, shape, dt))

        def sem(name):
            return ctx.enter_context(nc.semaphore(name))

        q_st = [sb(f"q_st{i}", [SHIFT_ROW + 1, HG, L], F32R) for i in range(SLOTS)]
        k_st = [sb(f"k_st{i}", [SHIFT_ROW + 1, HG, L], F32R) for i in range(SLOTS)]
        v_sb = [sb(f"v_sb{i}", [P, TT, P]) for i in range(SLOTS)]
        prob = sb("prob", [P, PBUF, HG, BANK])
        ones = sb("ones", [P, HD])
        ident_b = sb("ident_b", [P, P], BF16)
        mask_b = sb("mask_b", [P, P], BF16)
        part_max = sb("part_max", [P, HG * TT, QC])
        row_max = sb("row_max", [P, HG * TT])
        shift = sb("shift", [HG * TT, P], F32R)
        att = sb("att", [P, QC, BANK])
        sums = sb("sums", [P, QC, BANK])
        ps_s = [ctx.enter_context(nc.psum_tensor(f"ps_s{i}", [P, 2, BANK], F32)) for i in range(2)]
        ps_r = [ctx.enter_context(nc.psum_tensor(f"ps_r{i}", [P, BANK], F32)) for i in range(2)]
        ps_o = ctx.enter_context(nc.psum_tensor("ps_o", [P, BANK], F32))
        ps_sum = ctx.enter_context(nc.psum_tensor("ps_sum", [P, BANK], F32))

        const_ready, pool_const = sem("const_ready"), sem("pool_const")
        qkv_loaded = [sem(f"qkv_loaded{i}") for i in range(SLOTS)]
        slot_free = sem("slot_free")
        row_done, row_free, max_ready, dve_chain = sem("row_done"), sem("row_free"), sem("max_ready"), sem("dve_chain3")
        shift_loaded = [sem(f"shift_loaded{i}") for i in range(SLOTS)]
        score_done, score_free, masked = sem("score_done"), sem("score_free"), sem("masked")
        prob_free, out_free = sem("prob_free"), sem("out_free")
        att_stored = [sem(f"att_stored{i}") for i in range(QC)]
        block = ctx.enter_context(nc.Block())

        def groups(eng, body):
            with eng.Fori(0, NG // SLOTS - 1) as tb:
                for i in range(SLOTS):
                    body(tb, i, False)
            for i in range(SLOTS):
                body(NG // SLOTS - 1, i, True)

        @block.sync
        def _(sp):
            def load(t, slot):
                for place, part in ((0, 0), (1, 1), (2, 0)):
                    sp.dma_start(q_st[slot][place * HD:(place + 1) * HD].bitcast(F32), qk_split[t, part].rearrange("(h d) n -> d h n", d=HD)).then_inc(qkv_loaded[slot], 16)
                for place, part in ((0, 2), (1, 2), (2, 3)):
                    sp.dma_start(k_st[slot][place * HD:(place + 1) * HD].bitcast(F32), qk_split[t, part].rearrange("(h d) n -> d h n", d=HD)).then_inc(qkv_loaded[slot], 16)
                sp.dma_start(v_sb[slot][:], v_tok[t]).then_inc(qkv_loaded[slot], 16)

            def load_shift(t, slot):
                sp.wait_ge(row_free, ROW_USES * (t + 1) + 2)
                sp.dma_start(q_st[slot][SHIFT_ROW:SHIFT_ROW + 1].bitcast(F32).rearrange("o h n -> o (h n)"),
                             shift[:].bitcast(F32)).then_inc(shift_loaded[slot], 16)

            for t in range(SLOTS - 1):
                load(t, t)
            load_shift(0, 0)

            def group(tb, i, last):
                t = tb * SLOTS + i
                if not (last and i > 0):
                    sp.wait_ge(slot_free, t + 1)
                    load(t + SLOTS - 1, (i + SLOTS - 1) % SLOTS)
                if not (last and i == SLOTS - 1):
                    load_shift(t + 1, (i + 1) % SLOTS)
                b, g = (tb * SLOTS + i) // KT, (tb * SLOTS + i) % KT
                for n, k in enumerate(ends):
                    ch = steps[k][0]
                    cols = slice(ch * BANK, (ch + 1) * BANK)
                    wait_apart(sp, out_free, 2 * (QC * t + n + 1) + 2, tally)
                    sp.dma_start(att_raw[b, g, :, cols], att[:, ch]).then_inc(att_stored[ch], 16)
                    sp.dma_start(att_sum[b, g, :, cols], sums[::HD, ch]).then_inc(att_stored[ch], 16)

            groups(sp, group)
            for ch in range(QC):
                sp.wait_ge(att_stored[ch], 32 * (NG + 1))

        @block.gpsimd
        def _(pool):
            for i in range(SLOTS):
                nc.gpsimd.memset(k_st[i][SHIFT_ROW:SHIFT_ROW + 1].bitcast(F32), 1.0).then_inc(const_ready, 1)
            pool.wait_ge(const_ready, SLOTS)
            nc.gpsimd.memset(ones[:], 1.0).then_inc(const_ready, 1)
            nc.gpsimd.memset(mask_b[:], 0.0).then_inc(pool_const, 1)
            nc.gpsimd.tensor_copy(ident_b[:], ident[:]).then_inc(const_ready, 1)
            pool.wait_ge(pool_const, 1)
            nc.gpsimd.affine_select(out=mask_b[:], in_=mask_b[:], compare_op=ALU.is_ge, fill=MASKED, base=0,
                                    pattern=[[-1, P]], channel_multiplier=1).then_inc(const_ready, 1)

            def group(tb, i, last):
                t = tb * SLOTS + i
                for k, (ch, j) in enumerate(steps):
                    if k in diagonal:
                        wait_apart(pool, score_free, 2 * NSTEP * t + 2 * (k + 1) + 2, tally)
                        off = j * P - ch * BANK
                        block_p = prob[:, k % PBUF, :, off:off + P]
                        nc.gpsimd.affine_select(out=block_p, in_=block_p, compare_op=ALU.is_ge, fill=0.0, base=0,
                                                pattern=[[0, HG], [1, P]], channel_multiplier=-1).then_inc(masked, 1)

            groups(pool, group)

        @block.scalar
        def _(act):
            act.sem_inc(score_free, 2)
            act.sem_inc(out_free, 2)
            for ch in range(QC):
                act.sem_inc(att_stored[ch], 32)

            def copy_out(t, n):
                k = ends[n]
                ch = steps[k][0]
                act.wait_ge(att_stored[ch], 32 * (t + 1))
                act.wait_ge(prob_free, NSTEP * t + k + 1 + PBUF)
                nc.scalar.activation(att[:, ch], ps_o[:], ACT.Copy).then_inc(out_free, 1)
                nc.scalar.activation(sums[:, ch], ps_sum[:], ACT.Copy).then_inc(out_free, 1)

            def group(tb, i, last):
                t = tb * SLOTS + i
                for k, (ch, j) in enumerate(steps):
                    off = max(j * P - ch * BANK, 0)
                    act.wait_ge(prob_free, NSTEP * t + k + 1)
                    for pair in range(2):
                        act.wait_ge(score_done, 2 * NSTEP * t + 2 * k + pair + 1)
                        nc.scalar.activation(prob[:, k % PBUF, 2 * pair:2 * pair + 2, off:], ps_s[pair][:, :, off:], ACT.Exp, scale=SCALE).then_inc(score_free, 1)
                    if k - 1 in ends:
                        copy_out(t, ends.index(k - 1))
                copy_out(t, QC - 1)

            groups(act, group)

        @block.vector
        def _(dve):
            dve.sem_inc(row_free, 2)
            nc.vector.memset(part_max[:], MASKED).then_inc(dve_chain, 1)
            dve.wait_ge(dve_chain, 1)

            def max_row(t, parity, u):
                i, ch, h = rows[u]
                width = min(BANK, (i + 1) * P - ch * BANK)
                dve.wait_ge(row_done, ROW_USES * t + u + 1)
                nc.vector.reduce_max(part_max[:, h * TT + i, ch:ch + 1], ps_r[(parity + u) % 2][:, 0:width], AX.X).then_inc(row_free, 1)

            def max_all(t, parity, before):
                dve.wait_ge(row_free, ROW_USES * t + NROW + 2)
                nc.vector.reduce_max(row_max[:], part_max[:], AX.X).then_inc(max_ready, 1)
                if before is not None:
                    dve.wait_ge(*before)
                dve.wait_ge(row_done, ROW_USES * t + NROW + 1)
                nc.vector.tensor_scalar(shift[:], ps_r[(parity + NROW) % 2][0:HG * TT, 0:P], -1.0, None, ALU.mult).then_inc(row_free, 1)

            for u in range(NROW):
                max_row(0, 0, u)
            max_all(0, 0, None)
            for u in range(HALF):
                max_row(1, 1, u)

            def group(tb, i, last):
                t = tb * SLOTS + i
                for ahead, u in strewn(i, last):
                    if u < NROW:
                        max_row(t + ahead, i + ahead, u)
                    else:
                        max_all(t + 1, i + 1, (shift_loaded[i], 16 * (tb + 1)))

            groups(dve, group)

        @block.tensor
        def _(pe):
            pe.sem_inc(prob_free, PBUF)
            pe.sem_inc(slot_free, 1)
            pe.wait_ge(const_ready, SLOTS + 3)

            def row(t, parity, slot, u):
                i, ch, h = rows[u]
                width = min(BANK, (i + 1) * P - ch * BANK)
                cols = max(width, 2 * P)
                on_diagonal = ch == i // CT
                bank = ps_r[(parity + u) % 2]
                pe.wait_ge(row_free, ROW_USES * t + u + 1)
                last = nc.tensor.matmul(bank[:, 0:cols], q_st[slot][0:QK_ROWS, h, i * P:(i + 1) * P],
                                        k_st[slot][0:QK_ROWS, h, ch * BANK:ch * BANK + cols], start=True, stop=not on_diagonal)
                if on_diagonal:
                    last = nc.tensor.matmul(bank[:, width - P:width], ident_b[:], mask_b[:], start=False, stop=True)
                last.then_inc(row_done, 1)

            def turn_max(t, parity):
                pe.wait_ge(max_ready, t + 1)
                pe.wait_ge(row_free, ROW_USES * t + NROW + 1)
                nc.tensor.transpose(ps_r[(parity + NROW) % 2][0:HG * TT, 0:P], row_max[:], ident[:]).then_inc(row_done, 1)

            def scores(t, slot, k, pair):
                ch, j = steps[k]
                off = max(j * P - ch * BANK, 0)
                off = min(off, BANK - 2 * P)
                pe.wait_ge(score_free, 2 * NSTEP * t + 2 * k + pair + 1)
                for h in range(2):
                    last = nc.tensor.matmul(ps_s[pair][:, h, off:], k_st[slot][:, 2 * pair + h, j * P:(j + 1) * P],
                                            q_st[slot][:, 2 * pair + h, ch * BANK + off:(ch + 1) * BANK], start=True, stop=True)
                last.then_inc(score_done, 1)

            def weigh(t, slot, k):
                ch, j = steps[k]
                off = max(j * P - ch * BANK, 0)
                if j == 0:
                    pe.wait_ge(out_free, 2 * (QC * t + ends.index(k + (ch + 1) * CT - 1)) + 2)
                if k in diagonal:
                    pe.wait_ge(masked, len(diagonal) * t + diagonal.index(k) + 1)
                else:
                    pe.wait_ge(score_free, 2 * NSTEP * t + 2 * (k + 1) + 2)
                for h in range(HG):
                    part = slice(h * HD, (h + 1) * HD)
                    nc.tensor.matmul(ps_o[part, off:], v_sb[slot][:, j, part], prob[:, k % PBUF, h, off:], start=j == 0, stop=k in ends)

            def add_up(k):
                ch, j = steps[k]
                off = max(j * P - ch * BANK, 0)
                for h in range(HG):
                    last = nc.tensor.matmul(ps_sum[h * HD:(h + 1) * HD, off:], ones[:], prob[:, k % PBUF, h, off:], start=j == 0, stop=k in ends)
                last.then_inc(prob_free, 1)

            pe.wait_ge(qkv_loaded[0], 16 * 7)
            for u in range(NROW):
                row(0, 0, 0, u)
            turn_max(0, 0)
            pe.wait_ge(qkv_loaded[1], 16 * 7)
            for u in range(HALF):
                row(1, 1, 1, u)

            def group(tb, i, last):
                t = tb * SLOTS + i
                todo = strewn(i, last)

                def pass_1():
                    if todo:
                        ahead, u = todo.pop(0)
                        if u == NROW:
                            turn_max(t + 1, i + 1)
                        else:
                            slot = (i + ahead) % SLOTS
                            if ahead == 2 and u == 0:
                                pe.wait_ge(qkv_loaded[slot], 16 * 7 * (tb + 1 + (i + 2) // SLOTS))
                            row(t + ahead, i + ahead, slot, u)

                pe.wait_ge(shift_loaded[i], 16 * (tb + 1))
                for k in range(NSTEP):
                    scores(t, i, k, 0)
                    pass_1()
                    if k > 0:
                        weigh(t, i, k - 1)
                    pass_1()
                    scores(t, i, k, 1)
                    pass_1()
                    if k > 0:
                        add_up(k - 1)
                    pass_1()
                while todo:
                    pass_1()
                weigh(t, i, NSTEP - 1)
                add_up(NSTEP - 1)
                pe.wait_ge(prob_free, NSTEP * (t + 1) + PBUF)
                pe.sem_inc(slot_free, 1)

            groups(pe, group)


def finish(nc, s):
    tally = s["tally"]
    (x, out, bo, NB, L, D, KT, E, R, ER, NR, ident, mod2_col, down_t, up_t, mod_rows, w_split, att_raw, att_sum, att_inv, HD, HG) = (
        s[n] for n in "x out bo NB L D KT E R ER NR ident mod2_col down_t up_t mod_rows w_split att_raw att_sum att_inv HD HG".split())
    T = 2
    CW = T * P
    CPB = L // CW
    NC = NB * CPB
    HV = D // BANK
    UN = T * HV
    KP = BANK // CW
    TG = KT // KP
    with ExitStack() as ctx:
        def sb(name, shape, dt=F32):
            return ctx.enter_context(nc.sbuf_tensor(name, shape, dt))

        def sem(name):
            return ctx.enter_context(nc.semaphore(name))

        wo_hi = sb("wo_hi", [P, KT, D], F32R)
        wo_lo = sb("wo_lo", [P, KT, D], F32R)
        at_hi = [sb(f"at_hi{i}", [P, KT, CW], F32R) for i in range(2)]
        at_lo = [sb(f"at_lo{i}", [P, KT, CW], F32R) for i in range(2)]
        res = [sb(f"res{i}", [P, T, D]) for i in range(2)]
        at_raw = sb("at_raw", [P, KT, CW])
        at_inv = sb("at_inv", [P, KT, CW])
        inv = sb("inv", [P, NB * HEADS * L // P])
        gates_bc = sb("gates_bc", [P, 2, 2, D])
        bo_bc = sb("bo_bc", [P, D])
        att_y = sb("att_y", [P, T, D])
        xn = sb("xn4", [P, T, D])
        h2t = sb("h2t", [P, KT, CW])
        delta = sb("delta", [P, T, D])
        stats = sb("stats4", [P, 2, 6])
        mean_var = sb("mean_var4", [P, T, 2])
        rstd = sb("rstd4", [P, T])
        minus_half = sb("minus_half4", [P, 1])
        lower = sb("lower", [P, E, E])
        down = sb("down", [P, T, NR])
        top1 = sb("top1", [P, T])
        above = sb("above", [P, T, E, E])
        equal = sb("equal", [P, T, E, E])
        rank = sb("rank", [P, T, E])
        logit = sb("logit", [P, T, E])
        expo = sb("expo", [P, T, E])
        kept = sb("kept", [P, T, E])
        denom = sb("denom", [P, T])
        gate = sb("gate", [P, T, E])
        mid = sb("mid", [P, T, ER])
        mid_t = sb("mid_t", [ER, CW])
        ps_y = [ctx.enter_context(nc.psum_tensor(f"ps_y{i}", [P, BANK], F32)) for i in range(UN)]
        ps_t = [ctx.enter_context(nc.psum_tensor(f"ps_t{i}", [P, BANK], F32)) for i in range(2)]
        ps_l = ctx.enter_context(nc.psum_tensor("ps_l", [P, BANK], F32))
        ps_d = ctx.enter_context(nc.psum_tensor("ps_d", [P, BANK], F32))

        wo_loaded = [sem(f"wo_loaded{i}") for i in range(HV)]
        bc_loaded, gates_loaded, const_ready = sem("bc_loaded"), sem("gates_loaded"), sem("const_ready4")
        at_loaded, at_divided = sem("at_loaded"), sem("at_divided")
        at_hi_done, at_lo_done = sem("at_hi_done"), sem("at_lo_done")
        sums_loaded, inv_ready, inv_stored = sem("sums_loaded"), sem("inv_ready"), sem("inv_stored")
        res_loaded = [sem(f"res_loaded{i}") for i in range(2)]
        y_done, y_free, gated, x1_ready = sem("y_done"), sem("y_free"), sem("gated"), sem("x1_ready")
        dve_chain, var_ready, rstd_ready, xn_ready = sem("dve_chain4"), sem("var_ready4"), sem("rstd_ready4"), sem("xn_ready4")
        turned, h2_ready, down_done = sem("turned"), sem("h2_ready"), sem("down_done")
        logit_ready, exp_ready, mid_ready = sem("logit_ready"), sem("exp_ready"), sem("mid_ready")
        mid_turned, mid_t_ready = sem("mid_turned"), sem("mid_t_ready")
        d_done, d_free, out_ready, out_stored = sem("d_done"), sem("d_free"), sem("out_ready"), sem("out_stored")
        block = ctx.enter_context(nc.Block())

        def chunks(eng, body):
            with eng.Fori(0, NB - 1) as b:
                for i in range(CPB):
                    body(b, i, False)
            for i in range(CPB):
                body(NB - 1, i, True)

        def tokens(a, b, i):
            return a[b + i // CPB, (i % CPB) * CW:(i % CPB + 1) * CW, :].rearrange("(t p) d -> p t d", p=P)

        @block.sync
        def _(sp):
            def load_at(b, i):
                cols = slice((i % CPB) * CW, (i % CPB + 1) * CW)
                sp.dma_start(at_raw[:], att_raw[b + i // CPB].rearrange("g p n -> p g n")[:, :, cols]).then_inc(at_loaded, 16)
                for h in range(HG):
                    src = att_inv[b + i // CPB, :, h, cols].unsqueeze(0).to_broadcast([HD, KT, CW])
                    sp.dma_start(at_inv[h * HD:(h + 1) * HD], src).then_inc(at_loaded, 16)

            def load_res(b, i):
                sp.dma_start(res[i % 2][:], tokens(x, b, i)).then_inc(res_loaded[i % 2], 16)

            def load_gates(b):
                for n, v in enumerate((2, 5)):
                    sp.dma_start(gates_bc[:, n, b % 2], mod_rows[bass.ds(b, 1), v * D:(v + 1) * D].to_broadcast([P, D])).then_inc(gates_loaded, 16)

            sums_flat = att_sum.rearrange("b g h n -> (b g h n)").rearrange("(p n) -> p n", p=P)
            inv_flat = att_inv.rearrange("b g h n -> (b g h n)").rearrange("(p n) -> p n", p=P)
            sp.dma_start(inv[:], sums_flat).then_inc(sums_loaded, 16)
            for hv in range(HV):
                for w, dst in ((0, wo_hi), (1, wo_lo)):
                    for t in range(hv * KT // HV, (hv + 1) * KT // HV):
                        sp.dma_start(dst[:, :, t * P:(t + 1) * P].bitcast(F32), w_split[3, t, w].rearrange("p (g n) -> p g n", g=KT)).then_inc(wo_loaded[hv], 16)
                if hv == 0:
                    sp.wait_ge(inv_ready, 1)
                    sp.dma_start(inv_flat, inv[:]).then_inc(inv_stored, 16)
                    sp.dma_start(bo_bc[:], bo.rearrange("(o d) -> o d", o=1).to_broadcast([P, D])).then_inc(bc_loaded, 16)
                    load_gates(0)
                    load_res(0, 0)
                    sp.wait_ge(inv_stored, 16)
                    load_at(0, 0)
            sp.wait_ge(gates_loaded, 32)
            load_gates(1)
            load_res(0, 1)
            for i in (1, 2):
                sp.wait_ge(at_lo_done, i)
                load_at(0, i)

            def chunk(b, i, last):
                n = b * CPB + i
                if not (last and i + 3 >= CPB):
                    wait_apart(sp, at_lo_done, n + 3, tally)
                    load_at(b, i + 3)
                wait_apart(sp, out_ready, T * (n + 1), tally)
                sp.dma_start(tokens(out, b, i), delta[:]).then_inc(out_stored, 16)
                if not (last and i + 2 >= CPB):
                    load_res(b, i + 2)
                if i == CPB - 1 and not last:
                    wait_apart(sp, gates_loaded, 32 * (b + 2), tally)
                    load_gates((b + 2) % NB)

            chunks(sp, chunk)
            sp.wait_ge(gates_loaded, 32 * (NB + 1))
            sp.wait_ge(out_stored, 16 * (NC + 1))

        @block.gpsimd
        def _(pool):
            nc.gpsimd.memset(minus_half[:], -0.5).then_inc(const_ready, 1)
            nc.gpsimd.memset(lower[:], 1.0).then_inc(const_ready, 1)
            pool.wait_ge(const_ready, 2)
            nc.gpsimd.affine_select(out=lower[:], in_=lower[:], compare_op=ALU.is_gt, fill=0.0, base=0,
                                    pattern=[[1, E], [-1, E]], channel_multiplier=0).then_inc(const_ready, 1)

            def divide(b, i):
                pool.wait_ge(at_loaded, 16 * (1 + HG) * (b * CPB + i + 1))
                nc.gpsimd.tensor_tensor(at_raw[:], at_raw[:], at_inv[:], ALU.mult).then_inc(at_divided, 1)

            def split_lo(b, i):
                pool.wait_ge(at_hi_done, b * CPB + i + 1)
                nc.gpsimd.tensor_tensor(at_lo[i % 2][:], at_raw[:], at_hi[i % 2][:].bitcast(F32), ALU.subtract).then_inc(at_lo_done, 1)

            def residual(b, i, a):
                n = b * CPB + i
                bb = b + i // CPB
                pool.wait_ge(gates_loaded, 32 * (bb + 1))
                wait_apart(pool, y_free, UN * n + HV * (a + 1) + UN, tally)
                nc.gpsimd.tensor_tensor(att_y[:, a], att_y[:, a], gates_bc[:, 0, bb % 2], ALU.mult).then_inc(gated, 1)
                pool.wait_ge(gated, T * n + a + 1)
                pool.wait_ge(res_loaded[i % 2], 16 * (b * (CPB // 2) + i // 2 + 1))
                nc.gpsimd.tensor_tensor(res[i % 2][:, a], res[i % 2][:, a], att_y[:, a], ALU.add).then_inc(x1_ready, 1)

            def rsqrt(b, i, a):
                pool.wait_ge(var_ready, T * (b * CPB + i) + a + 1)
                nc.gpsimd.tensor_tensor(rstd[:, a:a + 1], mean_var[:, a, 1:2], minus_half[:], ALU.pow).then_inc(rstd_ready, 1)

            for i in range(2):
                divide(0, i)
                split_lo(0, i)
            for a in range(T):
                residual(0, 0, a)
                rsqrt(0, 0, a)

            def chunk(b, i, last):
                n = b * CPB + i
                ahead = not (last and i == CPB - 1)
                split = not (last and i + 2 >= CPB)
                if split:
                    divide(b, i + 2)
                if ahead:
                    residual(b, i + 1, 0)
                    rsqrt(b, i + 1, 0)
                if split:
                    split_lo(b, i + 2)
                if ahead:
                    residual(b, i + 1, 1)
                for a in range(T):
                    pool.wait_ge(d_free, UN * n + HV * (a + 1) + 1)
                    nc.gpsimd.tensor_tensor(delta[:, a], delta[:, a], res[i % 2][:, a], ALU.add).then_inc(out_ready, 1)
                if ahead:
                    rsqrt(b, i + 1, 1)

            chunks(pool, chunk)

        @block.scalar
        def _(act):
            act.sem_inc(h2_ready, 2 * KP)
            cols = mod2_col[:].rearrange("p (b v k) -> p b v k", b=NB, v=2)

            def split_hi(b, i, first=False):
                n = b * CPB + i
                if not first:
                    act.wait_ge(y_done, UN * (n - 1))
                act.wait_ge(at_divided, n + 1)
                nc.scalar.copy(at_hi[i % 2][:], at_raw[:]).then_inc(at_hi_done, 1)

            for i in range(2):
                split_hi(0, i, first=True)

            def chunk(b, i, last):
                n = b * CPB + i
                if not (last and i + 2 >= CPB):
                    split_hi(b, i + 2)
                for q in range(TG):
                    if q == 0:
                        act.wait_ge(down_done, n + 1)
                    wait_apart(act, turned, TG * n + q + 1, tally)
                    for j in range(KP):
                        k = q * KP + j
                        nc.scalar.activation(h2t[:, k], ps_t[q % 2][:, j * CW:(j + 1) * CW], ACT.Identity,
                                             bias=cols[:, b, 0, k:k + 1], scale=cols[:, b, 1, k:k + 1]).then_inc(h2_ready, 1)
                act.wait_ge(logit_ready, n + 1)
                nc.scalar.activation(expo[:], logit[:], ACT.Exp).then_inc(exp_ready, 1)

            chunks(act, chunk)

        @block.vector
        def _(dve):
            dve.sem_inc(y_free, UN)
            dve.sem_inc(d_free, 1)
            dve.sem_inc(mid_t_ready, 1)
            dve.sem_inc(out_stored, 16)

            def add_bo(b, i, u, first=False):
                n = b * CPB + i
                a, hv = divmod(u, HV)
                cols = slice(hv * BANK, (hv + 1) * BANK)
                dve.wait_ge(y_done, UN * n + u + 1)
                if hv == 0 and not first:
                    dve.wait_ge(x1_ready, T * (n - 1) + a + 1)
                nc.vector.tensor_tensor(att_y[:, a, cols], ps_y[u][:], bo_bc[:, cols], ALU.add).then_inc(y_free, 1)

            def layernorm(b, i, a, chain):
                n = b * CPB + i
                r = res[i % 2]
                dve.wait_ge(x1_ready, T * n + a + 1)
                for hv in range(2):
                    chain.link(nc.vector.bn_stats(stats[:, hv], r[:, a, hv * (D // 2):(hv + 1) * (D // 2)]))
                chain.link(nc.vector.bn_aggr(mean_var[:, a], stats[:].rearrange("p a b -> p (a b)")))
                nc.vector.tensor_scalar_add(mean_var[:, a, 1:2], mean_var[:, a, 1:2], EPS).then_inc(var_ready, 1)
                dve.wait_ge(rstd_ready, T * n + a + 1)
                nc.vector.tensor_scalar(xn[:, a], r[:, a], mean_var[:, a, 0:1], rstd[:, a:a + 1], ALU.subtract, ALU.mult).then_inc(xn_ready, 1)

            def gates(n, chain):
                dve.wait_ge(down_done, n + 2)
                chain.link(nc.vector.tensor_copy(down[:], ps_l[:, 0:T * NR].rearrange("p (t r) -> p t r", t=T)))
                lg = down[:, :, ER:NR]
                own = lg.unsqueeze(3).to_broadcast([P, T, E, E])
                other = lg.unsqueeze(2).to_broadcast([P, T, E, E])
                chain.link(nc.vector.reduce_max(top1[:], lg, AX.X))
                nc.vector.tensor_tensor(logit[:], lg, top1[:].unsqueeze(2).to_broadcast([P, T, E]), ALU.subtract).then_inc(logit_ready, 1)
                chain.link(nc.vector.tensor_tensor(above[:], other, own, ALU.is_gt))
                chain.link(nc.vector.tensor_tensor(equal[:], other, own, ALU.is_equal))
                chain.link(nc.vector.tensor_tensor(equal[:], equal[:], lower[:].unsqueeze(1).to_broadcast([P, T, E, E]), ALU.mult))
                chain.link(nc.vector.tensor_tensor(above[:], above[:], equal[:], ALU.add))
                chain.link(nc.vector.reduce_sum(rank[:], above[:], AX.X))
                dve.wait_ge(exp_ready, n + 1)
                chain.link(nc.vector.scalar_tensor_tensor(kept[:], rank[:], 2.0, expo[:], ALU.is_lt, ALU.mult))
                chain.link(nc.vector.reduce_sum(denom[:], kept[:], AX.X))
                chain.link(nc.vector.reciprocal(denom[:], denom[:]))
                chain.link(nc.vector.scalar_tensor_tensor(gate[:], kept[:], LORA_SCALE, denom[:].unsqueeze(2).to_broadcast([P, T, E]), ALU.mult, ALU.mult))
                nc.vector.tensor_tensor(mid[:].rearrange("p t (e r) -> p t e r", e=E), down[:, :, 0:ER].rearrange("p t (e r) -> p t e r", e=E),
                                        gate[:].unsqueeze(3).to_broadcast([P, T, E, R]), ALU.mult).then_inc(mid_ready, 1)

            def experts(b, i):
                n = b * CPB + i
                for u in range(UN):
                    a, hv = divmod(u, HV)
                    cols = slice(hv * BANK, (hv + 1) * BANK)
                    if u == 0:
                        dve.wait_ge(gates_loaded, 32 * (b + 1))
                        dve.wait_ge(out_stored, 16 * (n + 1))
                    wait_apart(dve, d_done, UN * n + u + 1, tally)
                    nc.vector.tensor_tensor(delta[:, a, cols], ps_d[:], gates_bc[:, 1, b % 2, cols], ALU.mult).then_inc(d_free, 1)

            dve.wait_ge(sums_loaded, 16)
            nc.vector.reciprocal(inv[:], inv[:]).then_inc(inv_ready, 1)
            dve.wait_ge(bc_loaded, 16)
            dve.wait_ge(const_ready, 3)
            chain = Chain(dve, dve_chain, tally)
            for u in range(UN):
                add_bo(0, 0, u, first=True)
            for a in range(T):
                layernorm(0, 0, a, chain)
            PRO = 3 * T

            def chunk(b, i, last):
                n = b * CPB + i
                ahead = not (last and i == CPB - 1)
                chain = Chain(dve, dve_chain, tally, n * (PRO + 11) + PRO)
                if ahead:
                    add_bo(b, i + 1, 0)
                    add_bo(b, i + 1, 1)
                gates(n, chain)
                dve.wait_ge(mid_turned, n + 1)
                nc.vector.tensor_copy(mid_t[:], ps_l[0:ER, CW:CW + CW]).then_inc(mid_t_ready, 1)
                if ahead:
                    add_bo(b, i + 1, 2)
                    layernorm(b, i + 1, 0, chain)
                    add_bo(b, i + 1, 3)
                experts(b, i)
                if ahead:
                    layernorm(b, i + 1, 1, chain)

            chunks(dve, chunk)

        @block.tensor
        def _(pe):
            pe.sem_inc(down_done, 1)

            def project(b, i, u, first=False):
                n = b * CPB + i
                a, hv = divmod(u, HV)
                if u == 0:
                    pe.wait_ge(at_lo_done, n + 1)
                if first and a == 0:
                    pe.wait_ge(wo_loaded[hv], 16 * 2 * KT // HV)
                pe.wait_ge(y_free, UN * n + u + 1)
                tok, cols = slice(a * P, (a + 1) * P), slice(hv * BANK, (hv + 1) * BANK)
                for g in range(KT):
                    for j, (h, w) in enumerate(((at_hi, wo_hi), (at_lo, wo_hi), (at_hi, wo_lo))):
                        last = nc.tensor.matmul(ps_y[u][:], h[i % 2][:, g, tok], w[:, g, cols], start=g == 0 and j == 0, stop=g == KT - 1 and j == 2)
                last.then_inc(y_done, 1)

            def turn(n):
                pe.wait_ge(xn_ready, T * (n + 1))
                for q in range(TG):
                    pe.wait_ge(h2_ready, KT * n + (q + 1) * KP)
                    for j in range(KP):
                        for a in range(T):
                            k = q * KP + j
                            last = nc.tensor.transpose(ps_t[q % 2][:, j * CW + a * P:j * CW + (a + 1) * P], xn[:, a, k * P:(k + 1) * P], ident[:])
                    last.then_inc(turned, 1)

            def go_down(n):
                pe.wait_ge(h2_ready, KT * (n + 1) + 2 * KP)
                pe.wait_ge(mid_t_ready, n + 1)
                for a in range(T):
                    for k in range(KT):
                        last = nc.tensor.matmul(ps_l[:, a * NR:(a + 1) * NR], h2t[:, k, a * P:(a + 1) * P], down_t[:, k], start=k == 0, stop=k == KT - 1)
                last.then_inc(down_done, 1)

            def turn_mid(n):
                wait_apart(pe, mid_ready, n + 1, tally)
                for a in range(T):
                    last = nc.tensor.transpose(ps_l[0:ER, CW + a * P:CW + (a + 1) * P], mid[:, a], ident[:])
                last.then_inc(mid_turned, 1)

            def go_up(n):
                pe.wait_ge(mid_t_ready, n + 2)
                for u in range(UN):
                    a, hv = divmod(u, HV)
                    pe.wait_ge(d_free, UN * n + u + 1)
                    nc.tensor.matmul(ps_d[:], mid_t[:, a * P:(a + 1) * P], up_t[:, hv * BANK:(hv + 1) * BANK], start=True, stop=True).then_inc(d_done, 1)

            for u in range(UN):
                project(0, 0, u, first=True)

            def chunk(b, i, last):
                n = b * CPB + i
                ahead = not (last and i == CPB - 1)
                for u, other in enumerate((turn, go_down, turn_mid, go_up)):
                    if ahead:
                        project(b, i + 1, u)
                    other(n)

            chunks(pe, chunk)


_INS = ["L0_attn_x", "L0_attn_Wq", "L0_attn_bq", "L0_attn_Wk", "L0_attn_bk", "L0_attn_Wv", "L0_attn_bv", "L0_attn_Wo",
        "L0_attn_bo", "L0_ffn_router_w", "L0_ffn_A", "L0_ffn_B", "L0_c", "L0_wmod"]


def kernel(**inputs):
    import concourse.bacc as _bacc
    from concourse.bass_utils import run_bass_kernel_spmd as _run

    nc = _bacc.Bacc("TRN2", target_bir_lowering=False, num_devices=1)
    arrays, args = {}, []
    for name in _INS:
        a = np.ascontiguousarray(inputs[name])
        arrays[f"in_{name}"] = a
        args.append(nc.dram_tensor(f"in_{name}", a.shape, mybir.dt.from_np(a.dtype), kind="ExternalInput").ap())
    out = nc.dram_tensor("out_x", arrays["in_L0_attn_x"].shape, F32, kind="ExternalOutput").ap()
    adaln_block(nc, *args, out)
    r = _run(nc, [arrays], core_ids=[0])
    return r.results[0]["out_x"]
```

```python
from contextlib import ExitStack

import numpy as np

import concourse.bass as bass
from concourse import mybir

F32 = mybir.dt.float32
F32R = mybir.dt.float32r
BF16 = mybir.dt.bfloat16
ALU = mybir.AluOpType
ACT = mybir.ActivationFunctionType
AX = mybir.AxisListType

P = 128
BANK = 512
HEADS = 32
EPS = 1e-5
LORA_SCALE = 4.0
MASKED = -3.0e38


def wait_apart(eng, sem, value, tally):
    eng.wait_ge(sem, value)
    eng.sem_inc(tally, 1)


class Chain:

    def __init__(self, eng, sem, tally, base=0):
        self.eng, self.sem, self.tally, self.value = eng, sem, tally, base

    def link(self, ins):
        ins.then_inc(self.sem, 1)
        self.value = self.value + 1
        wait_apart(self.eng, self.sem, self.value, self.tally)


def adaln_block(nc, x, Wq, bq, Wk, bk, Wv, bv, Wo, bo, router_w, lora_a, lora_b, c, wmod, out):
    NB, L, D = x.shape
    KT = D // P
    TT = L // P
    HD = D // HEADS
    HG = P // HD
    E, R, _ = lora_a.shape
    ER = E * R
    NR = ER + E
    QC = L // BANK
    NG = NB * KT
    SCALE = float(HD) ** -0.5
    QK_ROWS = 3 * HD
    SHIFT_ROW = QK_ROWS
    assert HD == 32 and L == 1024 and D == 1024

    gate_rows = nc.dram_tensor("gate_rows", [NB, 2, D], F32).ap()
    mod_rows = nc.dram_tensor("mod_rows", [NB, 6 * D], F32).ap()
    w_cols = nc.dram_tensor("w_cols", [3, KT, P, D], F32).ap()
    qk_split = nc.dram_tensor("qk_split", [NG, 4, P, L], F32).ap()
    v_tok = nc.dram_tensor("v_tok", [NG, P, TT, P], F32).ap()
    att_raw = nc.dram_tensor("att_raw", [NB, KT, P, L], F32).ap()
    att_sum = nc.dram_tensor("att_sum", [NB, KT, HG, L], F32).ap()
    att_inv = nc.dram_tensor("att_inv", [NB, KT, HG, L], F32).ap()

    with ExitStack() as top:
        def keep(name, shape, dt=F32):
            return top.enter_context(nc.sbuf_tensor(name, shape, dt))

        ident = keep("ident", [P, P])
        bias_col = keep("bias_col", [P, 3 * KT])
        mod1_col = keep("mod1_col", [P, NB * 2 * KT])
        silu_c = keep("silu_c", [P, KT, NB])
        down_t = keep("down_t", [P, KT, NR])
        up_t = keep("up_t", [ER, D])

        tally = top.enter_context(nc.semaphore("tally"))

        with ExitStack() as early:
            xn = early.enter_context(nc.sbuf_tensor("xn", [P, TT, D], F32))
            x_loaded = [early.enter_context(nc.semaphore(f"x_loaded{i}")) for i in range(QC)]

            def load_x(sp, b):
                half = TT // QC
                for i in range(QC):
                    sp.dma_start(xn[:, i * half:(i + 1) * half], x[b, i * BANK:(i + 1) * BANK, :].rearrange("(t p) d -> p t d", p=P)).then_inc(x_loaded[i], 16)

            prepare(nc, locals())
            project(nc, locals())
        attend(nc, locals())
        finish(nc, locals())


def prepare(nc, s):
    tally = s["tally"]
    (NB, D, KT, NR, ER, E, R, ident, bias_col, mod1_col, silu_c, down_t, up_t, mod_rows) = (
        s[n] for n in "NB D KT NR ER E R ident bias_col mod1_col silu_c down_t up_t mod_rows".split())
    MC = 2 * D // BANK
    CB = NB * KT
    MR = 2 * KT * NB
    with ExitStack() as ctx:
        def sb(name, shape, dt=F32):
            return ctx.enter_context(nc.sbuf_tensor(name, shape, dt))

        def sem(name):
            return ctx.enter_context(nc.semaphore(name))

        c_in = sb("c_in", [CB, P])
        bias_in = sb("bias_in", [3 * KT, P])
        down_in = sb("down_in", [NR, D])
        up_in = sb("up_in", [P, KT, ER])
        mod1_in = sb("mod1_in", [MR, P])
        silu_e = sb("silu_e", [P, CB])
        silu_r = sb("silu_r", [P, CB])
        wm = sb("wm", [P, KT, MC * BANK])
        rows = sb("rows", [P, BANK])
        ps_small = ctx.enter_context(nc.psum_tensor("ps_small", [P, BANK], F32))
        ps_mod = ctx.enter_context(nc.psum_tensor("ps_mod", [P, BANK], F32))

        ident_ready = sem("ident_ready")
        small_loaded, mod_loaded = sem("small_loaded"), sem("mod_loaded")
        small_done, small_copied = sem("small_done"), sem("small_copied")
        silu_exp, silu_ready, dve_chain = sem("silu_exp"), sem("silu_ready"), sem("dve_chain")
        wm_loaded = [sem(f"wm_loaded{k}") for k in range(KT)]
        mod_done, rows_ready, rows_stored = sem("mod_done"), sem("rows_ready"), sem("rows_stored")
        block = ctx.enter_context(nc.Block())

        wm_view = s["wmod"].rearrange("(k p) n -> p k n", p=P)

        @block.sync
        def _(sp):
            sp.dma_start(c_in[:], s["c"].rearrange("b (k p) -> (b k) p", p=P)).then_inc(small_loaded, 16)
            for i, b in enumerate((s["bq"], s["bk"], s["bv"])):
                sp.dma_start(bias_in[i * KT:(i + 1) * KT, :], b.rearrange("(g p) -> g p", p=P)).then_inc(small_loaded, 16)
            sp.dma_start(down_in[0:ER, :], s["lora_a"].rearrange("e r d -> (e r) d")).then_inc(small_loaded, 16)
            sp.dma_start(down_in[ER:NR, :], s["router_w"]).then_inc(small_loaded, 16)
            lb = s["lora_b"].rearrange("e (t p) r -> e p t r", p=P)
            for e in range(E):
                sp.dma_start(up_in[:, :, e * R:(e + 1) * R], lb[e]).then_inc(small_loaded, 16)
            for k in range(KT):
                sp.dma_start(wm[:, k], wm_view[:, k, 0:2 * D]).then_inc(wm_loaded[k], 16)
            s["load_x"](sp, 0)
            sp.wait_ge(rows_ready, MC)
            for j in range(0, MC, 2):
                sp.dma_start(mod_rows[:, j * BANK:(j + 1) * BANK], rows[32 * j:32 * j + NB]).then_inc(rows_stored, 16)
            sp.wait_ge(rows_stored, 16 * MC)
            for b in range(0, NB, 2):
                sp.dma_start(mod1_in[b * 2 * KT:(b + 1) * 2 * KT, :], mod_rows[b, 0:2 * D].rearrange("(r p) -> r p", p=P)).then_inc(mod_loaded, 16)

        @block.gpsimd
        def _(pool):
            nc.gpsimd.memset(ident[:], 0.0).then_inc(ident_ready, 1)
            pool.wait_ge(ident_ready, 1)
            nc.gpsimd.affine_select(out=ident[:], in_=ident[:], compare_op=ALU.not_equal, fill=1.0, base=0,
                                    pattern=[[-1, P]], channel_multiplier=1).then_inc(ident_ready, 1)

        @block.tensor
        def _(pe):
            pe.wait_ge(ident_ready, 2)
            pe.wait_ge(small_loaded, 16 * (6 + E))
            nc.tensor.transpose(ps_small[:, 0:CB], c_in[:], ident[0:CB, 0:CB])
            nc.tensor.transpose(ps_small[:, P:P + 3 * KT], bias_in[:], ident[0:3 * KT, 0:3 * KT]).then_inc(small_done, 1)
            pe.wait_ge(silu_ready, 1)
            for k in range(KT):
                pe.wait_ge(small_copied, k + 1)
                nc.tensor.transpose(ps_small[:, 0:NR], down_in[:, k * P:(k + 1) * P], ident[0:NR, 0:NR])
                nc.tensor.transpose(ps_small[0:ER, P:2 * P], up_in[:, k], ident[:]).then_inc(small_done, 1)
            for k in range(KT):
                pe.wait_ge(wm_loaded[k], 16)
                for j in range(MC):
                    last = nc.tensor.matmul(ps_mod[32 * j:32 * j + NB], silu_c[:, k], wm[:, k, j * BANK:(j + 1) * BANK],
                                            start=k == 0, stop=k == KT - 1)
            last.then_inc(mod_done, 1)
            pe.wait_ge(mod_loaded, 16 * NB)
            pe.wait_ge(small_copied, KT + 1)
            nc.tensor.transpose(ps_small[:, 0:MR], mod1_in[:], ident[0:MR, 0:MR]).then_inc(small_done, 1)

        @block.scalar
        def _(act):
            act.wait_ge(small_done, 1)
            nc.scalar.activation(silu_e[:], ps_small[:, 0:CB], ACT.Exp, scale=-1.0).then_inc(silu_exp, 1)
            act.wait_ge(rows_ready, MC)
            for j in range(1, MC, 2):
                act.dma_start(mod_rows[:, j * BANK:(j + 1) * BANK], rows[32 * j:32 * j + NB]).then_inc(rows_stored, 16)
            act.wait_ge(rows_stored, 16 * MC)
            for b in range(1, NB, 2):
                act.dma_start(mod1_in[b * 2 * KT:(b + 1) * 2 * KT, :], mod_rows[b, 0:2 * D].rearrange("(r p) -> r p", p=P)).then_inc(mod_loaded, 16)

        @block.vector
        def _(dve):
            chain = Chain(dve, dve_chain, tally)
            dve.wait_ge(silu_exp, 1)
            chain.link(nc.vector.tensor_scalar_add(silu_e[:], silu_e[:], 1.0))
            chain.link(nc.vector.reciprocal(silu_r[:], silu_e[:]))
            nc.vector.tensor_tensor(silu_c[:].rearrange("p k b -> p b k"), ps_small[:, 0:CB].rearrange("p (b k) -> p b k", b=NB),
                                    silu_r[:].rearrange("p (b k) -> p b k", b=NB), ALU.mult).then_inc(silu_ready, 1)
            chain.link(nc.vector.tensor_copy(bias_col[:], ps_small[:, P:P + 3 * KT]))
            dve.sem_inc(small_copied, 1)
            for k in range(KT):
                dve.wait_ge(small_done, k + 2)
                chain.link(nc.vector.tensor_copy(down_t[:, k], ps_small[:, 0:NR]))
                nc.vector.tensor_copy(up_t[:, k * P:(k + 1) * P], ps_small[0:ER, P:2 * P]).then_inc(small_copied, 1)
            dve.wait_ge(mod_done, 1)
            for j in range(MC):
                part = slice(32 * j, 32 * j + NB)
                nc.vector.tensor_copy(rows[part], ps_mod[part]).then_inc(rows_ready, 1)
            dve.wait_ge(small_done, KT + 2)
            src = ps_small[:, 0:MR].rearrange("p (b v k) -> p b v k", b=NB, v=2)
            col = mod1_col[:].rearrange("p (b v k) -> p b v k", b=NB, v=2)
            chain.link(nc.vector.tensor_copy(col[:, :, 0], src[:, :, 0]))
            chain.link(nc.vector.tensor_scalar_add(col[:, :, 1], src[:, :, 1], 1.0))



def project(nc, s):
    tally = s["tally"]
    (xn, x_loaded, load_x, NB, L, D, KT, TT, QC, NG, ident, bias_col, mod1_col, silu_c, mod_rows, w_cols, qk_split, v_tok) = (
        s[n] for n in "xn x_loaded load_x NB L D KT TT QC NG ident bias_col mod1_col silu_c mod_rows w_cols qk_split v_tok".split())
    NH = KT * QC
    UNITS = 3 * QC
    ORDER = (2, 0, 1)
    with ExitStack() as ctx:
        def sb(name, shape, dt=F32):
            return ctx.enter_context(nc.sbuf_tensor(name, shape, dt))

        def sem(name):
            return ctx.enter_context(nc.semaphore(name))

        first_stats = sb("first_stats", [P, TT, 2, 6])
        first_mv = sb("first_mv", [P, TT, 2])
        first_rstd = sb("first_rstd", [P, TT])
        stats = sb("stats", [P, 2, 6])
        mean_var = sb("mean_var", [P, 2])
        rstd = sb("rstd", [P, 1])
        minus_half = sb("minus_half", [P, TT])
        h_full = sb("h_full", [P, 3, BANK])
        h_hi = sb("h_hi", [P, KT, L], F32R)
        h_lo = sb("h_lo", [P, KT, L], F32R)
        w_nat = sb("w_nat", [P, 3, D])
        w_raw = sb("w_raw", [P, 3, KT, P])
        w_hi = sb("w_hi2", [P, 3, KT, P], F32R)
        w_lo = sb("w_lo2", [P, 3, KT, P], F32R)
        qk_hi = sb("qk_hi", [P, 2, L], F32R)
        qk_lo = sb("qk_lo", [P, 2, L], F32R)
        v_feat = sb("v_feat", [P, QC, BANK])
        v_out = sb("v_out", [P, TT, P])
        wm = sb("wm2", [P, KT, BANK])
        rows = sb("rows2", [P, KT, P])
        ps_h = [ctx.enter_context(nc.psum_tensor(f"ps_h{i}", [P, BANK], F32)) for i in range(2)]
        ps_u = [ctx.enter_context(nc.psum_tensor(f"ps_u{i}", [P, BANK], F32)) for i in range(2)]
        ps_v = [ctx.enter_context(nc.psum_tensor(f"ps_v{i}", [P, BANK], F32)) for i in range(QC)]

        ps_w = ctx.enter_context(nc.psum_tensor("ps_w", [P, KT, P], F32))
        weights = [s[("Wq", "Wk", "Wv")[w]] for w in ORDER]
        SEG = BANK // P
        MOD0 = 2 * D
        assert 6 * D - MOD0 == KT * BANK

        first_chain, var_ready, rstd_ready, dve_chain = sem("first_chain"), sem("var_ready"), sem("rstd_ready"), sem("dve_chain2")
        xn_ready = sem("xn_ready")
        h_turned, h_full_done, h_hi_done, h_lo_done = sem("h_turned"), sem("h_full_done"), sem("h_hi_done"), sem("h_lo_done")
        w_loaded = [sem(f"w_loaded_{n}") for n in "vqk"]
        nat_loaded = [sem(f"nat_loaded_{n}") for n in "vqk"]
        w_kept = [sem(f"w_kept_{n}") for n in "vqk"]
        w_turned, w_copied = sem("w_turned"), sem("w_copied")
        wm_loaded, mod_done, rows_ready, rows_stored = sem("wm_loaded2"), sem("mod_done2"), sem("rows_ready2"), sem("rows_stored2")
        w_hi_done, w_lo_done = sem("w_hi_done2"), sem("w_lo_done2")
        unit_done, unit_free, hi_done = sem("unit_done"), sem("unit_free"), sem("hi_done")
        v_turned, v_copied = sem("v_turned"), sem("v_copied")
        v_stored, q_stored, k_stored = sem("v_stored"), sem("q_stored"), sem("k_stored")
        half_set = sem("half_set")
        block = ctx.enter_context(nc.Block())

        def load_weights(sp, m, g):
            sp.dma_start(w_raw[:, m], w_cols[ORDER[m], g].rearrange("p (k n) -> p k n", k=KT)).then_inc(w_loaded[m], 16)

        def load_natural(sp, m, g):
            sp.dma_start(w_nat[:, m], weights[m].rearrange("(g p) n -> g p n", p=P)[g]).then_inc(nat_loaded[m], 16)

        def load_mod(sp, g):
            src = s["wmod"].rearrange("(k p) n -> p k n", p=P)[:, :, MOD0:].rearrange("p k (g n) -> g p k n", n=BANK)
            sp.dma_start(wm[:], src[g]).then_inc(wm_loaded, 16)

        def batches(eng, body):
            body(0, first=True)
            with eng.Fori(1, NB - 1) as b:
                body(b)
            body(NB - 1, last=True)

        def groups(eng, body, *cuts):
            for part, (lo, hi) in enumerate(zip((0,) + cuts, cuts + (KT,))):
                if hi - lo == 1:
                    body(lo, part)
                else:
                    with eng.Fori(lo, hi) as g:
                        body(g, part)

        @block.sync
        def _(sp):
            def keep(n, m):
                wait_apart(sp, w_copied, 3 * n + m + 1, tally)
                sp.dma_start(w_cols[ORDER[m], n], w_raw[:, m].rearrange("p k n -> p (k n)")).then_inc(w_kept[m], 16)

            for m in range(3):
                load_natural(sp, m, 0)
            for m in range(3):
                sp.wait_ge(w_turned, m + 1)
                load_natural(sp, m, 1)
                keep(0, m)

            def batch(b, first=False, last=False):
                if not last:
                    wait_apart(sp, h_turned, NH * (b + 1), tally)
                    load_x(sp, b + 1)
                else:
                    load_mod(sp, 0)

                def group(g, part):
                    n = b * KT + g

                    def refill(m):
                        if first and part < 2:
                            keep(n + 1, m)
                        if first and part == 0:
                            wait_apart(sp, w_turned, 3 * (n + 1) + m + 1, tally)
                            load_natural(sp, m, g + 2)
                        else:
                            if first and part == 1:
                                sp.wait_ge(w_kept[m], 16 * KT)
                            if last and part > 0:
                                return
                            wait_apart(sp, w_lo_done, 3 * (n + 1) + m + 1, tally)
                            load_weights(sp, m, (g + 2) % KT)

                    wait_apart(sp, v_copied, QC * (n + 2), tally)
                    sp.dma_start(v_tok[n], v_out[:]).then_inc(v_stored, 16)
                    refill(0)
                    sp.wait_ge(unit_free, UNITS * n + 4 + 2)
                    sp.dma_start(qk_split[n, 0], qk_hi[:, 0].bitcast(F32)).then_inc(q_stored, 16)
                    sp.dma_start(qk_split[n, 1], qk_lo[:, 0].bitcast(F32)).then_inc(q_stored, 16)
                    refill(1)
                    sp.wait_ge(unit_free, UNITS * n + 6 + 2)
                    sp.dma_start(qk_split[n, 2], qk_hi[:, 1].bitcast(F32)).then_inc(k_stored, 16)
                    sp.dma_start(qk_split[n, 3], qk_lo[:, 1].bitcast(F32)).then_inc(k_stored, 16)
                    refill(2)
                    if last and part < 2:
                        wait_apart(sp, mod_done, g + 1, tally)
                        load_mod(sp, g + 1)

                groups(sp, group, *((KT - 2, KT - 1) if first or last else ()))

            batches(sp, batch)
            sp.wait_ge(rows_ready, SEG * (KT + 1))
            for j in range(SEG):
                dst = mod_rows[:, MOD0:].rearrange("b (g j n) -> j b g n", j=SEG, n=P)[j]
                sp.dma_start(dst, rows[32 * j:32 * j + NB]).then_inc(rows_stored, 16)
            sp.wait_ge(rows_stored, 16 * SEG)
            sp.wait_ge(wm_loaded, 16 * KT)
            sp.wait_ge(v_stored, 16 * (NG + 1))
            sp.wait_ge(q_stored, 32 * (NG + 1))
            sp.wait_ge(k_stored, 32 * (NG + 1))
            for m in range(3):
                sp.wait_ge(w_loaded[m], 16 * (NG - KT))

        @block.gpsimd
        def _(pool):
            nc.gpsimd.memset(minus_half[:], -0.5).then_inc(half_set, 1)
            pool.wait_ge(half_set, 1)

            def rsqrt(tile):
                pool.wait_ge(var_ready, tile + 1)
                nc.gpsimd.tensor_tensor(rstd[:], mean_var[:, 1:2], minus_half[:, 0:1], ALU.pow).then_inc(rstd_ready, 1)

            def batch(b, first=False, last=False):
                for i in range(NH):
                    half, k = divmod(i, KT)
                    pool.wait_ge(h_hi_done, NH * b + i + 1)
                    cols = slice(half * BANK, (half + 1) * BANK)
                    nc.gpsimd.tensor_tensor(h_lo[:, k, cols], h_full[:, i % 3], h_hi[:, k, cols].bitcast(F32), ALU.subtract).then_inc(h_lo_done, 1)

                def group(g, part):
                    if not (last and part == 1):
                        for m in range(3):
                            weights_lo(b * KT + g + 1, m)
                    if not last:
                        rsqrt((b + 1) * TT + g)

                groups(pool, group, *((KT - 1,) if last else ()))

            def weights_lo(n, m):
                pool.wait_ge(w_hi_done, 3 * n + m + 1)
                nc.gpsimd.tensor_tensor(w_lo[:, m], w_raw[:, m], w_hi[:, m].bitcast(F32), ALU.subtract).then_inc(w_lo_done, 1)

            half = TT // QC
            for i in range(QC):
                pool.wait_ge(var_ready, (i + 1) * half)
                tiles = slice(i * half, (i + 1) * half)
                nc.gpsimd.tensor_tensor(first_rstd[:, tiles], first_mv[:, tiles, 1], minus_half[:, tiles], ALU.pow).then_inc(rstd_ready, half)
            for m in range(3):
                weights_lo(0, m)
            batches(pool, batch)

        @block.scalar
        def _(act):
            for st, n in ((v_stored, 16), (q_stored, 32), (k_stored, 32)):
                act.sem_inc(st, n)
            act.sem_inc(v_copied, QC)

            def split_hi(n, g, u):
                m, ch = divmod(u, QC)
                if ch == 0:
                    act.wait_ge((q_stored, k_stored)[m - 1], 32 * (n + 1))
                wait_apart(act, unit_done, UNITS * n + u + 1, tally)
                bias = bias_col[:, bass.ds(ORDER[m] * KT + g, 1)]
                nc.scalar.activation(qk_hi[:, m - 1, ch * BANK:(ch + 1) * BANK], ps_u[u % 2][:], ACT.Identity, bias=bias, scale=1.0).then_inc(hi_done, 1)

            def copy_v(n, ch):
                act.wait_ge(v_turned, QC * n + ch + 1)
                if ch == 0:
                    act.wait_ge(v_stored, 16 * (n + 1))
                half = TT // QC
                nc.scalar.activation(v_out[:, ch * half:(ch + 1) * half], ps_v[ch][:].rearrange("p (t n) -> p t n", n=P), ACT.Copy).then_inc(v_copied, 1)

            def copy_w(n, m):
                if not (isinstance(n, int) and n == 0):
                    act.wait_ge(w_lo_done, 3 * (n - 1) + m + 1)
                    act.wait_ge(w_kept[m], 16 * n)
                act.wait_ge(w_turned, 3 * n + m + 1)
                nc.scalar.activation(w_raw[:, m], ps_w[:], ACT.Copy).then_inc(w_copied, 1)

            def weights_hi(n, m, copied):
                if copied:
                    copy_w(n, m)
                    act.wait_ge(w_copied, 3 * n + m + 1)
                else:
                    act.wait_ge(w_loaded[m], 16 * (n + 1 - KT))
                nc.scalar.activation(w_hi[:, m], w_raw[:, m], ACT.Copy).then_inc(w_hi_done, 1)

            for m in range(3):
                weights_hi(0, m, True)

            def batch(b, first=False, last=False):
                for i in range(NH):
                    half, k = divmod(i, KT)
                    act.wait_ge(h_full_done, NH * b + i + 1 + 2)
                    nc.scalar.activation(h_hi[:, k, half * BANK:(half + 1) * BANK], h_full[:, i % 3], ACT.Copy).then_inc(h_hi_done, 1)

                def group(g, part):
                    n = b * KT + g
                    copied = first and part == 0
                    more = not (last and part == 1)
                    split_hi(n, g, 2)
                    if more:
                        weights_hi(n + 1, 0, copied)
                    copy_v(n, 0)
                    copy_v(n, 1)
                    split_hi(n, g, 3)
                    split_hi(n, g, 4)
                    if more:
                        weights_hi(n + 1, 1, copied)
                    split_hi(n, g, 5)
                    if more:
                        weights_hi(n + 1, 2, copied)

                groups(act, group, *((KT - 1,) if first or last else ()))

            batches(act, batch)

        @block.vector
        def _(dve):
            dve.sem_inc(unit_free, 2)
            dve.sem_inc(h_full_done, 2)
            dve.sem_inc(h_lo_done, 3)

            def layernorm(tile, t):
                chain = Chain(dve, dve_chain, tally, (tile - TT) * 3)
                src = xn[:, t]
                for i in range(2):
                    last = nc.vector.bn_stats(stats[:, i], src[:, i * (D // 2):(i + 1) * (D // 2)])
                    chain.link(last)
                chain.link(nc.vector.bn_aggr(mean_var[:], stats[:].rearrange("p a b -> p (a b)")))
                nc.vector.tensor_scalar_add(mean_var[:, 1:2], mean_var[:, 1:2], EPS).then_inc(var_ready, 1)
                dve.wait_ge(rstd_ready, tile + 1)
                nc.vector.tensor_scalar(src, src, mean_var[:, 0:1], rstd[:], ALU.subtract, ALU.mult).then_inc(xn_ready, 1)

            def batch(b, first=False, last=False):
                cols = mod1_col[:].rearrange("p (b v k) -> p b v k", b=NB, v=2)
                for i in range(NH):
                    half, k = divmod(i, KT)
                    dve.wait_ge(h_turned, NH * b + i + 1)
                    dve.wait_ge(h_lo_done, NH * b + i + 1)
                    nc.vector.tensor_scalar(h_full[:, i % 3], ps_h[i % 2][:], cols[:, b, 1, k:k + 1], cols[:, b, 0, k:k + 1],
                                            ALU.mult, ALU.add).then_inc(h_full_done, 1)
                with dve.Fori(0, KT) as g:
                    n = b * KT + g
                    for u in range(UNITS):
                        if last and u == UNITS - 1:
                            wait_apart(dve, mod_done, g + 1, tally)
                            for j in range(SEG):
                                part = slice(32 * j, 32 * j + NB)
                                nc.vector.tensor_copy(rows[part, bass.ds(g, 1)], ps_w[part, 0:1]).then_inc(rows_ready, 1)
                        m, ch = divmod(u, QC)
                        bias = bias_col[:, bass.ds(ORDER[m] * KT + g, 1)]
                        if m == 0:
                            dve.wait_ge(unit_done, UNITS * n + u + 1)
                            dve.wait_ge(v_copied, QC * n + ch + 1)
                            nc.vector.tensor_scalar(v_feat[:, ch], ps_u[u % 2][:], bias, None, ALU.add).then_inc(unit_free, 1)
                        else:
                            dve.wait_ge(hi_done, (UNITS - QC) * n + u - QC + 1)
                            part = slice(ch * BANK, (ch + 1) * BANK)
                            nc.vector.scalar_tensor_tensor(qk_lo[:, m - 1, part], ps_u[u % 2][:], bias, qk_hi[:, m - 1, part].bitcast(F32),
                                                           ALU.add, ALU.subtract).then_inc(unit_free, 1)
                    if not last:
                        for i in range(QC):
                            dve.wait_ge(x_loaded[i], 16 * (b + 2))
                        layernorm((b + 1) * TT + g, g)

            half = TT // QC
            for i in range(QC):
                dve.wait_ge(x_loaded[i], 16)
                for t in range(i * half, (i + 1) * half):
                    for p in range(2):
                        nc.vector.bn_stats(first_stats[:, t, p], xn[:, t, p * (D // 2):(p + 1) * (D // 2)]).then_inc(first_chain, 1)
                for t in range(i * half, (i + 1) * half):
                    dve.wait_ge(first_chain, (3 * i + 2) * half)
                    nc.vector.bn_aggr(first_mv[:, t], first_stats[:, t].rearrange("p a b -> p (a b)")).then_inc(first_chain, 1)
                dve.wait_ge(first_chain, 3 * (i + 1) * half)
                tiles = slice(i * half, (i + 1) * half)
                nc.vector.tensor_scalar_add(first_mv[:, tiles, 1], first_mv[:, tiles, 1], EPS).then_inc(var_ready, half)
            for i in range(QC):
                dve.wait_ge(rstd_ready, (i + 1) * half)
                for t in range(i * half, (i + 1) * half):
                    nc.vector.tensor_scalar(xn[:, t], xn[:, t], first_mv[:, t, 0:1], first_rstd[:, t:t + 1], ALU.subtract, ALU.mult).then_inc(xn_ready, 1)
            batches(dve, batch)

        @block.tensor
        def _(pe):
            def turn_w(n, m):
                pe.wait_ge(nat_loaded[m], 16 * (n + 1))
                if not (isinstance(n, int) and n == 0 and m == 0):
                    pe.wait_ge(w_copied, 3 * n + m)
                for k in range(KT):
                    last = nc.tensor.transpose(ps_w[:, k], w_nat[:, m, k * P:(k + 1) * P], ident[:])
                last.then_inc(w_turned, 1)

            for m in range(3):
                turn_w(0, m)

            def batch(b, first=False, last=False):
                for i in range(NH):
                    half, k = divmod(i, KT)
                    if k == 0:
                        pe.wait_ge(xn_ready, TT * b + (half + 1) * (TT // QC))
                    pe.wait_ge(h_full_done, NH * b + i + 1)
                    for t in range(BANK // P):
                        done = nc.tensor.transpose(ps_h[i % 2][:, t * P:(t + 1) * P], xn[:, half * (BANK // P) + t, k * P:(k + 1) * P], ident[:])
                    done.then_inc(h_turned, 1)

                def group(g, part):
                    n = b * KT + g
                    turn = first and part == 0

                    def unit(u):
                        m, ch = divmod(u, QC)
                        if ch == 0:
                            pe.wait_ge(w_lo_done, 3 * n + m + 1)
                        if m == 0:
                            wait_apart(pe, h_lo_done, NH * b + KT * (ch + 1) + 3, tally)
                        pe.wait_ge(unit_free, UNITS * n + u + 1)
                        tok = slice(ch * BANK, (ch + 1) * BANK)
                        for k in range(KT):
                            for j, (w, h) in enumerate(((w_hi, h_hi), (w_lo, h_hi), (w_hi, h_lo))):
                                last = nc.tensor.matmul(ps_u[u % 2][:], w[:, m, k], h[:, k, tok], start=k == 0 and j == 0, stop=k == KT - 1 and j == 2)
                        last.then_inc(unit_done, 1)

                    def turn_v(ch):
                        pe.wait_ge(unit_free, UNITS * n + ch + 1 + 2)
                        pe.wait_ge(v_copied, QC * n + ch + 1)
                        for t in range(BANK // P):
                            last = nc.tensor.transpose(ps_v[ch][:, t * P:(t + 1) * P], v_feat[:, ch, t * P:(t + 1) * P], ident[:])
                        last.then_inc(v_turned, 1)

                    unit(0)
                    unit(1)
                    unit(2)
                    turn_v(0)
                    turn_v(1)
                    if turn:
                        turn_w(n + 1, 0)
                    if last:
                        pe.wait_ge(wm_loaded, 16 * (g + 1))
                        wait_apart(pe, rows_ready, SEG * g + SEG, tally)
                        for k in range(KT):
                            for j in range(SEG):
                                done = nc.tensor.matmul(ps_w[32 * j:32 * j + NB, 0], silu_c[:, k], wm[:, k, j * P:(j + 1) * P],
                                                        start=k == 0, stop=k == KT - 1)
                        done.then_inc(mod_done, 1)
                    unit(3)
                    unit(4)
                    if turn:
                        turn_w(n + 1, 1)
                    unit(5)
                    if turn:
                        turn_w(n + 1, 2)

                groups(pe, group, *((KT - 1,) if first else ()))

            pe.sem_inc(rows_ready, SEG)
            batches(pe, batch)



def attend(nc, s):
    tally = s["tally"]
    (L, KT, TT, HD, HG, QC, NG, SCALE, QK_ROWS, SHIFT_ROW, ident, qk_split, v_tok, att_raw, att_sum) = (
        s[n] for n in "L KT TT HD HG QC NG SCALE QK_ROWS SHIFT_ROW ident qk_split v_tok att_raw att_sum".split())
    SLOTS = 4
    CT = BANK // P
    steps = [(ch, j) for ch in reversed(range(QC)) for j in range((ch + 1) * CT)]
    NSTEP = len(steps)
    diagonal = [k for k, (ch, j) in enumerate(steps) if j >= ch * CT]
    full = [k for k, (ch, j) in enumerate(steps) if j < ch * CT]
    ADDS = HG * (len(full) - 1)
    PBUF = 4
    rows = [(i, ch, h) for i in range(TT) for ch in range(i // CT + 1) for h in range(HG)]
    NROW = len(rows)
    ROW_USES = NROW + 1
    HALF = NROW // 2
    ends = [k for k, (ch, j) in enumerate(steps) if j == (ch + 1) * CT - 1]
    assert QC == 2 and full == list(range(PBUF))
    assert NROW == 4 * NSTEP and NG % SLOTS == 0 and NSTEP % PBUF == 0

    def strewn(i, last):
        one = [(1, u) for u in range(HALF, NROW)] if not (last and i + 1 >= SLOTS) else []
        two = [(2, u) for u in range(HALF)] if not (last and i + 2 >= SLOTS) else []
        return one + two[:3] + [(1, NROW)] + two[3:] if one else []

    def order(t, p):
        return ROW_USES * (t + 1) + HALF + p

    with ExitStack() as ctx:
        def sb(name, shape, dt=F32):
            return ctx.enter_context(nc.sbuf_tensor(name, shape, dt))

        def sem(name):
            return ctx.enter_context(nc.semaphore(name))

        q_st = [sb(f"q_st{i}", [SHIFT_ROW + 1, HG, L], F32R) for i in range(SLOTS)]
        k_st = [sb(f"k_st{i}", [SHIFT_ROW + 1, HG, L], F32R) for i in range(SLOTS)]
        v_sb = [sb(f"v_sb{i}", [P, TT, P]) for i in range(SLOTS)]
        prob = sb("prob", [P, PBUF, HG, BANK])
        added = sb("added", [P, HG, BANK])
        ones = sb("ones", [P, HD])
        ident_b = sb("ident_b", [P, P], BF16)
        mask_b = sb("mask_b", [P, P], BF16)
        part_max = sb("part_max", [P, HG * TT, QC])
        row_max = sb("row_max", [P, HG * TT])
        shift = sb("shift", [HG * TT, P], F32R)
        att = sb("att", [P, QC, BANK])
        sums = sb("sums", [P, QC, BANK])
        ps_s = [ctx.enter_context(nc.psum_tensor(f"ps_s{i}", [P, 2, BANK], F32)) for i in range(2)]
        ps_r = [ctx.enter_context(nc.psum_tensor(f"ps_r{i}", [P, BANK], F32)) for i in range(2)]
        first_banks = ps_r + [ps[:, j] for ps in ps_s for j in range(2)]
        FB = len(first_banks)
        ps_o = ctx.enter_context(nc.psum_tensor("ps_o", [P, BANK], F32))
        ps_sum = ctx.enter_context(nc.psum_tensor("ps_sum", [P, BANK], F32))

        const_ready, mask_ready, pool_const = sem("const_ready"), sem("mask_ready"), sem("pool_const")
        qkv_loaded = [sem(f"qkv_loaded{i}") for i in range(SLOTS)]
        slot_free = sem("slot_free")
        row_done, row_free, max_ready, dve_chain = sem("row_done"), sem("row_free"), sem("max_ready"), sem("dve_chain3")
        shift_loaded = [sem(f"shift_loaded{i}") for i in range(SLOTS)]
        score_done, score_free, masked = sem("score_done"), sem("score_free"), sem("masked")
        prob_free, out_free, add_done = sem("prob_free"), sem("out_free"), sem("add_done")
        att_stored = [sem(f"att_stored{i}") for i in range(QC)]
        block = ctx.enter_context(nc.Block())

        def groups(eng, body):
            with eng.Fori(0, NG // SLOTS - 1) as tb:
                for i in range(SLOTS):
                    body(tb, i, False)
            for i in range(SLOTS):
                body(NG // SLOTS - 1, i, True)

        @block.sync
        def _(sp):
            def load(t, slot):
                for place, part in ((0, 0), (1, 1), (2, 0)):
                    sp.dma_start(q_st[slot][place * HD:(place + 1) * HD].bitcast(F32), qk_split[t, part].rearrange("(h d) n -> d h n", d=HD)).then_inc(qkv_loaded[slot], 16)
                for place, part in ((0, 2), (1, 2), (2, 3)):
                    sp.dma_start(k_st[slot][place * HD:(place + 1) * HD].bitcast(F32), qk_split[t, part].rearrange("(h d) n -> d h n", d=HD)).then_inc(qkv_loaded[slot], 16)
                sp.dma_start(v_sb[slot][:], v_tok[t]).then_inc(qkv_loaded[slot], 16)

            def load_shift(slot, before):
                sp.wait_ge(row_free, before + 1 + 2)
                sp.dma_start(q_st[slot][SHIFT_ROW:SHIFT_ROW + 1].bitcast(F32).rearrange("o h n -> o (h n)"),
                             shift[:].bitcast(F32)).then_inc(shift_loaded[slot], 16)

            for t in range(SLOTS - 1):
                load(t, t)
            load_shift(0, NROW)

            def group(tb, i, last):
                t = tb * SLOTS + i
                if not (last and i > 0):
                    sp.wait_ge(slot_free, t + 1)
                    load(t + SLOTS - 1, (i + SLOTS - 1) % SLOTS)
                if not (last and i == SLOTS - 1):
                    load_shift((i + 1) % SLOTS, order(t, strewn(i, last).index((1, NROW))))
                b, g = (tb * SLOTS + i) // KT, (tb * SLOTS + i) % KT
                for n, k in enumerate(ends):
                    ch = steps[k][0]
                    cols = slice(ch * BANK, (ch + 1) * BANK)
                    wait_apart(sp, out_free, 2 * (QC * t + n + 1) + 2, tally)
                    sp.dma_start(att_raw[b, g, :, cols], att[:, ch]).then_inc(att_stored[ch], 16)
                    sp.dma_start(att_sum[b, g, :, cols], sums[::HD, ch]).then_inc(att_stored[ch], 16)

            groups(sp, group)
            for ch in range(QC):
                sp.wait_ge(att_stored[ch], 32 * (NG + 1))

        @block.gpsimd
        def _(pool):
            nc.gpsimd.memset(mask_b[:], 0.0).then_inc(pool_const, 1)
            nc.gpsimd.tensor_copy(ident_b[:], ident[:]).then_inc(mask_ready, 1)
            pool.wait_ge(pool_const, 1)
            nc.gpsimd.affine_select(out=mask_b[:], in_=mask_b[:], compare_op=ALU.is_ge, fill=MASKED, base=0,
                                    pattern=[[-1, P]], channel_multiplier=1).then_inc(mask_ready, 1)
            nc.gpsimd.memset(ones[:], 1.0).then_inc(const_ready, 1)
            pool.wait_ge(mask_ready, 2)
            pool.wait_ge(const_ready, 1)
            for i in range(SLOTS):
                nc.gpsimd.memset(k_st[i][SHIFT_ROW:SHIFT_ROW + 1].bitcast(F32), 1.0).then_inc(const_ready, 1)
            pool.wait_ge(const_ready, SLOTS + 1)

            def group(tb, i, last):
                t = tb * SLOTS + i
                def add(k, h, heads):
                    if h == 0:
                        wait_apart(pool, score_free, 2 * NSTEP * t + 2 * (k + 1) + 2, tally)
                    if k > 1:
                        pool.wait_ge(add_done, ADDS * t + HG * (k - 2) + h + heads)
                    part = slice(h, h + heads)
                    so_far = prob[:, 0, part] if k == 1 else added[:, part]
                    nc.gpsimd.tensor_tensor(added[:, part], so_far, prob[:, k % PBUF, part], ALU.add).then_inc(add_done, heads)

                def mask(k):
                    ch, j = steps[k]
                    wait_apart(pool, score_free, 2 * NSTEP * t + 2 * (k + 1) + 2, tally)
                    off = j * P - ch * BANK
                    block_p = prob[:, k % PBUF, :, off:off + P]
                    nc.gpsimd.affine_select(out=block_p, in_=block_p, compare_op=ALU.is_ge, fill=0.0, base=0,
                                            pattern=[[0, HG], [1, P]], channel_multiplier=-1).then_inc(masked, 1)

                for k in full[1:-1]:
                    add(k, 0, HG)
                cuts = iter(((0, 2), (2, 1), (3, 1)))
                for k in diagonal:
                    mask(k)
                    for h, heads in [next(cuts)] if k in diagonal[:3] else []:
                        add(full[-1], h, heads)

            groups(pool, group)

        @block.scalar
        def _(act):
            act.sem_inc(score_free, 2)
            act.sem_inc(out_free, 2)
            for ch in range(QC):
                act.sem_inc(att_stored[ch], 32)

            def copy_out(t, n):
                k = ends[n]
                ch = steps[k][0]
                act.wait_ge(att_stored[ch], 32 * (t + 1))
                act.wait_ge(prob_free, NSTEP * t + k + 1 + PBUF)
                nc.scalar.activation(att[:, ch], ps_o[:], ACT.Copy).then_inc(out_free, 1)
                nc.scalar.activation(sums[:, ch], ps_sum[:], ACT.Copy).then_inc(out_free, 1)

            def group(tb, i, last):
                t = tb * SLOTS + i
                for k, (ch, j) in enumerate(steps):
                    off = max(j * P - ch * BANK, 0)
                    act.wait_ge(prob_free, NSTEP * t + k + 1)
                    if k - PBUF in full:
                        act.wait_ge(add_done, ADDS * t + HG * max(k - PBUF, 1))
                    for pair in range(2):
                        act.wait_ge(score_done, 2 * NSTEP * t + 2 * k + pair + 1)
                        nc.scalar.activation(prob[:, k % PBUF, 2 * pair:2 * pair + 2, off:], ps_s[pair][:, :, off:], ACT.Exp, scale=SCALE).then_inc(score_free, 1)
                    if k - 1 in ends:
                        copy_out(t, ends.index(k - 1))
                copy_out(t, QC - 1)

            groups(act, group)

        @block.vector
        def _(dve):
            dve.sem_inc(row_free, 2)
            nc.vector.memset(part_max[:], MASKED).then_inc(dve_chain, 1)
            dve.wait_ge(dve_chain, 1)

            def max_row(u, before, bank):
                i, ch, h = rows[u]
                width = min(BANK, (i + 1) * P - ch * BANK)
                dve.wait_ge(row_done, before + 1)
                nc.vector.reduce_max(part_max[:, h * TT + i, ch:ch + 1], bank[:, 0:width], AX.X).then_inc(row_free, 1)

            def max_all(n, before):
                dve.wait_ge(row_free, before + 2)
                nc.vector.reduce_max(row_max[:], part_max[:], AX.X).then_inc(max_ready, 1)
                dve.wait_ge(max_ready, n + 1)

            def max_shift(before, bank):
                dve.wait_ge(row_done, before + 1)
                nc.vector.tensor_scalar(shift[:], bank[0:HG * TT, 0:P], -1.0, None, ALU.mult).then_inc(row_free, 1)

            for u in range(NROW):
                max_row(u, u, first_banks[u % FB])
            max_all(0, NROW)
            max_shift(NROW, first_banks[NROW % FB])
            for u in range(HALF):
                max_row(u, ROW_USES + u, first_banks[(ROW_USES + u) % FB])

            def group(tb, i, last):
                t = tb * SLOTS + i
                for p, (ahead, u) in enumerate(strewn(i, last)):
                    bank = ps_r[order(i, p) % 2]
                    if u == NROW:
                        dve.wait_ge(shift_loaded[i], 16 * (tb + 1))
                        max_shift(order(t, p), bank)
                    else:
                        max_row(u, order(t, p), bank)
                    if (ahead, u) == (1, NROW - 1):
                        max_all(t + 1, order(t, p + 1))

            groups(dve, group)

        @block.tensor
        def _(pe):
            pe.sem_inc(prob_free, PBUF)
            pe.sem_inc(slot_free, 1)
            pe.wait_ge(mask_ready, 2)

            def row(slot, u, before, bank, banks=2):
                i, ch, h = rows[u]
                width = min(BANK, (i + 1) * P - ch * BANK)
                cols = max(width, 2 * P)
                on_diagonal = ch == i // CT
                if not (isinstance(before, int) and before < banks):
                    pe.wait_ge(row_free, before - banks + 1 + 2)
                last = nc.tensor.matmul(bank[:, 0:cols], q_st[slot][0:QK_ROWS, h, i * P:(i + 1) * P],
                                        k_st[slot][0:QK_ROWS, h, ch * BANK:ch * BANK + cols], start=True, stop=not on_diagonal)
                if on_diagonal:
                    last = nc.tensor.matmul(bank[:, width - P:width], ident_b[:], mask_b[:], start=False, stop=True)
                last.then_inc(row_done, 1)

            def turn_max(t, before, bank, banks=2):
                pe.wait_ge(max_ready, t + 1)
                pe.wait_ge(row_free, before - banks + 1 + 2)
                nc.tensor.transpose(bank[0:HG * TT, 0:P], row_max[:], ident[:]).then_inc(row_done, 1)

            def scores(t, slot, k, pair):
                ch, j = steps[k]
                off = max(j * P - ch * BANK, 0)
                off = min(off, BANK - 2 * P)
                pe.wait_ge(score_free, 2 * NSTEP * t + 2 * k + pair + 1)
                for h in range(2):
                    last = nc.tensor.matmul(ps_s[pair][:, h, off:], k_st[slot][:, 2 * pair + h, j * P:(j + 1) * P],
                                            q_st[slot][:, 2 * pair + h, ch * BANK + off:(ch + 1) * BANK], start=True, stop=True)
                last.then_inc(score_done, 1)

            def weigh(t, slot, k):
                ch, j = steps[k]
                off = max(j * P - ch * BANK, 0)
                if j == 0:
                    pe.wait_ge(out_free, 2 * (QC * t + ends.index(k + (ch + 1) * CT - 1)) + 2)
                if k in diagonal:
                    pe.wait_ge(masked, len(diagonal) * t + diagonal.index(k) + 1)
                else:
                    pe.wait_ge(score_free, 2 * NSTEP * t + 2 * (k + 1) + 2)
                for h in range(HG):
                    part = slice(h * HD, (h + 1) * HD)
                    last = nc.tensor.matmul(ps_o[part, off:], v_sb[slot][:, j, part], prob[:, k % PBUF, h, off:], start=j == 0, stop=k in ends)
                if k in full:
                    last.then_inc(prob_free, 1)

            def add_up(t, k):
                if k in full:
                    return
                ch, j = steps[k]
                off = max(j * P - ch * BANK, 0)
                if k in ends and ch > 0:
                    pe.wait_ge(add_done, ADDS * (t + 1))
                    for h in range(HG):
                        nc.tensor.matmul(ps_sum[h * HD:(h + 1) * HD, :], ones[:], added[:, h], start=False, stop=False)
                for h in range(HG):
                    last = nc.tensor.matmul(ps_sum[h * HD:(h + 1) * HD, off:], ones[:], prob[:, k % PBUF, h, off:], start=j == ch * CT, stop=k in ends)
                last.then_inc(prob_free, 1)

            pe.wait_ge(qkv_loaded[0], 16 * 7)
            for u in range(NROW):
                row(0, u, u, first_banks[u % FB], FB)
            turn_max(0, NROW, first_banks[NROW % FB], FB)
            pe.wait_ge(qkv_loaded[1], 16 * 7)
            for u in range(HALF):
                row(1, u, ROW_USES + u, first_banks[(ROW_USES + u) % FB], FB)

            pe.wait_ge(const_ready, SLOTS + 1)
            pe.wait_ge(row_free, ROW_USES + HALF + 2)

            def group(tb, i, last):
                t = tb * SLOTS + i
                todo = list(enumerate(strewn(i, last)))

                def pass_1():
                    if todo:
                        p, (ahead, u) = todo.pop(0)
                        bank = ps_r[order(i, p) % 2]
                        if u == NROW:
                            turn_max(t + 1, order(t, p), bank)
                        else:
                            slot = (i + ahead) % SLOTS
                            if ahead == 2 and u == 0:
                                pe.wait_ge(qkv_loaded[slot], 16 * 7 * (tb + 1 + (i + 2) // SLOTS))
                            row(slot, u, order(t, p), bank)

                pe.wait_ge(shift_loaded[i], 16 * (tb + 1))
                for k in range(NSTEP):
                    scores(t, i, k, 0)
                    pass_1()
                    if k > 0:
                        weigh(t, i, k - 1)
                    pass_1()
                    scores(t, i, k, 1)
                    pass_1()
                    if k > 0:
                        add_up(t, k - 1)
                    pass_1()
                while todo:
                    pass_1()
                weigh(t, i, NSTEP - 1)
                add_up(t, NSTEP - 1)
                pe.wait_ge(prob_free, NSTEP * (t + 1) + PBUF)
                pe.sem_inc(slot_free, 1)

            groups(pe, group)


def finish(nc, s):
    tally = s["tally"]
    (x, out, bo, NB, L, D, KT, E, R, ER, NR, ident, down_t, up_t, mod_rows, gate_rows, Wo, att_raw, att_sum, att_inv, HD, HG) = (
        s[n] for n in "x out bo NB L D KT E R ER NR ident down_t up_t mod_rows gate_rows Wo att_raw att_sum att_inv HD HG".split())
    T = 2
    CW = T * P
    CPB = L // CW
    NC = NB * CPB
    HV = D // BANK
    UN = T * HV
    KP = BANK // CW
    TG = KT // KP
    TB = TG - 1
    with ExitStack() as ctx:
        def sb(name, shape, dt=F32):
            return ctx.enter_context(nc.sbuf_tensor(name, shape, dt))

        def sem(name):
            return ctx.enter_context(nc.semaphore(name))

        wo_hi = sb("wo_hi", [P, KT, D], F32R)
        wo_lo = sb("wo_lo", [P, KT, D], F32R)
        at_hi = [sb(f"at_hi{i}", [P, KT, CW], F32R) for i in range(2)]
        at_lo = [sb(f"at_lo{i}", [P, KT, CW], F32R) for i in range(2)]
        res = [sb(f"res{i}", [P, T, D]) for i in range(2)]
        at_raw = sb("at_raw", [P, KT, CW])
        at_inv = sb("at_inv", [P, KT, CW])
        mod2_in = sb("mod2_in", [2 * KT * NB, P])
        mod2_col = sb("mod2_col", [P, NB * 2 * KT])
        gate_in = sb("gate_in", [2 * KT * NB, P])
        sign = sb("sign", [2 * KT * NB, P])
        mag = sb("mag", [2 * KT * NB, P])
        inv = sb("inv", [P, NB, HEADS * L // P])
        gates_bc = sb("gates_bc", [P, 2, 2, D])
        bo_bc = sb("bo_bc", [P, D])
        att_y = sb("att_y", [P, UN, BANK])
        xn = sb("xn4", [P, T, D])
        h2t = sb("h2t", [P, KT, CW])
        delta = sb("delta", [P, T, D])
        stats = sb("stats4", [P, 2, 6])
        mean_var = sb("mean_var4", [P, T, 2])
        rstd = sb("rstd4", [P, T])
        minus_half = sb("minus_half4", [P, 1])
        lower = sb("lower", [P, E, E])
        down = sb("down", [P, T, NR])
        top1 = sb("top1", [P, T])
        above = sb("above", [P, T, E, E])
        equal = sb("equal", [P, T, E, E])
        rank = sb("rank", [P, T, E])
        logit = sb("logit", [P, T, E])
        expo = sb("expo", [P, T, E])
        kept = sb("kept", [P, T, E])
        denom = sb("denom", [P, T])
        gate = sb("gate", [P, T, E])
        mid = sb("mid", [P, T, ER])
        mid_t = sb("mid_t", [ER, CW])
        ps_y2 = ctx.enter_context(nc.psum_tensor("ps_y", [P, 2, BANK], F32))
        ps_t = [ctx.enter_context(nc.psum_tensor(f"ps_t{i}", [P, BANK], F32)) for i in range(TB)]
        ps_l = ctx.enter_context(nc.psum_tensor("ps_l", [P, BANK], F32))
        ps_d2 = ctx.enter_context(nc.psum_tensor("ps_d", [P, 2, BANK], F32))
        ps_y, ps_d = [ps_y2[:, i] for i in range(2)], [ps_d2[:, i] for i in range(2)]
        wo_in = [xn[:, 0], xn[:, 1], delta[:, 0], delta[:, 1]]
        wo_in += [att_y[:, i * HV:(i + 1) * HV].rearrange("p a b -> p (a b)") for i in range(T)]
        wo_in += [h2t[:, i * KT // T:(i + 1) * KT // T].rearrange("p k c -> p (k c)") for i in range(T)]
        ps_wo = [ps.rearrange("p a (k n) -> p (a k) n", n=P) for ps in (ps_y2[:], ps_d2[:])]
        assert len(wo_in) == KT

        wo_loaded = [sem(f"wo_loaded{t}") for t in range(KT)]
        wo_turned, wo_hi_done, wo_lo_done = sem("wo_turned"), sem("wo_hi_done"), sem("wo_lo_done")
        bc_loaded, gates_loaded, const_ready = sem("bc_loaded"), sem("gates_loaded"), sem("const_ready4")
        mod_loaded, mod_turned, mod_ready = sem("mod_loaded4"), sem("mod_turned"), sem("mod_ready")
        gate_loaded, gate_ready, gate_stored = sem("gate_loaded"), sem("gate_ready"), sem("gate_stored")
        at_loaded, at_divided = sem("at_loaded"), sem("at_divided")
        at_hi_done, at_lo_done = sem("at_hi_done"), sem("at_lo_done")
        sums_loaded, inv_ready, inv_stored = sem("sums_loaded"), sem("inv_ready"), sem("inv_stored")
        res_loaded = [sem(f"res_loaded{i}") for i in range(2)]
        y_done, y_free, x1_ready = sem("y_done"), sem("y_free"), sem("x1_ready")
        dve_chain, start_chain, var_ready, rstd_ready, xn_ready = sem("dve_chain4"), sem("start_chain"), sem("var_ready4"), sem("rstd_ready4"), sem("xn_ready4")
        turned, h2_ready, down_done = sem("turned"), sem("h2_ready"), sem("down_done")
        logit_ready, exp_ready, mid_ready = sem("logit_ready"), sem("exp_ready"), sem("mid_ready")
        mid_turned, mid_t_ready = sem("mid_turned"), sem("mid_t_ready")
        d_done, d_free, out_ready, out_stored = sem("d_done"), sem("d_free"), sem("out_ready"), sem("out_stored")
        block = ctx.enter_context(nc.Block())

        def chunks(eng, body):
            with eng.Fori(0, NB - 1) as b:
                for i in range(CPB):
                    body(b, i, False)
            for i in range(CPB):
                body(NB - 1, i, True)

        def tokens(a, b, i):
            return a[b + i // CPB, (i % CPB) * CW:(i % CPB + 1) * CW, :].rearrange("(t p) d -> p t d", p=P)

        @block.sync
        def _(sp):
            def load_raw(b, i):
                cols = slice((i % CPB) * CW, (i % CPB + 1) * CW)
                sp.dma_start(at_raw[:], att_raw[b + i // CPB].rearrange("g p n -> p g n")[:, :, cols]).then_inc(at_loaded, 16)

            def load_inv(b, i):
                cols = slice((i % CPB) * CW, (i % CPB + 1) * CW)
                for h in range(HG):
                    src = att_inv[b + i // CPB, :, h, cols].unsqueeze(0).to_broadcast([HD, KT, CW])
                    sp.dma_start(at_inv[h * HD:(h + 1) * HD], src).then_inc(at_loaded, 16)

            def load_at(b, i):
                load_raw(b, i)
                load_inv(b, i)

            def load_res(b, i):
                sp.dma_start(res[i % 2][:], tokens(x, b, i)).then_inc(res_loaded[i % 2], 16)

            def load_gates(b):
                src = gate_rows[bass.ds(b, 1)].to_broadcast([P, 2, D])
                sp.dma_start(gates_bc[:, :, b % 2], src).then_inc(gates_loaded, 16)

            def by_partition(a, b):
                return a[b].rearrange("g h n -> (g h n)").rearrange("(p n) -> p n", p=P)

            def load_wo(t):
                sp.dma_start(wo_in[t], Wo[t * P:(t + 1) * P, :]).then_inc(wo_loaded[t], 16)

            sp.dma_start(inv[:, 0], by_partition(att_sum, 0)).then_inc(sums_loaded, 16)
            for t in range(KT // 2):
                load_wo(t)
            load_raw(0, 0)
            sp.wait_ge(inv_ready, 1)
            sp.dma_start(by_partition(att_inv, 0), inv[:, 0]).then_inc(inv_stored, 16)
            load_wo(KT // 2)
            sp.wait_ge(inv_stored, 16)
            load_inv(0, 0)
            for t in range(KT // 2 + 1, KT):
                load_wo(t)
            for b in range(NB):
                rows = slice(b * 2 * KT, (b + 1) * 2 * KT)
                sp.dma_start(mod2_in[rows, :], mod_rows[b, 3 * D:5 * D].rearrange("(r p) -> r p", p=P)).then_inc(mod_loaded, 16)
                for i, v in enumerate((2, 5)):
                    rows = slice((b * 2 + i) * KT, (b * 2 + i + 1) * KT)
                    sp.dma_start(gate_in[rows, :], mod_rows[b, v * D:(v + 1) * D].rearrange("(r p) -> r p", p=P)).then_inc(gate_loaded, 16)
            for b in range(1, NB):
                sp.dma_start(inv[:, b], by_partition(att_sum, b)).then_inc(sums_loaded, 16)
            sp.dma_start(bo_bc[:], bo.rearrange("(o d) -> o d", o=1).to_broadcast([P, D])).then_inc(bc_loaded, 16)
            load_res(0, 0)
            sp.wait_ge(gate_ready, 1)
            sp.dma_start(gate_rows.rearrange("b v (r p) -> (b v r) p", p=P), gate_in[:]).then_inc(gate_stored, 16)
            sp.wait_ge(at_lo_done, 1)
            load_at(0, 1)
            sp.wait_ge(gate_stored, 16)
            load_gates(0)
            sp.wait_ge(inv_ready, 2)
            for b in range(1, NB):
                sp.dma_start(by_partition(att_inv, b), inv[:, b]).then_inc(inv_stored, 16)
            sp.wait_ge(inv_stored, 16 * NB)
            sp.wait_ge(gates_loaded, 16)
            load_gates(1)
            load_res(0, 1)
            sp.wait_ge(at_lo_done, 2)
            load_at(0, 2)

            def chunk(b, i, last):
                n = b * CPB + i
                if not (last and i + 3 >= CPB):
                    wait_apart(sp, at_lo_done, n + 3, tally)
                    load_at(b, i + 3)
                wait_apart(sp, out_ready, T * (n + 1), tally)
                sp.dma_start(tokens(out, b, i), delta[:]).then_inc(out_stored, 16)
                if not (last and i + 2 >= CPB):
                    load_res(b, i + 2)
                if i == CPB - 1 and not last:
                    wait_apart(sp, gates_loaded, 16 * (b + 2), tally)
                    load_gates((b + 2) % NB)

            chunks(sp, chunk)
            sp.wait_ge(gates_loaded, 16 * (NB + 1))
            sp.wait_ge(out_stored, 16 * (NC + 1))

        @block.gpsimd
        def _(pool):
            nc.gpsimd.memset(minus_half[:], -0.5).then_inc(const_ready, 1)
            nc.gpsimd.memset(lower[:], 1.0).then_inc(const_ready, 1)
            pool.wait_ge(const_ready, 2)
            nc.gpsimd.affine_select(out=lower[:], in_=lower[:], compare_op=ALU.is_gt, fill=0.0, base=0,
                                    pattern=[[1, E], [-1, E]], channel_multiplier=0).then_inc(const_ready, 1)

            def split_lo(b, i):
                pool.wait_ge(at_hi_done, b * CPB + i + 1)
                nc.gpsimd.tensor_tensor(at_lo[i % 2][:], at_raw[:], at_hi[i % 2][:].bitcast(F32), ALU.subtract).then_inc(at_lo_done, 1)

            def rsqrt(b, i, a):
                pool.wait_ge(var_ready, T * (b * CPB + i) + a + 1)
                nc.gpsimd.tensor_tensor(rstd[:, a:a + 1], mean_var[:, a, 1:2], minus_half[:], ALU.pow).then_inc(rstd_ready, 1)

            for i in range(2):
                split_lo(0, i)
            for a in range(T):
                rsqrt(0, 0, a)

            def chunk(b, i, last):
                n = b * CPB + i
                if not (last and i + 2 >= CPB):
                    split_lo(b, i + 2)
                for a in range(T):
                    if not (last and i == CPB - 1):
                        rsqrt(b, i + 1, a)
                    pool.wait_ge(d_free, UN * n + HV * (a + 1) + 2)
                    nc.gpsimd.tensor_tensor(delta[:, a], delta[:, a], res[i % 2][:, a], ALU.add).then_inc(out_ready, 1)

            chunks(pool, chunk)

        @block.scalar
        def _(act):
            act.sem_inc(h2_ready, KP)
            cols = mod2_col[:].rearrange("p (b v k) -> p b v k", b=NB, v=2)

            def split_hi(b, i, first=False):
                n = b * CPB + i
                if not first:
                    act.wait_ge(y_done, UN * (n - 1))
                act.wait_ge(at_divided, n + 1)
                nc.scalar.copy(at_hi[i % 2][:], at_raw[:]).then_inc(at_hi_done, 1)

            for i in range(T):
                for t in range(i * KT // T, (i + 1) * KT // T):
                    act.wait_ge(wo_turned, t + 1)
                    nc.scalar.copy(wo_hi[:, :, t * P:(t + 1) * P], ps_wo[t % 2]).then_inc(wo_hi_done, 1)
                split_hi(0, i, first=True)

            act.wait_ge(mod_ready, 2)

            def chunk(b, i, last):
                n = b * CPB + i
                for q in range(TG):
                    if q == 0:
                        act.wait_ge(down_done, n + 1)
                    wait_apart(act, turned, TG * n + q + 1, tally)
                    for j in range(KP):
                        k = q * KP + j
                        nc.scalar.activation(h2t[:, k], ps_t[q % TB][:, j * CW:(j + 1) * CW], ACT.Identity,
                                             bias=cols[:, b, 0, k:k + 1], scale=cols[:, b, 1, k:k + 1]).then_inc(h2_ready, 1)
                if not (last and i + 2 >= CPB):
                    split_hi(b, i + 2)
                act.wait_ge(logit_ready, n + 1)
                nc.scalar.activation(expo[:], logit[:], ACT.Exp).then_inc(exp_ready, 1)

            chunks(act, chunk)

        @block.vector
        def _(dve):
            dve.sem_inc(wo_lo_done, 2)
            dve.sem_inc(y_free, 2)
            dve.sem_inc(d_free, 2)
            dve.sem_inc(mid_t_ready, 1)
            dve.sem_inc(out_stored, 16)

            def divide(b, i):
                dve.wait_ge(at_loaded, 16 * (1 + HG) * (b * CPB + i + 1))
                nc.vector.tensor_tensor(at_raw[:], at_raw[:], at_inv[:], ALU.mult).then_inc(at_divided, 1)

            def residual(b, i, u, chain):
                n = b * CPB + i
                bb = b + i // CPB
                a, hv = divmod(u, HV)
                cols = slice(hv * BANK, (hv + 1) * BANK)
                y = att_y[:, u]
                if u == 0:
                    dve.wait_ge(gates_loaded, 16 * (bb + 1))
                dve.wait_ge(y_done, UN * n + u + 1)
                nc.vector.tensor_tensor(y, ps_y[u % 2], bo_bc[:, cols], ALU.add).then_inc(y_free, 1)
                wait_apart(dve, y_free, UN * n + u + 1 + 2, tally)
                chain.link(nc.vector.tensor_tensor(y, y, gates_bc[:, 0, bb % 2, cols], ALU.mult))
                if u == 0:
                    dve.wait_ge(res_loaded[i % 2], 16 * (b * (CPB // 2) + i // 2 + 1))
                nc.vector.tensor_tensor(res[i % 2][:, a, cols], res[i % 2][:, a, cols], y, ALU.add).then_inc(x1_ready, 1)

            def layernorm(b, i, a, chain):
                n = b * CPB + i
                r = res[i % 2]
                dve.wait_ge(x1_ready, UN * n + HV * (a + 1))
                for hv in range(2):
                    chain.link(nc.vector.bn_stats(stats[:, hv], r[:, a, hv * (D // 2):(hv + 1) * (D // 2)]))
                chain.link(nc.vector.bn_aggr(mean_var[:, a], stats[:].rearrange("p a b -> p (a b)")))
                nc.vector.tensor_scalar_add(mean_var[:, a, 1:2], mean_var[:, a, 1:2], EPS).then_inc(var_ready, 1)
                dve.wait_ge(rstd_ready, T * n + a + 1)
                nc.vector.tensor_scalar(xn[:, a], r[:, a], mean_var[:, a, 0:1], rstd[:, a:a + 1], ALU.subtract, ALU.mult).then_inc(xn_ready, 1)

            def gates(n, chain):
                dve.wait_ge(down_done, n + 2)
                chain.link(nc.vector.tensor_copy(down[:], ps_l[:, 0:T * NR].rearrange("p (t r) -> p t r", t=T)))
                lg = down[:, :, ER:NR]
                own = lg.unsqueeze(3).to_broadcast([P, T, E, E])
                other = lg.unsqueeze(2).to_broadcast([P, T, E, E])
                chain.link(nc.vector.reduce_max(top1[:], lg, AX.X))
                nc.vector.tensor_tensor(logit[:], lg, top1[:].unsqueeze(2).to_broadcast([P, T, E]), ALU.subtract).then_inc(logit_ready, 1)
                chain.link(nc.vector.tensor_tensor(above[:], other, own, ALU.is_gt))
                chain.link(nc.vector.tensor_tensor(equal[:], other, own, ALU.is_equal))
                chain.link(nc.vector.tensor_tensor(equal[:], equal[:], lower[:].unsqueeze(1).to_broadcast([P, T, E, E]), ALU.mult))
                chain.link(nc.vector.tensor_tensor(above[:], above[:], equal[:], ALU.add))
                chain.link(nc.vector.reduce_sum(rank[:], above[:], AX.X))
                dve.wait_ge(exp_ready, n + 1)
                chain.link(nc.vector.scalar_tensor_tensor(kept[:], rank[:], 2.0, expo[:], ALU.is_lt, ALU.mult))
                chain.link(nc.vector.reduce_sum(denom[:], kept[:], AX.X))
                chain.link(nc.vector.reciprocal(denom[:], denom[:]))
                chain.link(nc.vector.scalar_tensor_tensor(gate[:], kept[:], LORA_SCALE, denom[:].unsqueeze(2).to_broadcast([P, T, E]), ALU.mult, ALU.mult))
                nc.vector.tensor_tensor(mid[:].rearrange("p t (e r) -> p t e r", e=E), down[:, :, 0:ER].rearrange("p t (e r) -> p t e r", e=E),
                                        gate[:].unsqueeze(3).to_broadcast([P, T, E, R]), ALU.mult).then_inc(mid_ready, 1)

            def experts(b, i, units):
                n = b * CPB + i
                for u in units:
                    a, hv = divmod(u, HV)
                    cols = slice(hv * BANK, (hv + 1) * BANK)
                    if u == 0:
                        dve.wait_ge(gates_loaded, 16 * (b + 1))
                        dve.wait_ge(out_stored, 16 * (n + 1))
                    wait_apart(dve, d_done, UN * n + u + 1, tally)
                    nc.vector.tensor_tensor(delta[:, a, cols], ps_d[u % 2], gates_bc[:, 1, b % 2, cols], ALU.mult).then_inc(d_free, 1)

            def modulation():
                start = Chain(dve, start_chain, tally)
                dve.wait_ge(gate_loaded, 16 * 2 * NB)
                start.link(nc.vector.tensor_scalar(sign[:], gate_in[:], 0.0, 2.0, ALU.is_ge, ALU.mult))
                start.link(nc.vector.tensor_scalar(mag[:], gate_in[:], -1.0, None, ALU.mult))
                start.link(nc.vector.tensor_tensor(mag[:], gate_in[:], mag[:], ALU.max))
                start.link(nc.vector.tensor_scalar(mag[:], mag[:], 0.25, None, ALU.max))
                nc.vector.scalar_tensor_tensor(gate_in[:], sign[:], -1.0, mag[:], ALU.add, ALU.mult).then_inc(gate_ready, 1)

            dve.wait_ge(sums_loaded, 16)
            nc.vector.reciprocal(inv[:, 0], inv[:, 0]).then_inc(inv_ready, 1)
            for i in range(T):
                for t in range(i * KT // T, (i + 1) * KT // T):
                    dve.wait_ge(wo_hi_done, t + 1)
                    nc.vector.tensor_tensor(wo_lo[:, :, t * P:(t + 1) * P], ps_wo[t % 2], wo_hi[:, :, t * P:(t + 1) * P].bitcast(F32),
                                            ALU.subtract).then_inc(wo_lo_done, 1)
                if i > 0:
                    dve.wait_ge(sums_loaded, 16 * NB)
                    nc.vector.reciprocal(inv[:, 1:], inv[:, 1:]).then_inc(inv_ready, 1)
                divide(0, i)
                if i == 0:
                    modulation()
            dve.wait_ge(mod_turned, 1)
            src = ps_l[:, 0:2 * KT * NB].rearrange("p (b v k) -> p b v k", b=NB, v=2)
            col = mod2_col[:].rearrange("p (b v k) -> p b v k", b=NB, v=2)
            nc.vector.tensor_copy(col[:, :, 0], src[:, :, 0]).then_inc(mod_ready, 1)
            nc.vector.tensor_scalar_add(col[:, :, 1], src[:, :, 1], 1.0).then_inc(mod_ready, 1)
            dve.wait_ge(bc_loaded, 16)
            dve.wait_ge(const_ready, 3)
            chain = Chain(dve, dve_chain, tally)
            for u in range(UN):
                residual(0, 0, u, chain)
            for a in range(T):
                layernorm(0, 0, a, chain)
            PRO = UN + 3 * T
            GATES = 11

            def chunk(b, i, last):
                n = b * CPB + i
                ahead = not (last and i == CPB - 1)
                chain = Chain(dve, dve_chain, tally, n * (PRO + GATES) + PRO)
                if not (last and i + 2 >= CPB):
                    divide(b, i + 2)
                if ahead:
                    residual(b, i + 1, 0, chain)
                gates(n, chain)
                if ahead:
                    residual(b, i + 1, 1, chain)
                dve.wait_ge(mid_turned, n + 1)
                nc.vector.tensor_copy(mid_t[:], ps_l[0:ER, CW:CW + CW]).then_inc(mid_t_ready, 1)
                if ahead:
                    residual(b, i + 1, 2, chain)
                    layernorm(b, i + 1, 0, chain)
                experts(b, i, range(2))
                if ahead:
                    residual(b, i + 1, 3, chain)
                    layernorm(b, i + 1, 1, chain)
                experts(b, i, range(2, UN))

            chunks(dve, chunk)

        @block.tensor
        def _(pe):
            pe.sem_inc(down_done, 1)

            def project(b, i, u):
                n = b * CPB + i
                a, hv = divmod(u, HV)
                if u == 0:
                    pe.wait_ge(at_lo_done, n + 1)
                pe.wait_ge(y_free, UN * n + u + 1)
                tok, cols = slice(a * P, (a + 1) * P), slice(hv * BANK, (hv + 1) * BANK)
                for g in range(KT):
                    for j, (h, w) in enumerate(((at_hi, wo_hi), (at_lo, wo_hi), (at_hi, wo_lo))):
                        last = nc.tensor.matmul(ps_y[u % 2], h[i % 2][:, g, tok], w[:, g, cols], start=g == 0 and j == 0, stop=g == KT - 1 and j == 2)
                last.then_inc(y_done, 1)

            def turn(n):
                pe.wait_ge(xn_ready, T * (n + 1))
                for q in range(TG):
                    if q % TB == 0:
                        pe.wait_ge(h2_ready, KT * n + (q // TB + 1) * KP)
                    for j in range(KP):
                        for a in range(T):
                            k = q * KP + j
                            last = nc.tensor.transpose(ps_t[q % TB][:, j * CW + a * P:j * CW + (a + 1) * P], xn[:, a, k * P:(k + 1) * P], ident[:])
                    last.then_inc(turned, 1)

            def go_down(n):
                pe.wait_ge(h2_ready, KT * (n + 1) + KP)
                pe.wait_ge(mid_t_ready, n + 1)
                for a in range(T):
                    for k in range(KT):
                        last = nc.tensor.matmul(ps_l[:, a * NR:(a + 1) * NR], h2t[:, k, a * P:(a + 1) * P], down_t[:, k], start=k == 0, stop=k == KT - 1)
                last.then_inc(down_done, 1)

            def turn_mid(n):
                wait_apart(pe, mid_ready, n + 1, tally)
                for a in range(T):
                    last = nc.tensor.transpose(ps_l[0:ER, CW + a * P:CW + (a + 1) * P], mid[:, a], ident[:])
                last.then_inc(mid_turned, 1)

            def go_up(n):
                pe.wait_ge(mid_t_ready, n + 2)
                for u in range(UN):
                    a, hv = divmod(u, HV)
                    pe.wait_ge(d_free, UN * n + u + 1)
                    nc.tensor.matmul(ps_d[u % 2], mid_t[:, a * P:(a + 1) * P], up_t[:, hv * BANK:(hv + 1) * BANK], start=True, stop=True).then_inc(d_done, 1)

            for t in range(KT):
                pe.wait_ge(wo_loaded[t], 16)
                pe.wait_ge(wo_lo_done, t + 1)
                for k in range(KT):
                    last = nc.tensor.transpose(ps_wo[t % 2][:, k], wo_in[t][:, k * P:(k + 1) * P], ident[:])
                last.then_inc(wo_turned, 1)
            pe.wait_ge(wo_lo_done, KT + 2)
            project(0, 0, 0)
            pe.wait_ge(mod_loaded, 16 * NB)
            nc.tensor.transpose(ps_l[:, 0:2 * KT * NB], mod2_in[:], ident[0:2 * KT * NB, 0:2 * KT * NB]).then_inc(mod_turned, 1)
            for u in range(1, UN):
                project(0, 0, u)

            def chunk(b, i, last):
                n = b * CPB + i
                ahead = not (last and i == CPB - 1)
                for u, other in enumerate((turn, go_down, turn_mid, go_up)):
                    if ahead:
                        project(b, i + 1, u)
                    other(n)

            chunks(pe, chunk)


_INS = ["L0_attn_x", "L0_attn_Wq", "L0_attn_bq", "L0_attn_Wk", "L0_attn_bk", "L0_attn_Wv", "L0_attn_bv", "L0_attn_Wo",
        "L0_attn_bo", "L0_ffn_router_w", "L0_ffn_A", "L0_ffn_B", "L0_c", "L0_wmod"]


def kernel(**inputs):
    import concourse.bacc as _bacc
    from concourse.bass_utils import run_bass_kernel_spmd as _run

    nc = _bacc.Bacc("TRN2", target_bir_lowering=False, num_devices=1)
    arrays, args = {}, []
    for name in _INS:
        a = np.ascontiguousarray(inputs[name])
        arrays[f"in_{name}"] = a
        args.append(nc.dram_tensor(f"in_{name}", a.shape, mybir.dt.from_np(a.dtype), kind="ExternalInput").ap())
    out = nc.dram_tensor("out_x", arrays["in_L0_attn_x"].shape, F32, kind="ExternalOutput").ap()
    adaln_block(nc, *args, out)
    r = _run(nc, [arrays], core_ids=[0])
    return r.results[0]["out_x"]
```
